# Optimizing a Trainium2 kernel written in Bass

```python
import numpy as np
import jax
import jax.numpy as jnp

def _softmax(x, axis=-1):
    return jax.nn.softmax(x, axis=axis)

def _gelu(x):
    return jax.nn.gelu(x, approximate=True)

def _silu(x):
    return jax.nn.silu(x)

def _sigmoid(x):
    return jax.nn.sigmoid(x)

def _layernorm(x, axis=-1, eps=1e-05):
    m = jnp.mean(x, axis=axis, keepdims=True)
    v = jnp.var(x, axis=axis, keepdims=True)
    return (x - m) / jnp.sqrt(v + eps)

def _scatter_add(tgt, idx, src, axis=0):
    return tgt.at[idx].add(src)

def _segment_sum(src, seg, n):
    return jax.ops.segment_sum(src, seg, n)
kernel_name = 'mk_adaln_d1_jaxref_r8_ad3f20'

def setup_inputs(seed: int=0):
    np.random.seed(seed)
    _w = jnp.asarray

    def _L0_attn_setup():
        import jax, jax.numpy as jnp
        import numpy as np
        NUM_HEADS = 16
        LN_EPS = 1e-05
        key = jax.random.key(seed)
        ks = jax.random.split(key, 5)
        B, S, E = (4, 128, 128)
        x = jax.random.normal(ks[0], (B, S, E), dtype=jnp.float32)
        Wq = jax.random.normal(ks[1], (E, E), dtype=jnp.float32) * E ** (-0.5)
        Wk = jax.random.normal(ks[2], (E, E), dtype=jnp.float32) * E ** (-0.5)
        Wv = jax.random.normal(ks[3], (E, E), dtype=jnp.float32) * E ** (-0.5)
        Wo = jax.random.normal(ks[4], (E, E), dtype=jnp.float32) * E ** (-0.5)
        gamma = jnp.ones((E,), dtype=jnp.float32)
        beta = jnp.zeros((E,), dtype=jnp.float32)
        return {'x': x, 'Wq': Wq, 'Wk': Wk, 'Wv': Wv, 'Wo': Wo, 'gamma': gamma, 'beta': beta}
    _L0_attn_in = _L0_attn_setup()

    def _L0_ffn_setup():
        import jax, jax.numpy as jnp
        import numpy as np
        E, K = (8, 2)
        key = jax.random.key(seed)
        ks = jax.random.split(key, 5)
        B, S, H, I = (2, 128, 128, 512)
        scale_h = 1.0 / np.sqrt(H)
        scale_i = 1.0 / np.sqrt(I)
        return {'hidden_states': jax.random.normal(ks[0], (B, S, H), jnp.float32), 'conf_w': jax.random.normal(ks[1], (E, H), jnp.float32) * 0.1 * scale_h, 'conf_b': jnp.zeros((E,), jnp.float32), 'gate_w': jax.random.normal(ks[2], (E, I, H), jnp.float32) * scale_h, 'up_w': jax.random.normal(ks[3], (E, I, H), jnp.float32) * scale_h, 'down_w': jax.random.normal(ks[4], (E, H, I), jnp.float32) * scale_i, 'wealth': jnp.ones((E,), jnp.float32)}
    _L0_ffn_in = _L0_ffn_setup()
    _L0_c = _w((lambda *s: np.random.randn(*s).astype(np.float32) * 0.05)(8, 128))
    _L0_wmod = _w((lambda *s: np.random.randn(*s).astype(np.float32) * 0.05)(128, 6 * 128) * 128 ** (-0.5))
    _d = {'L0_attn_x': _L0_attn_in['x'], 'L0_attn_Wq': _L0_attn_in['Wq'], 'L0_attn_Wk': _L0_attn_in['Wk'], 'L0_attn_Wv': _L0_attn_in['Wv'], 'L0_attn_Wo': _L0_attn_in['Wo'], 'L0_attn_gamma': _L0_attn_in['gamma'], 'L0_attn_beta': _L0_attn_in['beta'], 'L0_ffn_conf_w': _L0_ffn_in['conf_w'], 'L0_ffn_conf_b': _L0_ffn_in['conf_b'], 'L0_ffn_gate_w': _L0_ffn_in['gate_w'], 'L0_ffn_up_w': _L0_ffn_in['up_w'], 'L0_ffn_down_w': _L0_ffn_in['down_w'], 'L0_ffn_wealth': _L0_ffn_in['wealth'], 'L0_c': _L0_c, 'L0_wmod': _L0_wmod}
    _x0 = _d['L0_attn_x']
    _d['L0_attn_x'] = jax.random.normal(jax.random.fold_in(jax.random.key(seed), 1), (8, 512, 128), dtype=_x0.dtype)
    del _x0
    return _d

def reference(L0_attn_x, L0_attn_Wq, L0_attn_Wk, L0_attn_Wv, L0_attn_Wo, L0_attn_gamma, L0_attn_beta, L0_ffn_conf_w, L0_ffn_conf_b, L0_ffn_gate_w, L0_ffn_up_w, L0_ffn_down_w, L0_ffn_wealth, L0_c, L0_wmod):

    def _L0_attn_ref(x, Wq, Wk, Wv, Wo, gamma, beta):
        import jax, jax.numpy as jnp
        import numpy as np
        NUM_HEADS = 16
        LN_EPS = 1e-05
        B, S, E = x.shape
        H = NUM_HEADS
        D = E // H
        scale = 1.0 / D ** 0.5
        q = x @ Wq.T
        k = x @ Wk.T * scale
        v = x @ Wv.T
        qh = q.reshape(B, S, H, D)
        kh = k.reshape(B, S, H, D)
        qk = jnp.einsum('bthd,bshd->bhts', qh, kh)
        causal = jnp.tril(jnp.ones((S, S), dtype=bool))
        qk = jnp.where(causal, qk, -jnp.inf)
        attn = jax.nn.softmax(qk, axis=-1)
        vh = v.reshape(B, S, D, H)
        qkv = jnp.einsum('bsdh,bhts->bthd', vh, attn)
        qkv = qkv.reshape(B, S, E)
        mu = jnp.mean(qkv, axis=-1, keepdims=True)
        var = jnp.mean(jnp.square(qkv - mu), axis=-1, keepdims=True)
        ln = (qkv - mu) * jax.lax.rsqrt(var + LN_EPS) * gamma + beta
        return ln @ Wo.T

    def _L0_ffn_ref(hidden_states, conf_w, conf_b, gate_w, up_w, down_w, wealth):
        import jax, jax.numpy as jnp
        import numpy as np
        E, K = (8, 2)
        x = hidden_states
        confidences = jax.nn.sigmoid(jnp.einsum('bsh,eh->bse', x, conf_w) + conf_b)
        bids = confidences * wealth
        top_bids, selected_experts = jax.lax.top_k(bids, K)
        sorted_bids = -jnp.sort(-bids, axis=-1)
        payments = jnp.broadcast_to(sorted_bids[..., K:K + 1], top_bids.shape)
        routing_weights = jax.nn.softmax(top_bids, axis=-1)
        combine = jnp.sum(jax.nn.one_hot(selected_experts, E, dtype=x.dtype) * routing_weights[..., None], axis=2)

        def ffn(gw, uw, dw):
            g = jnp.einsum('bsh,ih->bsi', x, gw)
            u = jnp.einsum('bsh,ih->bsi', x, uw)
            return jnp.einsum('bsi,hi->bsh', jax.nn.silu(g) * u, dw)
        expert_out = jax.vmap(ffn)(gate_w, up_w, down_w)
        output = jnp.einsum('ebsh,bse->bsh', expert_out, combine)
        return output
    x = L0_attn_x
    mod = (_silu(L0_c) @ L0_wmod).reshape(L0_c.shape[0], 6, 1, -1)
    sa, ca, ga, sb, cb, gb = (mod[:, 0], mod[:, 1], mod[:, 2], mod[:, 3], mod[:, 4], mod[:, 5])
    ga = (2 * (ga >= 0) - 1) * jnp.maximum(jnp.abs(ga), 0.25)
    gb = (2 * (gb >= 0) - 1) * jnp.maximum(jnp.abs(gb), 0.25)
    h = _layernorm(x, axis=-1) * (1 + ca) + sa
    x = x + ga * _L0_attn_ref(h, L0_attn_Wq, L0_attn_Wk, L0_attn_Wv, L0_attn_Wo, L0_attn_gamma, L0_attn_beta)
    h = _layernorm(x, axis=-1) * (1 + cb) + sb
    x = x + gb * _L0_ffn_ref(h, L0_ffn_conf_w, L0_ffn_conf_b, L0_ffn_gate_w, L0_ffn_up_w, L0_ffn_down_w, L0_ffn_wealth)
    return x

_drawn_inputs = setup_inputs


def setup_inputs(seed=0):
    import zlib

    import numpy as np

    out = dict(_drawn_inputs(seed))
    spreads = {'L0_attn_gamma': (1.0, 0.2),
     'L0_attn_beta': (0.0, 0.33),
     'L0_ffn_conf_b': (0.0, 0.1),
     'L0_ffn_wealth': (1.0, 0.2)}
    factors = {}
    for name, (base, spread) in spreads.items():
        noise = np.random.default_rng([zlib.crc32(name.encode()), seed]).standard_normal(out[name].shape)
        drawn = base * np.exp(spread * noise) if base else spread * noise
        out[name] = jnp.asarray(drawn.astype(out[name].dtype))
    for name, factor in factors.items():
        out[name] = (out[name] * factor).astype(out[name].dtype)
    return out
```

```python
from contextlib import ExitStack

import concourse.bass as bass
from concourse import mybir

ALU = mybir.AluOpType
ACT = mybir.ActivationFunctionType
AX = mybir.AxisListType
F32 = mybir.dt.float32
BF16 = mybir.dt.bfloat16
I32 = mybir.dt.int32

P = 128
B = 8
S = 512
E = 128
H = 16
D = E // H
TB = S // P
G = 4
J = H // G
NT = B * TB
PARTS = 3
KROWS = D * PARTS * PARTS
MROW = KROWS
KALL = KROWS + PARTS
SOFTMAX_SCALE = float(D) ** -0.5
EPS = 1e-5
BIG = -1.0e30
NAT = 11
UNITS = 5
CHUNKS = (0, 1, 3, 2)

NX = 8
FF = 512
FC = FF // P
REGION = B * S + P
ROW = 132
TOK = B * S
FTILES = (2 * TOK) // P + NX
PLANE = TOK
YROWS = 2 * TOK + 2 * NX * P
XROWS = NX * REGION + NX * P
U = 6
TURNS = FTILES // U
C_TOK, C_E0, C_W0, C_W1 = 128, 129, 130, 131


def nat_blocks(k):
    if k < 4:
        return [(0, k, 3, 512)]
    if k < 8:
        return [(0, k - 4, 2, 384)]
    if k < 10:
        return [(0, 2 * (k - 8), 1, 256), (256, 2 * (k - 8) + 1, 1, 256)]
    return [(P * j, j, 0, P) for j in range(J)]


def exp_blocks(u):
    if u < J:
        return [(0, u, 0), (512, u, 1), (896, u, 3)]
    return [(256 * j, j, 2) for j in range(J)]


def probs_block(sb):
    return {0: (0, 1024), 1: (512, 1024), 3: (896, 1024), 2: (4096, 256)}[sb]


def adaln_attention_moe(nc, x, cT, wmod, wqT, wkT, wvT, woT, gamma, beta,
                        confT, conf_b, wealth, gateT, upT, downT, out):
    qd = nc.dram_tensor("q_parts_dram", [E, PARTS, PARTS, S], BF16, kind="Internal").ap()
    kd = nc.dram_tensor("k_parts_dram", [E, PARTS, PARTS, S], BF16, kind="Internal").ap()

    xd = nc.dram_tensor("dispatched", [XROWS, ROW], F32, kind="Internal").ap()
    yd = nc.dram_tensor("expert_out", [YROWS, E], F32, kind="Internal").ap()

    with ExitStack() as ctx:
        def sb(name, shape, dt=F32):
            return ctx.enter_context(nc.sbuf_tensor(name, shape, dt))

        sems = {}

        def sem(name):
            sems[name] = ctx.enter_context(nc.semaphore(name))
            return sems[name]

        psN = ctx.enter_context(nc.psum_tensor("psN", [P, 2, 512], F32))
        psT = ctx.enter_context(nc.psum_tensor("psT", [P, 2, 1024], F32))
        psO = ctx.enter_context(nc.psum_tensor("psO", [P, 512], F32))
        psM = ctx.enter_context(nc.psum_tensor("psM", [P, 512], F32))

        xall = sb("xall", [P, B, TB, E])
        qst_all = sb("qst_all", [P, G, J, S], BF16)
        kst_all = sb("kst_all", [P, G, J, S], BF16)
        qst = [qst_all[:, g] for g in range(G)]
        kst = [kst_all[:, g] for g in range(G)]
        probs = sb("probs", [P, 2, UNITS * 1024])
        vaug = sb("vaug", [P, TB, H, 32])
        vtmp = sb("vtmp", [P, TB, H, D])
        qparts = sb("qparts", [P, PARTS, S], BF16)
        kparts = sb("kparts", [P, PARTS, S], BF16)
        qres = sb("qres", [P, S])
        kres = sb("kres", [P, S])
        hT = sb("hT", [P, S])
        xn = sb("xn", [P, TB, E])
        oT = sb("oT", [P, S])
        on = sb("on", [P, TB, E])
        onn = sb("onn", [P, TB, E])
        lnT = sb("lnT", [P, S])
        proj = sb("proj", [P, TB, E])
        rec = sb("rec", [P, TB, J])
        negm = sb("negm", [P, 2, J, TB])
        mres = sb("mres", [P, J, TB])
        mparts = sb("mparts", [P, PARTS, J, TB], BF16)
        mrow = sb("mrow", [PARTS * J * TB, P], BF16)
        st = sb("st", [P, TB, 6])
        mv = sb("mv", [P, TB, 2])
        vare = sb("vare", [P, TB])
        rstd = sb("rstd", [P, TB])
        stO = sb("stO", [P, TB, 6])
        mvO = sb("mvO", [P, TB, 2])
        vareO = sb("vareO", [P, TB])
        rstdO = sb("rstdO", [P, TB])
        neghalf = sb("neghalf", [P, TB])
        identf = sb("identf", [P, P])
        identb = sb("identb", [P, P], BF16)
        zero_b = sb("zero_b", [P, P], BF16)
        maskts = sb("maskts", [P, P], BF16)
        cs = sb("cs", [P, B])
        cse = sb("cse", [P, B])
        csil = sb("csil", [P, B])
        wm = sb("wm", [P, 6 * E])
        modT = sb("modT", [P, 2, B])
        mod8 = sb("mod8", [B, 4, E])
        modbc = sb("modbc", [P, B, 4, E])
        wq = sb("wq", [P, E])
        wk = sb("wk", [P, E])
        wv = sb("wv", [P, E])
        wo = sb("wo", [P, E])
        gam = sb("gam", [P, 1])
        bet = sb("bet", [P, 1])

        gate_w = sb("gate_w", [P, NX, FF])
        up_w = sb("up_w", [P, NX, FF])
        down_w = sb("down_w", [P, NX, FC, E])
        conf_w = sb("conf_w", [P, NX])
        confb = sb("confb", [1, NX])
        wealth_bc = sb("wealth_bc", [P, NX])
        onesrow = sb("onesrow", [1, P])
        ones = sb("ones", [P, P])
        before_t = sb("before_t", [P, P])
        padtok = sb("padtok", [P, 2 * NX], I32)
        col = [sb(f"col{i}", [P, NT]) for i in range(6)]
        pri = sb("pri", [P, NX])
        pri_i = sb("pri_i", [P, NX], I32)
        tok_i = sb("tok_i", [P, NT], I32)
        base_i = sb("base_i", [P, NX], I32)
        base = sb("base", [P, NX])
        slots = sb("slots", [P, 2, NT], I32)
        thr_i = sb("thr_i", [P, NT], I32)
        thr = sb("thr", [P, NT])
        jv_i = sb("jv_i", [P, FTILES], I32)
        jv = sb("jv", [P, FTILES])
        part_i = sb("part_i", [P, 1], I32)
        part = sb("part", [P, 1])
        ntile = sb("ntile", [P, NX])
        cums = [sb(f"cums{i}", [P, 4 + NX]) for i in range(2)]
        padslot = sb("padslot", [P, NX])
        padslots = sb("padslots", [P, NX], I32)
        tile_e = sb("tile_e", [P, FTILES])
        tile_used = sb("tile_used", [P, FTILES])
        tile_row = sb("tile_row", [P, FTILES])
        tile_row_i = sb("tile_row_i", [P, FTILES], I32)
        tile_w_i = sb("tile_w_i", [P, FTILES], I32)
        xg = [sb(f"xg{i}", [P, ROW]) for i in range(U)]
        dsc = [sb(f"dsc{i}", [P, 4]) for i in range(U)]
        dest = [sb(f"dest{i}", [P, 1], I32) for i in range(U)]
        ysb = [sb(f"ysb{i}", [P, E]) for i in range(U)]

        ew_in, fc_in = sem("ew_in"), sem("fc_in")
        f_zero, f_const, f_chain = sem("f_zero"), sem("f_const"), sem("f_chain")
        sr_chain, rsr_chain, rsr_ready, xr_ready = sem("sr_chain"), sem("rsr_chain"), sem("rsr_ready"), sem("xr_ready")
        h2_chain, h2_ready, h2T_full, h2T_ready = sem("h2_chain"), sem("h2_ready"), sem("h2T_full"), sem("h2T_ready")
        z_full, z_ready = sem("z_full"), sem("z_ready")
        rows_ready = sem("rows_ready")
        r_chain, d_ready, ed_ready, both_ready, cum_full = (
            sem("r_chain"), sem("d_ready"), sem("ed_ready"), sem("both_ready"), sem("cum_full"))
        dispatch_ready, tiles_ready, dispatched, pads_out = (
            sem("dispatch_ready"), sem("tiles_ready"), sem("dispatched"), sem("pads_out"))
        xg_in = [sem(f"xg_in{i}") for i in range(U)]
        xgT_full, xgT_ready, gu_full, sg_ready, hh_ready = (
            sem("xgT_full"), sem("xgT_ready"), sem("gu_full"), sem("sg_ready"), sem("hh_ready"))
        hhT_full, hhT_ready, y_full, dsc_chain, y_ready = (
            sem("hhT_full"), sem("hhT_ready"), sem("y_full"), sem("dsc_chain"), sem("y_ready"))
        y_out = [sem(f"y_out{i}") for i in range(U)]
        yp_in = [sem(f"yp_in{i}") for i in range(2)]
        c2_chain, c2_ready, fin_ready = sem("c2_chain"), sem("c2_ready"), sem("fin_ready")
        fin_out = [sem(f"fin_out{i}") for i in range(2)]

        c_in, wm_in, w_in = sem("c_in"), sem("wm_in"), sem("w_in")
        x_in = [sem(f"x_in{b}") for b in range(B)]
        zeroed, ident_ready, consts_ready, vaug_set = sem("zeroed"), sem("ident_ready"), sem("consts_ready"), sem("vaug_set")
        c_exp, c_silu, c_chain = sem("c_exp"), sem("c_silu"), sem("c_chain")
        modT_full, modT_ready, mod8_full, mod8_chain, mod8_ready = (
            sem("modT_full"), sem("modT_ready"), sem("mod8_full"), sem("mod8_chain"), sem("mod8_ready"))
        bc_full, bc_ready = sem("bc_full"), sem("bc_ready")
        st_chain, rs_chain, rs_ready, xn_ready = sem("st_chain"), sem("rs_chain"), sem("rs_ready"), sem("xn_ready")
        xT_full, hT_ready = sem("xT_full"), sem("hT_ready")
        q_full, q_hi, q_r1, q_mid, q_parts = sem("q_full"), sem("q_hi"), sem("q_r1"), sem("q_mid"), sem("q_parts")
        k_full, k_hi, k_r1, k_mid, k_parts = sem("k_full"), sem("k_hi"), sem("k_r1"), sem("k_mid"), sem("k_parts")
        v_full, v_tmp, v_ready = sem("v_full"), sem("v_tmp"), sem("v_ready")
        qk_out = sem("qk_out")
        st_in = [sem(f"stack_in{g}") for g in range(G)]
        nat_full, nat_done = sem("nat_full"), sem("nat_done")
        m_chain, m_parts, mT_full, m_row = sem("m_chain"), sem("m_parts"), sem("mT_full"), sem("m_row")
        m_in = [sem(f"m_in{g}") for g in range(G)]
        t_full, exp_done, masked = sem("t_full"), sem("exp_done"), sem("masked")
        pv_done, oT_ready, og_full, og_rec, og_done = (
            sem("pv_done"), sem("oT_ready"), sem("og_full"), sem("og_rec"), sem("og_done"))
        so_chain, rso_chain, rso_ready, onn_ready = sem("so_chain"), sem("rso_chain"), sem("rso_ready"), sem("onn_ready")
        lnT_full, lnT_ready, wo_full, proj_ready, x1_ready = (
            sem("lnT_full"), sem("lnT_ready"), sem("wo_full"), sem("proj_ready"), sem("x1_ready"))
        out_done = sem("out_done")

        psG = [psN[:, i, :] for i in range(2)]
        psU = [psT[:, 0, 512 * i:512 * (i + 1)] for i in range(2)]
        psH = psT[:, 1, 0:512]
        psX = psT[:, 1, 512:512 + P]
        psY = psO[:, 0:E]
        rows = probs[:, 0, 0:NT * ROW].rearrange("p (b n c) -> p b n c", b=B, n=TB)
        abs8, clamp8, sign8 = (probs[0:B, 1, i * 4 * E:(i + 1) * 4 * E].rearrange("p (i e) -> p i e", i=4)
                               for i in range(3))
        rowsel = probs[0:B, 1, 12 * E:(12 + B) * E].rearrange("p (b t) -> p b t", b=B)
        space_v = [vaug[:].rearrange("p n h c -> p (n h c)"), 0]
        space_p = [probs[:, 1, :], 0]
        space_q = [qst_all[:].rearrange("p g j s -> p (g j s)").bitcast(F32), 0]

        def carve(space, *shape):
            n = 1
            for d in shape:
                n *= d
            v = space[0][:, space[1]:space[1] + n]
            space[1] += n
            if len(shape) == 1:
                return v
            names = "abc"[:len(shape)]
            return v.rearrange("p (" + " ".join(names) + ") -> p " + " ".join(names),
                               **dict(zip(names, shape)))

        sg, hh, hhT = ([carve(space_p, FF) for _ in range(2)] for _ in range(3))
        xgT = [carve(space_p, P) for _ in range(2)]
        passed_by, passed_n = (carve(space_p, FTILES, NX) for _ in range(2))
        scan = [carve(space_v, NX, 16 + NT) for _ in range(2)]
        slot = carve(space_v, NX, NT)
        en = carve(space_v, NT, NX)
        padrows = carve(space_q, 2 * NX, ROW)
        route = [carve(space_q, NT, NX) for _ in range(4)]
        first, second = (carve(space_q, NT, NX) for _ in range(2))
        both = carve(space_q, NX, NT)
        yp = [probs[:, i, 0:2 * TB * E].rearrange("p (k n e) -> p k n e", k=2, n=TB) for i in range(2)]
        ysum = [probs[:, i, 2 * TB * E:3 * TB * E].rearrange("p (n e) -> p n e", n=TB) for i in range(2)]

        passed = {e: sem(f"passed_{e}") for e in ("sp", "pe", "dve", "pool")}

        def hold(name, eng, s, value):
            eng.wait_ge(s, value)
            if not isinstance(value, int):
                eng.sem_inc(passed[name], 1)

        block = ctx.enter_context(nc.Block())

        @block.sync
        def _(sp):
            sp.dma_start(cs[:], cT).then_inc(c_in, 16)
            sp.dma_start(wm[:], wmod).then_inc(wm_in, 16)
            for b in range(B):
                sp.dma_start(xall[:, b], x[b].rearrange("(n p) e -> p n e", p=P)).then_inc(x_in[b], 16)
                if b == 1:
                    sp.dma_start(conf_w[:], confT).then_inc(fc_in, 16)
                    sp.dma_start(confb[:], conf_b).then_inc(fc_in, 16)
                    sp.dma_start(wealth_bc[:], wealth.broadcast_to([P, NX])).then_inc(fc_in, 16)
                if b == 0:
                    for dst, src in ((wq, wqT), (wk, wkT), (wv, wvT), (wo, woT)):
                        sp.dma_start(dst[:], src).then_inc(w_in, 16)
                    sp.dma_start(gam[:], gamma).then_inc(w_in, 16)
                    sp.dma_start(bet[:], beta).then_inc(w_in, 16)

            def parts_out(b):
                hold("sp", sp, q_parts, b + 1)
                for i in range(PARTS):
                    sp.dma_start(qd[:, :, i, :], qparts[:]).then_inc(qk_out, 16)
                hold("sp", sp, k_parts, b + 1)
                for i in range(PARTS):
                    sp.dma_start(kd[:, i, :, :], kparts[:]).then_inc(qk_out, 16)

            def stacks_in(g):
                rows = slice(g * J * D, (g + 1) * J * D)
                for dst, src in ((qst[g], qd), (kst[g], kd)):
                    sp.dma_start(dst[0:KROWS], src[rows].rearrange("(j d) a b t -> (d a b) j t", j=J)
                                 ).then_inc(st_in[g], 16)

            def max_rows(b, g):
                hold("sp", sp, m_row, 4 * b + g + 1)
                for a in range(PARTS):
                    sp.dma_start(qst[g][MROW + a:MROW + a + 1].rearrange("p j (n t) -> p (j n) t", t=P),
                                 mrow[a * J * TB:(a + 1) * J * TB, :]).then_inc(m_in[g], 16)

            def step(b, g, first=False, last=False):
                if not (last and g == G - 1):
                    max_rows(b + (g + 1) // G, (g + 1) % G)
                if g == 0:
                    if not first:
                        hold("sp", sp, t_full, 20 * b)
                        stacks_in(G - 1)
                    if not last:
                        hold("sp", sp, st_in[G - 1], 32 * (b + 1))
                        parts_out(b + 1)
                elif not last:
                    if g == 1:
                        hold("sp", sp, qk_out, 96 * (b + 2))
                    hold("sp", sp, t_full, 20 * b + 5 * g)
                    stacks_in(g - 1)

            hold("sp", sp, consts_ready, G)
            parts_out(0)
            hold("sp", sp, qk_out, 96)
            for g in range(G):
                stacks_in(g)
            max_rows(0, 0)
            sp.dma_start(gate_w[:], gateT).then_inc(ew_in, 16)
            sp.dma_start(up_w[:], upT).then_inc(ew_in, 16)
            sp.dma_start(down_w[:], downT).then_inc(ew_in, 16)
            for g in range(G):
                step(0, g, first=True)
            with sp.Fori(1, B - 1) as b:
                for g in range(G):
                    step(b, g)
            for g in range(G):
                step(B - 1, g, last=True)

            def tile_in(i, u):
                j = U * i + u
                if not (isinstance(i, int) and i == 0):
                    hold("sp", sp, xgT_full, j - U + 1)
                    hold("sp", sp, dsc_chain, 5 * (j - U + 1))
                row = sp.value_load(tile_row_i[0:1, bass.ds(j, 1)], min_val=0, max_val=XROWS - P)
                sp.dma_start(xg[u][:], xd[bass.ds(row, P), :]).then_inc(xg_in[u], 16)

            sp.wait_ge(pads_out, 16)
            sp.wait_ge(tiles_ready, 1)
            sp.wait_ge(dispatched, 16 * (2 * NT + NX))
            for u in range(U):
                tile_in(0, u)
            with sp.Fori(1, TURNS) as i:
                for u in range(U):
                    tile_in(i, u)

            def planes_in(i, par):
                b = 2 * i + par
                if not (isinstance(i, int) and i == 0):
                    hold("sp", sp, c2_chain, 2 * (b - 1))
                for k in range(2):
                    sp.dma_start(yp[par][:, k], yd[bass.ds(b * S + k * PLANE, S), :].rearrange("(n p) e -> p n e", p=P)
                                 ).then_inc(yp_in[par], 16)

            def store(i, par):
                b = 2 * i + par
                hold("sp", sp, fin_ready, b + 1)
                sp.dma_start(out[b].rearrange("(n p) e -> p n e", p=P), xall[:, b]).then_inc(fin_out[par], 16)

            for u in range(U):
                sp.wait_ge(y_out[u], 16 * TURNS)
            planes_in(0, 0)
            planes_in(0, 1)
            with sp.Fori(1, B // 2) as i:
                for par in range(2):
                    planes_in(i, par)
                    store(i - 1, par)
            for par in range(2):
                store(B // 2 - 1, par)
            for par in range(2):
                sp.wait_ge(fin_out[par], 16 * (B // 2))

        @block.tensor
        def _(pe):
            bank = [None]

            def take(free=None):
                if bank[0] is not None:
                    pe.wait_ge(*bank[0])
                bank[0] = free

            def nat(b, g, k):
                if k == 0:
                    pe.wait_ge(st_in[g], 32 * (b + 1))
                n = 44 * b + 11 * g + k
                slot = (11 * g + k) % 2
                if not (isinstance(n, int) and n < 2):
                    pe.wait_ge(nat_done, n - 1)
                for col, j, tb, w in nat_blocks(k):
                    pe.matmul(psN[:, slot, col:col + w], qst[g][0:KROWS, j, tb * P:(tb + 1) * P],
                              kst[g][0:KROWS, j, 0:w], start=True, stop=False)
                    mm = pe.matmul(psN[:, slot, col + w - P:col + w], identb[:], maskts[:],
                                   start=False, stop=True)
                mm.then_inc(nat_full, 1)

            def scores(b, g, u):
                n = 20 * b + 5 * g + u
                slot = (5 * g + u) % 2
                if u == 0:
                    pe.wait_ge(m_in[g], 48 * (b + 1))
                if not (isinstance(n, int) and n < 2):
                    pe.wait_ge(exp_done, n - 1)
                for col, j, blk in exp_blocks(u):
                    mm = pe.matmul(psT[:, slot, col:col + S - P * blk], kst[g][0:KALL, j, blk * P:(blk + 1) * P],
                                   qst[g][0:KALL, j, blk * P:S], start=True, stop=True)
                mm.then_inc(t_full, 1)

            def values(b, g, c):
                if c == 0:
                    if g == 0:
                        pe.wait_ge(v_ready, b + 1)
                    if not (isinstance(b, int) and b == 0 and g == 0):
                        pe.wait_ge(oT_ready, 4 * b + g)
                pe.wait_ge(masked, 16 * b + 4 * g + c + 1)
                blk = CHUNKS[c]
                base, stride = probs_block(blk)
                w = S - P * blk
                for j in range(J):
                    o = base + stride * j
                    mm = pe.matmul(psO[32 * j:32 * j + 32, blk * P:S], vaug[:, blk, g * J + j, :],
                                   probs[:, g % 2, o:o + w], start=(c == 0), stop=(c == TB - 1))
                mm.then_inc(pv_done, 1)

            def turn_values(b, g):
                take((og_done, 4 * b + g + 1))
                pe.wait_ge(oT_ready, 4 * b + g + 1)
                for n in range(TB):
                    mm = pe.transpose(psM[:, n * P:(n + 1) * P], oT[:, n * P:(n + 1) * P], identf[:])
                mm.then_inc(og_full, 1)

            def turn_max(b, g):
                take((m_row, 4 * b + g + 1))
                hold("pe", pe, m_parts, 4 * b + g + 1)
                pe.transpose(psM[:].bitcast(BF16)[0:PARTS * J * TB, 0:P], mparts[:].rearrange("p a j n -> p (a j n)"),
                             identb[:]).then_inc(mT_full, 1)

            def turn_x(b):
                take((hT_ready, b + 1))
                pe.wait_ge(xn_ready, b + 1)
                for n in range(TB):
                    mm = pe.transpose(psM[:, n * P:(n + 1) * P], xn[:, n, :], identf[:])
                mm.then_inc(xT_full, 1)

            def project_q(b):
                take((q_r1, b + 1))
                pe.matmul(psM[:], wq[:], hT[:], start=True, stop=True).then_inc(q_full, 1)

            def project_k(b):
                take((k_r1, b + 1))
                pe.matmul(psM[:], wk[:], hT[:], start=True, stop=True).then_inc(k_full, 1)

            def project_v(b):
                take((v_tmp, b + 1))
                for n in range(TB):
                    mm = pe.matmul(psM[:, n * P:(n + 1) * P], hT[:, n * P:(n + 1) * P], wv[:], start=True, stop=True)
                mm.then_inc(v_full, 1)

            def turn_attn(b):
                take((lnT_ready, b + 1))
                pe.wait_ge(onn_ready, b + 1)
                for n in range(TB):
                    mm = pe.transpose(psM[:, n * P:(n + 1) * P], onn[:, n, :], identf[:])
                mm.then_inc(lnT_full, 1)

            def project_o(b):
                take((proj_ready, b + 1))
                for n in range(TB):
                    mm = pe.matmul(psM[:, n * P:(n + 1) * P], lnT[:, n * P:(n + 1) * P], wo[:], start=True, stop=True)
                mm.then_inc(wo_full, 1)

            def before(b, g, n):
                q = g - n
                return (b + q // G, q % G)

            def step(b, g, first=False, last=False):
                s = 4 * b + g
                for k in range(NAT):
                    ahead = before(b, g, -2)
                    if not (last and g >= 2):
                        nat(ahead[0], ahead[1], k)
                    if k % 2 == 0 and k // 2 < UNITS:
                        scores(b, g, k // 2)
                    if k == 0 and not (first and g < 2):
                        turn_values(*before(b, g, 2))
                    if k == 1 and not (last and g == G - 1):
                        turn_max(*before(b, g, -1))
                    if k % 2 == 1 and k // 2 < TB and not (first and g == 0):
                        pb, pg = before(b, g, 1)
                        values(pb, pg, k // 2)
                    if g == 0 and not last:
                        if k == 3:
                            turn_x(b + 1)
                        if k == 5:
                            project_q(b + 1)
                        if k == 7:
                            project_k(b + 1)
                        if k == 9:
                            project_v(b + 1)
                    if g == 2 and not first:
                        if k == 3:
                            turn_attn(b - 1)
                        if k == 7:
                            project_o(b - 1)

            pe.wait_ge(wm_in, 16)
            pe.wait_ge(c_silu, 1)
            take((modT_ready, 1))
            for i in range(2):
                mm = pe.matmul(psM[:, i * B:(i + 1) * B], wm[:, i * E:(i + 1) * E], csil[:], start=True, stop=True)
            mm.then_inc(modT_full, 1)
            take((mod8_chain, 1))
            pe.matmul(psM[0:B, :], csil[:], wm[:, 2 * E:6 * E], start=True, stop=True).then_inc(mod8_full, 1)
            pe.wait_ge(ident_ready, 3)
            pe.wait_ge(w_in, 96)
            turn_x(0)
            pe.wait_ge(hT_ready, 1)
            project_q(0)
            project_k(0)
            project_v(0)
            pe.wait_ge(mod8_ready, 2)
            for b in range(B):
                if b >= 4:
                    pe.wait_ge(bc_ready, b - 3)
                pe.matmul(psT[:, b % 4 // 2, 512 * (b % 2):512 * (b % 2) + 512], rowsel[:, b, :],
                          mod8[:].rearrange("p i e -> p (i e)"), start=True, stop=True).then_inc(bc_full, 1)
            for k in range(NAT):
                nat(0, 0, k)
            turn_max(0, 0)
            for k in range(NAT):
                nat(0, 1, k)
            pe.wait_ge(bc_ready, B)
            for g in range(G):
                step(0, g, first=True)
            with pe.Fori(1, B - 1) as b:
                bank[0] = (m_row, 4 * b + 1)
                for g in range(G):
                    step(b, g)
            bank[0] = (m_row, 4 * (B - 1) + 1)
            for g in range(G):
                step(B - 1, g, last=True)
            L = B - 1
            turn_values(L, 2)
            for c in range(TB):
                values(L, 3, c)
            turn_values(L, 3)
            turn_attn(L)
            project_o(L)

            def turn_h(b):
                take((h2T_ready, b + 1))
                pe.wait_ge(h2_ready, b + 1)
                for n in range(TB):
                    mm = pe.transpose(psM[:, n * P:(n + 1) * P], onn[:, n, :], identf[:])
                mm.then_inc(h2T_full, 1)

            def experts(b):
                take((z_ready, b + 1))
                for n in range(TB):
                    pe.matmul(psM[:, n * NX:(n + 1) * NX], lnT[:, n * P:(n + 1) * P], conf_w[:], start=True, stop=False)
                    mm = pe.matmul(psM[:, n * NX:(n + 1) * NX], onesrow[:], confb[:], start=False, stop=True)
                mm.then_inc(z_full, 1)

            pe.wait_ge(fc_in, 48)
            pe.wait_ge(f_const, 2)
            turn_h(0)
            experts(0)
            with pe.Fori(1, B) as b:
                bank[0] = (z_ready, b)
                turn_h(b)
                experts(b)
            pe.wait_ge(z_ready, B)
            pe.wait_ge(both_ready, 1)
            pe.matmul(psM[:, 0:NX * NT], before_t[:], both.rearrange("p e t -> p (e t)"), start=True, stop=True)
            pe.matmul(psM[:, NX * NT:2 * NX * NT], ones[:], both.rearrange("p e t -> p (e t)"),
                      start=True, stop=True).then_inc(cum_full, 1)

            def turn_in(i, u):
                j, par = U * i + u, u % 2
                pe.wait_ge(xg_in[u], 16 * (i + 1))
                if not (isinstance(i, int) and j == 0):
                    pe.wait_ge(xgT_ready, j)
                pe.transpose(psX, xg[u][:, 0:E], identf[:]).then_inc(xgT_full, 1)

            def gate_up(i, u):
                j, par = U * i + u, u % 2
                e = pe.value_load(tile_w_i[0:1, bass.ds(j, 1)], min_val=0, max_val=NX - 1)
                pe.wait_ge(xgT_ready, j + 1)
                if not (isinstance(i, int) and j < 2):
                    pe.wait_ge(hh_ready, j - 1)
                pe.matmul(psG[par], xgT[par], gate_w[:, bass.ds(e, 1), :], start=True, stop=True)
                pe.matmul(psU[par], xgT[par], up_w[:, bass.ds(e, 1), :], start=True, stop=True).then_inc(gu_full, 1)

            def turn_hidden(i, u):
                j, par = U * i + u, u % 2
                pe.wait_ge(hh_ready, j + 1)
                if not (isinstance(i, int) and j == 0):
                    pe.wait_ge(hhT_ready, j)
                for c in range(FC):
                    mm = pe.transpose(psH[:, c * P:(c + 1) * P], hh[par][:, c * P:(c + 1) * P], identf[:])
                mm.then_inc(hhT_full, 1)

            def down(i, u):
                j, par = U * i + u, u % 2
                e = pe.value_load(tile_w_i[0:1, bass.ds(j, 1)], min_val=0, max_val=NX - 1)
                pe.wait_ge(hhT_ready, j + 1)
                if not (isinstance(i, int) and j == 0):
                    pe.wait_ge(y_ready, j)
                for c in range(FC):
                    mm = pe.matmul(psY, hhT[par][:, c * P:(c + 1) * P], down_w[:, bass.ds(e, 1), c, :],
                                   start=(c == 0), stop=(c == FC - 1))
                mm.then_inc(y_full, 1)

            def at(i, u):
                return i + u // U, u % U

            def turn(i, first=False, last=False):
                for u in range(U):
                    if not (last and u == U - 1):
                        turn_in(*at(i, u + 1))
                    gate_up(i, u)
                    if not (first and u < 1):
                        turn_hidden(*at(i, u - 1))
                    if not (first and u < 2):
                        down(*at(i, u - 2))

            pe.wait_ge(ew_in, 48)
            pe.wait_ge(tiles_ready, 1)
            turn_in(0, 0)
            turn(0, first=True)
            with pe.Fori(1, TURNS - 1) as i:
                turn(i)
            turn(TURNS - 1, last=True)
            turn_hidden(TURNS - 1, U - 1)
            down(TURNS - 1, U - 2)
            down(TURNS - 1, U - 1)

        @block.scalar
        def _(act):
            act.wait_ge(c_in, 16)
            nc.scalar.activation(cse[:], cs[:], ACT.Exp, scale=-1.0).then_inc(c_exp, 1)

            def shift_in(b):
                act.wait_ge(xT_full, b + 1)
                nc.scalar.activation(hT[:], psM[:], ACT.Identity, scale=modT[:, 1, bass.ds(b, 1)],
                                     bias=modT[:, 0, bass.ds(b, 1)]).then_inc(hT_ready, 1)

            def high(b, full, parts, done):
                act.wait_ge(full, b + 1)
                if not (isinstance(b, int) and b == 0):
                    act.wait_ge(qk_out, 96 * b)
                nc.scalar.activation(parts[:, 0, :], psM[:], ACT.Copy).then_inc(done, 1)

            def keep_v(b):
                act.wait_ge(v_full, b + 1)
                if not (isinstance(b, int) and b == 0):
                    act.wait_ge(v_ready, b)
                nc.scalar.activation(vtmp[:].rearrange("p n h d -> p (n h d)"), psM[:], ACT.Copy).then_inc(v_tmp, 1)

            def keep_max(b, g):
                act.wait_ge(mT_full, 4 * b + g + 1)
                s = 4 * b + g
                if not (isinstance(b, int) and s == 0):
                    pb, pg = (b, g - 1) if g else (b - 1, G - 1)
                    act.wait_ge(m_in[pg], 48 * (pb + 1))
                nc.scalar.activation(mrow[:], psM[:].bitcast(BF16)[0:PARTS * J * TB, 0:P], ACT.Copy).then_inc(m_row, 1)

            def exps(b, g, u):
                n = 20 * b + 5 * g + u
                act.wait_ge(t_full, n + 1)
                if u == 0 and not (isinstance(b, int) and 4 * b + g < 2):
                    act.wait_ge(pv_done, 16 * b + 4 * g - 4)
                nc.scalar.activation(probs[:, g % 2, 1024 * u:1024 * (u + 1)], psT[:, (5 * g + u) % 2, :], ACT.Exp,
                                     scale=SOFTMAX_SCALE).then_inc(exp_done, 1)

            def keep_values(b, g):
                act.wait_ge(pv_done, 16 * b + 4 * g + 4)
                if not (isinstance(b, int) and 4 * b + g < 1):
                    act.wait_ge(og_full, 4 * b + g)
                nc.scalar.activation(oT[:], psO[:], ACT.Copy).then_inc(oT_ready, 1)

            def keep_attn(b):
                act.wait_ge(lnT_full, b + 1)
                nc.scalar.activation(lnT[:], psM[:], ACT.Identity, scale=gam[:, 0:1], bias=bet[:, 0:1]
                                     ).then_inc(lnT_ready, 1)

            def step(b, g, first=False, last=False):
                for k in range(NAT):
                    if k % 2 == 0 and k // 2 < UNITS:
                        exps(b, g, k // 2)
                    if k == 1 and not (last and g == G - 1):
                        keep_max(b + (g + 1) // G, (g + 1) % G)
                    if k == 8 and not (first and g == 0):
                        keep_values(*((b, g - 1) if g else (b - 1, G - 1)))
                    if g == 0 and not last:
                        if k == 3:
                            shift_in(b + 1)
                        if k == 5:
                            high(b + 1, q_full, qparts, q_hi)
                        if k == 7:
                            high(b + 1, k_full, kparts, k_hi)
                        if k == 9:
                            keep_v(b + 1)
                    if g == 2 and k == 3 and not first:
                        keep_attn(b - 1)

            act.wait_ge(modT_ready, 1)
            shift_in(0)
            high(0, q_full, qparts, q_hi)
            high(0, k_full, kparts, k_hi)
            keep_v(0)
            for b in range(B):
                act.wait_ge(bc_full, b + 1)
                nc.scalar.activation(modbc[:, b].rearrange("p i e -> p (i e)"),
                                     psT[:, b % 4 // 2, 512 * (b % 2):512 * (b % 2) + 512], ACT.Copy).then_inc(bc_ready, 1)
            keep_max(0, 0)
            for g in range(G):
                step(0, g, first=True)
            with act.Fori(1, B - 1) as b:
                for g in range(G):
                    step(b, g)
            for g in range(G):
                step(B - 1, g, last=True)
            keep_values(B - 1, 3)
            keep_attn(B - 1)

            def keep_h(b):
                act.wait_ge(h2_ready, b + 1)
                nc.scalar.activation(rows[:, b, :, 0:E], onn[:], ACT.Copy).then_inc(rows_ready, 1)
                act.wait_ge(h2T_full, b + 1)
                nc.scalar.activation(lnT[:], psM[:], ACT.Copy).then_inc(h2T_ready, 1)
                act.wait_ge(z_full, b + 1)
                nc.scalar.activation(en[:, bass.ds(b * TB, TB), :].rearrange("p n e -> p (n e)"), psM[:, 0:TB * NX],
                                     ACT.Exp, scale=-1.0).then_inc(z_ready, 1)

            with act.Fori(0, B) as b:
                keep_h(b)
            act.wait_ge(d_ready, 1)
            nc.scalar.activation(col[4][:], col[2][:], ACT.Exp).then_inc(ed_ready, 1)

            def silu(i, u):
                j, par = U * i + u, u % 2
                act.wait_ge(gu_full, j + 1)
                if not (isinstance(i, int) and j < 2):
                    act.wait_ge(hh_ready, j - 1)
                nc.scalar.activation(sg[par], psG[par], ACT.Silu).then_inc(sg_ready, 1)

            def keep_hidden(i, u):
                j, par = U * i + u, u % 2
                act.wait_ge(hhT_full, j + 1)
                if not (isinstance(i, int) and j < 2):
                    act.wait_ge(y_full, j - 1)
                nc.scalar.activation(hhT[par], psH, ACT.Copy).then_inc(hhT_ready, 1)

            def turn(i, first=False):
                for u in range(U):
                    silu(i, u)
                    if not (first and u == 0):
                        keep_hidden(i + (u - 1) // U, (u - 1) % U)

            nc.scalar.preload_act_table(ACT.Silu)
            turn(0, first=True)
            with act.Fori(1, TURNS) as i:
                turn(i)
            keep_hidden(TURNS - 1, U - 1)

        @block.vector
        def _(dve):
            for g in range(G):
                nc.vector.memset(kst[g][64:96], 1.0).then_inc(consts_ready, 1)
            dve.wait_ge(c_exp, 1)
            nc.vector.tensor_scalar_add(cse[:], cse[:], 1.0).then_inc(c_chain, 1)
            dve.wait_ge(c_chain, 1)
            nc.vector.reciprocal(cse[:], cse[:]).then_inc(c_chain, 1)
            dve.wait_ge(c_chain, 2)
            nc.vector.tensor_tensor(csil[:], cs[:], cse[:], ALU.mult).then_inc(c_silu, 1)

            def stats(src, s6, m2, chain, b):
                for n in range(TB):
                    nc.vector.bn_stats(s6[:, n, :], src(n)).then_inc(chain, 1)
                hold("dve", dve, chain, 8 * b + 4)
                for n in range(TB):
                    nc.vector.bn_aggr(m2[:, n, :], s6[:, n, :]).then_inc(chain, 1)

            def x_stats(b):
                stats(lambda n: xall[:, b, n, :], st, mv, st_chain, b)

            def x_norm(b):
                dve.wait_ge(rs_ready, b + 1)
                if not (isinstance(b, int) and b == 0):
                    dve.wait_ge(xT_full, b)
                for n in range(TB):
                    last = nc.vector.tensor_scalar(xn[:, n, :], xall[:, b, n, :], mv[:, n, 0:1], rstd[:, n:n + 1],
                                                   ALU.subtract, ALU.mult)
                last.then_inc(xn_ready, 1)

            def o_stats(b):
                dve.wait_ge(og_done, 4 * b + 4)
                stats(lambda n: on[:, n, :], stO, mvO, so_chain, b)

            def o_norm(b):
                dve.wait_ge(rso_ready, b + 1)
                if not (isinstance(b, int) and b == 0):
                    dve.wait_ge(lnT_full, b)
                for n in range(TB):
                    last = nc.vector.tensor_scalar(onn[:, n, :], on[:, n, :], mvO[:, n, 0:1], rstdO[:, n:n + 1],
                                                   ALU.subtract, ALU.mult)
                last.then_inc(onn_ready, 1)

            def residue(b, hi, parts, res, done, split):
                dve.wait_ge(hi, b + 1)
                if not (isinstance(b, int) and b == 0):
                    dve.wait_ge(split, b)
                nc.vector.tensor_tensor(res[:], psM[:], parts[:, 0, :], ALU.subtract).then_inc(done, 1)

            def maxima(b, g, k):
                n = 44 * b + 11 * g + k
                slot = (11 * g + k) % 2
                dve.wait_ge(nat_full, n + 1)
                if k == 0 and not (isinstance(b, int) and 4 * b + g < 2):
                    dve.wait_ge(m_parts, 4 * b + g - 1)
                blocks = nat_blocks(k)
                w = blocks[0][3]
                dst = negm[:, g % 2, blocks[0][1]:blocks[-1][1] + 1, blocks[0][2]]
                src = psN[:, slot, 0:w * len(blocks)].rearrange("p (h s) -> p h s", s=w)
                nc.vector.tensor_reduce(dst, src, axis=AX.X, op=ALU.max, negate=True).then_inc(nat_done, 1)

            def normalise(b, g):
                dve.wait_ge(og_full, 4 * b + g + 1)
                v = psM[:].rearrange("p (n j c) -> p n j c", n=TB, j=J)
                nc.vector.reciprocal(rec[:], v[:, :, :, D]).then_inc(og_rec, 1)
                dve.wait_ge(og_rec, 4 * b + g + 1)
                nc.vector.tensor_tensor(on[:, :, g * J * D:(g + 1) * J * D].rearrange("p n (j d) -> p n j d", j=J),
                                        v[:, :, :, 0:D], rec[:].unsqueeze(3).broadcast_to([P, TB, J, D]),
                                        ALU.mult).then_inc(og_done, 1)

            def gate_out(b):
                dve.wait_ge(wo_full, b + 1)
                if not (isinstance(b, int) and b == 0):
                    dve.wait_ge(x1_ready, b)
                nc.vector.tensor_tensor(proj[:], psM[:].rearrange("p (n e) -> p n e", n=TB),
                                        modbc[:, b, 0:1, :].broadcast_to([P, TB, E]), ALU.mult).then_inc(proj_ready, 1)

            def step(b, g, first=False, last=False):
                for k in range(NAT):
                    if not (last and g >= 2):
                        maxima(b + (g + 2) // G, (g + 2) % G, k)
                    if k == 0 and not (first and g < 2):
                        normalise(b + (g - 2) // G, (g - 2) % G)
                    if g == 0 and not last:
                        if k == 1:
                            x_stats(b + 1)
                        if k == 2:
                            x_norm(b + 1)
                        if k == 6:
                            residue(b + 1, q_hi, qparts, qres, q_r1, q_parts)
                        if k == 8:
                            residue(b + 1, k_hi, kparts, kres, k_r1, k_parts)
                    if g == 1 and not first:
                        if k == 2:
                            o_stats(b - 1)
                        if k == 4:
                            o_norm(b - 1)
                    if g == 2 and k == 8 and not first:
                        gate_out(b - 1)

            dve.wait_ge(x_in[0], 16)
            x_stats(0)
            dve.wait_ge(modT_full, 1)
            nc.vector.tensor_scalar_add(modT[:, 1, :], psM[:, B:2 * B], 1.0).then_inc(c_chain, 1)
            nc.vector.tensor_copy(modT[:, 0, :], psM[:, 0:B]).then_inc(modT_ready, 1)
            dve.wait_ge(mod8_full, 1)
            nc.vector.tensor_copy(mod8[:].rearrange("p i e -> p (i e)"), psM[0:B, :]).then_inc(mod8_chain, 1)
            x_norm(0)
            dve.wait_ge(mod8_chain, 1)
            for i in (0, 3):
                nc.vector.scalar_tensor_tensor(out=abs8[:, i, :], in0=mod8[:, i, :], scalar=-1.0, in1=mod8[:, i, :],
                                               op0=ALU.mult, op1=ALU.max).then_inc(mod8_chain, 1)
                nc.vector.tensor_scalar(sign8[:, i, :], mod8[:, i, :], 0.0, 2.0, ALU.is_ge, ALU.mult).then_inc(mod8_chain, 1)
            dve.wait_ge(mod8_chain, 5)
            for i in (0, 3):
                nc.vector.tensor_scalar_max(clamp8[:, i, :], abs8[:, i, :], 0.25).then_inc(mod8_chain, 1)
            dve.wait_ge(mod8_chain, 7)
            for i in (0, 3):
                nc.vector.scalar_tensor_tensor(out=mod8[:, i, :], in0=sign8[:, i, :], scalar=-1.0, in1=clamp8[:, i, :],
                                               op0=ALU.add, op1=ALU.mult).then_inc(mod8_chain, 1)
            nc.vector.tensor_scalar_add(mod8[:, 2, :], mod8[:, 2, :], 1.0).then_inc(mod8_chain, 1)
            dve.wait_ge(mod8_chain, 10)
            nc.vector.nop().then_inc(mod8_ready, 1)
            residue(0, q_hi, qparts, qres, q_r1, q_parts)
            residue(0, k_hi, kparts, kres, k_r1, k_parts)
            for g in range(2):
                for k in range(NAT):
                    maxima(0, g, k)
            for b in range(1, B):
                dve.wait_ge(x_in[b], 16)
            for g in range(G):
                step(0, g, first=True)
            with dve.Fori(1, B - 1) as b:
                for g in range(G):
                    step(b, g)
            for g in range(G):
                step(B - 1, g, last=True)
            normalise(B - 1, 2)
            normalise(B - 1, 3)
            o_stats(B - 1)
            o_norm(B - 1)
            gate_out(B - 1)

            with dve.Fori(0, B) as b:
                hold("dve", dve, x1_ready, b + 1)
                for n in range(TB):
                    nc.vector.bn_stats(st[:, n, :], xall[:, b, n, :]).then_inc(sr_chain, 1)
                hold("dve", dve, sr_chain, 8 * b + 4)
                for n in range(TB):
                    nc.vector.bn_aggr(mv[:, n, :], st[:, n, :]).then_inc(sr_chain, 1)
                hold("dve", dve, rsr_ready, b + 1)
                for n in range(TB):
                    last = nc.vector.tensor_scalar(xn[:, n, :], xall[:, b, n, :], mv[:, n, 0:1], rstd[:, n:n + 1],
                                                   ALU.subtract, ALU.mult)
                last.then_inc(xr_ready, 1)
                hold("dve", dve, h2_ready, b + 1)

            links = [0]

            def link(ins, s=f_chain):
                ins.then_inc(s, 1)
                links[0] += 1
                dve.wait_ge(s, links[0])

            def over(ap, shape):
                return ap.unsqueeze(2).broadcast_to(shape)

            V = nc.vector
            full = [P, NT, NX]
            bids, masked_b, t2, t3 = route
            dve.wait_ge(z_ready, B)
            dve.wait_ge(rows_ready, B)
            dve.wait_ge(fc_in, 48)
            dve.wait_ge(f_const, 3)
            for dst, src in ((pri, pri_i), (base, base_i), (thr, thr_i), (jv, jv_i), (part, part_i)):
                link(V.tensor_copy(dst[:], src[:]))
            link(V.tensor_copy(rows[:, :, :, C_TOK].rearrange("p b n -> p (b n)"), tok_i[:]))
            link(V.memset(padrows, 0.0))
            link(V.memset(padrows[:, :, C_E0], -1.0))
            V.tensor_copy(padrows[:, :, C_TOK], padtok[:]).then_inc(dispatch_ready, 1)
            link(V.tensor_scalar_add(t2, en, 1.0))
            link(V.reciprocal(t3, t2))
            link(V.tensor_tensor(bids, t3, wealth_bc[:].unsqueeze(1).broadcast_to(full), ALU.mult))
            for n, (src, pick, mx, fm) in enumerate(((bids, first, col[0], col[1]), (masked_b, second, col[2], col[3]))):
                link(V.tensor_reduce(mx[:], src, axis=AX.X, op=ALU.max))
                link(V.tensor_tensor(t2, src, over(mx[:], full), ALU.is_equal))
                link(V.tensor_tensor(t3, t2, pri[:].unsqueeze(1).broadcast_to(full), ALU.mult))
                link(V.tensor_reduce(fm[:], t3, axis=AX.X, op=ALU.max))
                link(V.tensor_tensor(pick, t3, over(fm[:], full), ALU.is_equal))
                if n == 0:
                    link(V.scalar_tensor_tensor(out=masked_b, in0=pick, scalar=BIG, in1=src,
                                                op0=ALU.mult, op1=ALU.add))
            link(V.tensor_tensor(both.rearrange("p e t -> p t e"), first, second, ALU.add))
            V.tensor_tensor(col[2][:], col[2][:], col[0][:], ALU.subtract).then_inc(d_ready, 1)
            V.tensor_scalar(rows[:, :, :, C_E0].rearrange("p b n -> p (b n)"), col[1][:], -1.0, float(NX),
                            ALU.mult, ALU.add).then_inc(both_ready, 1)
            dve.wait_ge(ed_ready, 1)
            link(V.tensor_scalar_add(col[5][:], col[4][:], 1.0))
            link(V.reciprocal(col[1][:], col[5][:]))
            link(V.tensor_copy(rows[:, :, :, C_W0].rearrange("p b n -> p (b n)"), col[1][:]))
            link(V.tensor_tensor(rows[:, :, :, C_W1].rearrange("p b n -> p (b n)"), col[4][:], col[1][:], ALU.mult))
            dve.wait_ge(cum_full, 1)
            cum = psM[:, 0:NX * NT].rearrange("p (e t) -> p e t", e=NX)
            tot = psM[:, NX * NT:2 * NX * NT].rearrange("p (e t) -> p e t", e=NX)
            link(V.memset(scan[0][:, :, 0:16], 0.0))
            link(V.memset(scan[1][:, :, 0:16], 0.0))
            link(V.tensor_copy(scan[0][:, :, 16:], tot))
            a, c = scan
            for sh in (1, 2, 4, 8, 16):
                link(V.tensor_tensor(c[:, :, 16:], a[:, :, 16:], a[:, :, 16 - sh:16 + NT - sh], ALU.add))
                a, c = c, a
            link(V.tensor_tensor(slot, a[:, :, 16:], tot, ALU.subtract))
            link(V.tensor_tensor(slot, slot, cum, ALU.add))
            link(V.tensor_tensor(slot, slot, over(base[:], [P, NX, NT]), ALU.add))
            for k, pick in enumerate((first, second)):
                link(V.tensor_tensor(t2, pick, slot.rearrange("p e t -> p t e"), ALU.mult))
                link(V.tensor_reduce(col[0][:], t2, axis=AX.X, op=ALU.add))
                link(V.tensor_copy(slots[:, k, :], col[0][:]))
            V.nop().then_inc(dispatch_ready, 1)
            count = a[:, :, 15 + NT]
            link(V.tensor_tensor(padslot[:], count, base[:], ALU.add))
            link(V.tensor_scalar(padslots[:], padslot[:], part[:, 0:1], None, ALU.add))
            V.nop().then_inc(dispatch_ready, 1)
            link(V.tensor_tensor(slot, over(count, [P, NX, NT]), thr[:].unsqueeze(1).broadcast_to([P, NX, NT]), ALU.is_gt))
            link(V.tensor_reduce(ntile[:], slot, axis=AX.X, op=ALU.add))
            link(V.memset(cums[0][:, 0:4], 0.0))
            link(V.memset(cums[1][:, 0:4], 0.0))
            link(V.tensor_copy(cums[0][:, 4:], ntile[:]))
            a, c = cums
            for sh in (1, 2, 4):
                link(V.tensor_tensor(c[:, 4:], a[:, 4:], a[:, 4 - sh:4 + NX - sh], ALU.add))
                a, c = c, a
            wide = [P, FTILES, NX]
            link(V.tensor_tensor(passed_by, over(jv[:], wide), a[:, 4:].unsqueeze(1).broadcast_to(wide), ALU.is_ge))
            link(V.tensor_reduce(tile_e[:], passed_by, axis=AX.X, op=ALU.add))
            link(V.tensor_tensor(passed_n, passed_by, ntile[:].unsqueeze(1).broadcast_to(wide), ALU.mult))
            link(V.tensor_reduce(tile_used[:], passed_n, axis=AX.X, op=ALU.add))
            link(V.tensor_tensor(tile_used[:], jv[:], tile_used[:], ALU.subtract))
            link(V.tensor_scalar(tile_row[:], tile_e[:], float(REGION), None, ALU.mult))
            link(V.scalar_tensor_tensor(out=tile_row_i[:], in0=tile_used[:], scalar=float(P), in1=tile_row[:],
                                        op0=ALU.mult, op1=ALU.add))
            link(V.tensor_scalar(tile_w_i[:], tile_e[:], float(NX - 1), None, ALU.min))
            V.nop().then_inc(tiles_ready, 1)

            def keep_tile(i, u):
                j, par = U * i + u, u % 2
                dve.wait_ge(xgT_full, j + 1)
                if not (isinstance(i, int) and j < 2):
                    dve.wait_ge(gu_full, j - 1)
                V.tensor_copy(xgT[par], psX).then_inc(xgT_ready, 1)

            def multiply(i, u):
                j, par = U * i + u, u % 2
                dve.wait_ge(sg_ready, j + 1)
                if not (isinstance(i, int) and j < 2):
                    dve.wait_ge(hhT_full, j - 1)
                V.tensor_tensor(hh[par], sg[par], psU[par], ALU.mult).then_inc(hh_ready, 1)

            def weights(i, u):
                j = U * i + u
                dve.wait_ge(xg_in[u], 16 * (i + 1))
                if not (isinstance(i, int) and i == 0):
                    dve.wait_ge(y_out[u], 16 * i)
                m = xg[u]
                e = tile_e[:, bass.ds(j, 1)]
                d = dsc[u]
                V.scalar_tensor_tensor(out=d[:, 0:1], in0=m[:, C_E0:C_E0 + 1], scalar=e, in1=m[:, C_W0:C_W0 + 1],
                                       op0=ALU.is_equal, op1=ALU.mult).then_inc(dsc_chain, 1)
                V.scalar_tensor_tensor(out=d[:, 1:2], in0=m[:, C_E0:C_E0 + 1], scalar=e, in1=m[:, C_W1:C_W1 + 1],
                                       op0=ALU.not_equal, op1=ALU.mult).then_inc(dsc_chain, 1)
                V.tensor_scalar(d[:, 2:3], m[:, C_E0:C_E0 + 1], e, float(PLANE), ALU.not_equal, ALU.mult).then_inc(dsc_chain, 1)
                dve.wait_ge(dsc_chain, 5 * j + 3)
                V.tensor_tensor(d[:, 3:4], d[:, 0:1], d[:, 1:2], ALU.add).then_inc(dsc_chain, 1)
                V.tensor_tensor(dest[u][:], d[:, 2:3], m[:, C_TOK:C_TOK + 1], ALU.add).then_inc(dsc_chain, 1)

            def weigh(i, u):
                j = U * i + u
                dve.wait_ge(y_full, j + 1)
                dve.wait_ge(dsc_chain, 5 * j + 5)
                V.tensor_scalar(ysb[u][:], psY, dsc[u][:, 3:4], None, ALU.mult).then_inc(y_ready, 1)

            def at(i, u):
                return i + u // U, u % U

            def turn(i, first=False, last=False):
                for u in range(U):
                    if not (last and u == U - 1):
                        keep_tile(*at(i, u + 1))
                    multiply(i, u)
                    if not (first and u < 2):
                        weigh(*at(i, u - 2))
                    weights(i, u)

            keep_tile(0, 0)
            turn(0, first=True)
            with dve.Fori(1, TURNS - 1) as i:
                turn(i)
            turn(TURNS - 1, last=True)
            weigh(TURNS - 1, U - 2)
            weigh(TURNS - 1, U - 1)

            def combine(i, par):
                b = 2 * i + par
                dve.wait_ge(yp_in[par], 32 * (i + 1))
                if not (isinstance(i, int) and i == 0):
                    dve.wait_ge(fin_ready, b - 1)
                V.tensor_tensor(ysum[par], yp[par][:, 0], yp[par][:, 1], ALU.add).then_inc(c2_chain, 1)
                dve.wait_ge(c2_chain, 2 * b + 1)
                V.tensor_tensor(ysum[par], ysum[par], modbc[:, b, 3:4, :].broadcast_to([P, TB, E]), ALU.mult
                                ).then_inc(c2_chain, 1)

            combine(0, 0)
            combine(0, 1)
            with dve.Fori(1, B // 2) as i:
                combine(i, 0)
                combine(i, 1)

        @block.gpsimd
        def _(pool):
            gp = nc.gpsimd
            gp.memset(neghalf[:], -0.5).then_inc(zeroed, 1)
            gp.memset(identf[:], 0.0).then_inc(zeroed, 1)
            gp.memset(identb[:], 0.0).then_inc(zeroed, 1)
            gp.memset(zero_b[:], 0.0).then_inc(zeroed, 1)
            gp.memset(rowsel, 0.0).then_inc(zeroed, 1)
            hold("pool", pool, zeroed, 5)
            gp.affine_select(out=identf[:], in_=identf[:], compare_op=ALU.not_equal, fill=1.0, base=0,
                             pattern=[[-1, P]], channel_multiplier=1).then_inc(ident_ready, 1)
            gp.affine_select(out=identb[:], in_=identb[:], compare_op=ALU.not_equal, fill=1.0, base=0,
                             pattern=[[-1, P]], channel_multiplier=1).then_inc(ident_ready, 1)
            gp.affine_select(out=maskts[:], in_=zero_b[:], compare_op=ALU.is_ge, fill=BIG, base=0,
                             pattern=[[-1, P]], channel_multiplier=1).then_inc(ident_ready, 1)

            def inv_std(m2, ve, rs, src_chain, chain, done, b, freed):
                hold("pool", pool, src_chain, 8 * b + 8)
                if not (isinstance(b, int) and b == 0):
                    hold("pool", pool, freed, b)
                gp.tensor_scalar(ve[:], m2[:, :, 1], EPS, None, ALU.add).then_inc(chain, 1)
                hold("pool", pool, chain, b + 1)
                gp.tensor_tensor(rs[:], ve[:], neghalf[:], ALU.pow).then_inc(done, 1)

            def split(b, res, parts, r1, mid, done):
                hold("pool", pool, r1, b + 1)
                gp.tensor_copy(parts[:, 1, :], res[:]).then_inc(mid, 1)
                hold("pool", pool, mid, b + 1)
                gp.tensor_tensor(parts[:, 2, :], res[:], parts[:, 1, :], ALU.subtract).then_inc(done, 1)

            def split_max(b, g):
                s = 4 * b + g
                hold("pool", pool, nat_done, 44 * b + 11 * g + 11)
                if not (isinstance(b, int) and s == 0):
                    hold("pool", pool, mT_full, s)
                src = negm[:, g % 2]
                gp.tensor_copy(mparts[:, 0], src).then_inc(m_chain, 1)
                hold("pool", pool, m_chain, 3 * s + 1)
                gp.tensor_tensor(mres[:], src, mparts[:, 0], ALU.subtract).then_inc(m_chain, 1)
                hold("pool", pool, m_chain, 3 * s + 2)
                gp.tensor_copy(mparts[:, 1], mres[:]).then_inc(m_chain, 1)
                hold("pool", pool, m_chain, 3 * s + 3)
                gp.tensor_tensor(mparts[:, 2], mres[:], mparts[:, 1], ALU.subtract).then_inc(m_parts, 1)

            def place_v(b):
                hold("pool", pool, v_tmp, b + 1)
                if not (isinstance(b, int) and b == 0):
                    hold("pool", pool, pv_done, 16 * b)
                gp.tensor_copy(vaug[:, :, :, 0:D], vtmp[:]).then_inc(v_ready, 1)

            def mask(b, g):
                for c in range(TB):
                    blk = CHUNKS[c]
                    hold("pool", pool, exp_done, 20 * b + 5 * g + (4 if blk != 2 else 5))
                    base, stride = probs_block(blk)
                    v = probs[:, g % 2, base:base + J * stride].rearrange("p (j c) -> p j c", j=J)[:, :, 0:P]
                    gp.affine_select(out=v, in_=v, compare_op=ALU.is_ge, fill=0.0, base=0,
                                     pattern=[[0, J], [1, P]], channel_multiplier=-1).then_inc(masked, 1)

            def add_attn(b):
                hold("pool", pool, proj_ready, b + 1)
                gp.tensor_tensor(xall[:, b], xall[:, b], proj[:], ALU.add).then_inc(x1_ready, 1)

            def step(b, g, first=False, last=False):
                if not (last and g == G - 1):
                    split_max(b + (g + 1) // G, (g + 1) % G)
                if g == 0 and not last:
                    inv_std(mv, vare, rstd, st_chain, rs_chain, rs_ready, b + 1, xn_ready)
                    split(b + 1, qres, qparts, q_r1, q_mid, q_parts)
                    split(b + 1, kres, kparts, k_r1, k_mid, k_parts)
                if g == 0 and not first:
                    place_v(b)
                if g == 1 and not first:
                    inv_std(mvO, vareO, rstdO, so_chain, rso_chain, rso_ready, b - 1, onn_ready)
                if g == 2 and not first:
                    add_attn(b - 1)
                mask(b, g)

            inv_std(mv, vare, rstd, st_chain, rs_chain, rs_ready, 0, None)
            gp.affine_select(out=rowsel, in_=rowsel, compare_op=ALU.not_equal, fill=1.0, base=0,
                             pattern=[[-1, B], [0, P]], channel_multiplier=1).then_inc(mod8_ready, 1)
            split(0, qres, qparts, q_r1, q_mid, q_parts)
            split(0, kres, kparts, k_r1, k_mid, k_parts)
            gp.memset(vaug[:], 0.0).then_inc(vaug_set, 1)
            hold("pool", pool, vaug_set, 1)
            gp.memset(vaug[:, :, :, D:D + 1], 1.0).then_inc(vaug_set, 1)
            place_v(0)
            split_max(0, 0)
            for g in range(G):
                step(0, g, first=True)
            with pool.Fori(1, B - 1) as b:
                for g in range(G):
                    step(b, g)
            for g in range(G):
                step(B - 1, g, last=True)
            inv_std(mvO, vareO, rstdO, so_chain, rso_chain, rso_ready, B - 1, onn_ready)
            add_attn(B - 1)

            gp.memset(onesrow[:], 1.0).then_inc(f_const, 1)
            gp.memset(ones[:], 1.0).then_inc(f_zero, 1)
            pool.wait_ge(f_zero, 1)
            gp.affine_select(out=before_t[:], in_=ones[:], compare_op=ALU.is_ge, fill=0.0, base=-1,
                             pattern=[[1, P]], channel_multiplier=-1).then_inc(f_const, 1)
            gp.iota(pri_i[:], pattern=[[-1, NX]], base=NX, channel_multiplier=0)
            gp.iota(base_i[:], pattern=[[REGION, NX]], base=0, channel_multiplier=0)
            gp.iota(thr_i[:], pattern=[[P, NT]], base=0, channel_multiplier=0)
            gp.iota(jv_i[:], pattern=[[1, FTILES]], base=0, channel_multiplier=0)
            gp.iota(part_i[:], pattern=[[0, 1]], base=0, channel_multiplier=1)
            gp.iota(tok_i[:], pattern=[[P, NT]], base=0, channel_multiplier=1)
            gp.iota(padtok[:], pattern=[[P, 2 * NX]], base=TOK, channel_multiplier=1).then_inc(f_const, 1)

            def modulate(b):
                hold("pool", pool, sr_chain, 8 * b + 8)
                gp.tensor_scalar(vare[:], mv[:, :, 1], EPS, None, ALU.add).then_inc(rsr_chain, 1)
                hold("pool", pool, rsr_chain, b + 1)
                gp.tensor_tensor(rstd[:], vare[:], neghalf[:], ALU.pow).then_inc(rsr_ready, 1)
                hold("pool", pool, xr_ready, b + 1)
                gp.tensor_tensor(xn[:], xn[:], modbc[:, b, 2:3, :].broadcast_to([P, TB, E]), ALU.mult).then_inc(h2_chain, 1)
                hold("pool", pool, h2_chain, b + 1)
                if not (isinstance(b, int) and b == 0):
                    hold("pool", pool, h2T_ready, b)
                    hold("pool", pool, rows_ready, b)
                gp.tensor_tensor(onn[:], xn[:], modbc[:, b, 1:2, :].broadcast_to([P, TB, E]), ALU.add
                                 ).then_inc(h2_ready, 1)

            modulate(0)
            with pool.Fori(1, B) as b:
                modulate(b)

            pool.wait_ge(dispatch_ready, 1)
            pool.dma_start(xd[NX * REGION:XROWS, :].rearrange("(n p) c -> p n c", p=P), padrows[:, NX:, :]
                           ).then_inc(pads_out, 16)
            pool.wait_ge(dispatch_ready, 2)
            for t in range(NT):
                for k in range(2):
                    gp.indirect_dma_start(xd[:, :], bass.IndirectOffsetOnAxis(ap=slots[:, k, t:t + 1], axis=0),
                                          rows[:, t // TB, t % TB, :], None).then_inc(dispatched, 16)
            pool.wait_ge(dispatch_ready, 3)
            for e in range(NX):
                gp.indirect_dma_start(xd[:, :], bass.IndirectOffsetOnAxis(ap=padslots[:, e:e + 1], axis=0),
                                      padrows[:, e, :], None).then_inc(dispatched, 16)

            def send(i, u):
                hold("pool", pool, y_ready, U * i + u + 1)
                gp.indirect_dma_start(yd[:, :], bass.IndirectOffsetOnAxis(ap=dest[u][:, 0:1], axis=0),
                                      ysb[u][:], None).then_inc(y_out[u], 16)

            with pool.Fori(0, TURNS) as i:
                for u in range(U):
                    send(i, u)
            with pool.Fori(0, B // 2) as i:
                for par in range(2):
                    hold("pool", pool, c2_chain, 2 * (2 * i + par) + 2)
                    gp.tensor_tensor(xall[:, 2 * i + par], xall[:, 2 * i + par], ysum[par], ALU.add).then_inc(fin_ready, 1)


def kernel(**inputs):
    import numpy as np
    import concourse.bacc as bacc
    from concourse import mybir as mb
    from concourse.bass_utils import run_bass_kernel_spmd as run

    a = {n: np.asarray(v) for n, v in inputs.items()}
    arrays = {
        "x": a["L0_attn_x"],
        "cT": a["L0_c"].T,
        "wmod": a["L0_wmod"],
        "wqT": a["L0_attn_Wq"].T,
        "wkT": a["L0_attn_Wk"].T,
        "wvT": a["L0_attn_Wv"].reshape(D, H, E).transpose(2, 1, 0).reshape(E, E),
        "woT": a["L0_attn_Wo"].T,
        "gamma": a["L0_attn_gamma"].reshape(E, 1),
        "beta": a["L0_attn_beta"].reshape(E, 1),
        "confT": a["L0_ffn_conf_w"].T,
        "conf_b": a["L0_ffn_conf_b"].reshape(1, NX),
        "wealth": a["L0_ffn_wealth"].reshape(1, NX),
        "gateT": a["L0_ffn_gate_w"].transpose(2, 0, 1),
        "upT": a["L0_ffn_up_w"].transpose(2, 0, 1),
        "downT": a["L0_ffn_down_w"].reshape(NX, E, FC, P).transpose(3, 0, 2, 1),
    }
    nc = bacc.Bacc("TRN2", target_bir_lowering=False, num_devices=1)
    feed, args = {}, []
    for name, v in arrays.items():
        v = np.ascontiguousarray(v)
        feed["in_" + name] = v
        args.append(nc.dram_tensor("in_" + name, v.shape, mb.dt.from_np(v.dtype), kind="ExternalInput").ap())
    out = nc.dram_tensor("out_0", (B, S, E), mb.dt.float32, kind="ExternalOutput").ap()
    adaln_attention_moe(nc, *args, out)
    r = run(nc, [feed], core_ids=[0])
    return r.results[0]["out_0"]
```

```python
from contextlib import ExitStack

import concourse.bass as bass
from concourse import mybir

ALU = mybir.AluOpType
ACT = mybir.ActivationFunctionType
AX = mybir.AxisListType
F32 = mybir.dt.float32
BF16 = mybir.dt.bfloat16
I32 = mybir.dt.int32

P = 128
B = 8
S = 512
E = 128
H = 16
D = E // H
TB = S // P
G = 4
J = H // G
NT = B * TB
PARTS = 3
KROWS = D * PARTS * PARTS
MROW = KROWS
MPARTS = 2
KALL = KROWS + MPARTS
STEPS = B * G
SOFTMAX_SCALE = float(D) ** -0.5
EPS = 1e-5
BIG = -1.0e30
NAT = 11
UNITS = 10
NBANKS, TBANKS = 4, 2
CHUNKS = (0, 1, 3, 2)

NX = 8
FF = 512
FC = FF // P
REGION = B * S + P
ROW = 132
TOK = B * S
FTILES = (2 * TOK) // P + NX
PLANE = TOK
YROWS = 2 * TOK + 2 * NX * P
XROWS = NX * REGION + NX * P
U = 6
TURNS = FTILES // U
LINKS = 27
C_TOK, C_E0, C_W0, C_W1 = 128, 129, 130, 131


def nat_blocks(k):
    if k < 4:
        return [(0, k, 3, 512)]
    if k < 8:
        return [(0, k - 4, 2, 384)]
    if k < 10:
        return [(0, 2 * (k - 8), 1, 256), (256, 2 * (k - 8) + 1, 1, 256)]
    return [(P * j, j, 0, P) for j in range(J)]


def exp_blocks(u):
    if u < J:
        return [(0, u, 0)]
    if u < 2 * J:
        return [(0, u - J, 1), (384, u - J, 3)]
    return [(0, 2 * (u - 2 * J), 2), (256, 2 * (u - 2 * J) + 1, 2)]


def probs_block(sb):
    return {0: (0, 512, J), 1: (512 * J, 512, 2 * J), 3: (512 * J + 384, 512, 2 * J), 2: (1024 * J, 256, UNITS)}[sb]


def freed_by(unit, units, banks):
    return banks if unit >= banks else units - max(u for u in range(units) if u % banks == unit) + unit


def adaln_attention_moe(nc, x, cT, wmod, wqT, wkT, wvT, woT, gamma, beta,
                        confT, conf_b, wealth, gateT, upT, downT, out):
    qd = nc.dram_tensor("q_parts_dram", [B * E, PARTS, PARTS, S], BF16, kind="Internal").ap()
    kd = nc.dram_tensor("k_parts_dram", [B * E, PARTS, PARTS, S], BF16, kind="Internal").ap()

    xd = nc.dram_tensor("dispatched", [XROWS, ROW], F32, kind="Internal").ap()
    yd = nc.dram_tensor("expert_out", [YROWS, E], F32, kind="Internal").ap()

    with ExitStack() as ctx:
        def sb(name, shape, dt=F32):
            return ctx.enter_context(nc.sbuf_tensor(name, shape, dt))

        sems = {}

        def sem(name):
            sems[name] = ctx.enter_context(nc.semaphore(name))
            return sems[name]

        psN = ctx.enter_context(nc.psum_tensor("psN", [P, NBANKS, 512], F32))
        psT = ctx.enter_context(nc.psum_tensor("psT", [P, TBANKS, 512], F32))
        psO = ctx.enter_context(nc.psum_tensor("psO", [P, 512], F32))
        psM = ctx.enter_context(nc.psum_tensor("psM", [P, 512], F32))

        xall = sb("xall", [P, B, TB, E])
        qst_all = sb("qst_all", [P, G, J, S], BF16)
        kst_all = sb("kst_all", [P, G, J, S], BF16)
        qst = [qst_all[:, g] for g in range(G)]
        kst = [kst_all[:, g] for g in range(G)]
        probs = sb("probs", [P, 2, UNITS * 512])
        vaug = sb("vaug", [P, TB, H, 32])
        vtmp = sb("vtmp", [P, TB, H, D])
        qparts = sb("qparts", [P, PARTS, S], BF16)
        kparts = sb("kparts", [P, PARTS, S], BF16)
        qres = sb("qres", [P, S])
        kres = sb("kres", [P, S])
        hT = sb("hT", [P, S])
        xn = sb("xn", [P, TB, E])
        oT = sb("oT", [P, S])
        on = sb("on", [P, TB, E])
        onn = sb("onn", [P, TB, E])
        lnT = sb("lnT", [P, S])
        proj = sb("proj", [P, TB, E])
        rec = sb("rec", [P, TB, J])
        negm = sb("negm", [P, 2, J, TB])
        mparts = sb("mparts", [P, MPARTS, J, TB], BF16)
        mrow = sb("mrow", [MPARTS * J * TB, P], BF16)
        st = sb("st", [P, TB, 6])
        mv = sb("mv", [P, B, TB, 2])
        vare = sb("vare", [P, B, TB])
        rstd = sb("rstd", [P, B, TB])
        stO = sb("stO", [P, TB, 6])
        mvO = sb("mvO", [P, TB, 2])
        vareO = sb("vareO", [P, TB])
        rstdO = sb("rstdO", [P, TB])
        shift2 = sb("shift2", [P, TB])
        neghalf = sb("neghalf", [P, B, TB])
        identf = sb("identf", [P, P])
        identb = sb("identb", [P, P], BF16)
        zero_b = sb("zero_b", [P, P], BF16)
        maskts = sb("maskts", [P, P], BF16)
        cs = sb("cs", [P, B])
        cse = sb("cse", [P, B])
        csil = sb("csil", [P, B])
        modT = sb("modT", [P, 2, B])
        mod8 = sb("mod8", [B, 4, E])
        modbc = sb("modbc", [P, B, 4, E])
        wq = sb("wq", [P, E])
        wk = sb("wk", [P, E])
        wv = sb("wv", [P, E])
        wo = sb("wo", [P, E])
        gam = sb("gam", [P, 1])
        bet = sb("bet", [P, 1])

        gate_w = sb("gate_w", [P, NX, FF])
        up_w = sb("up_w", [P, NX, FF])
        down_w = sb("down_w", [P, NX, FC, E])
        conf_w = sb("conf_w", [P, NX])
        confb = sb("confb", [1, NX])
        wealth_bc = sb("wealth_bc", [P, NX])
        onesrow = sb("onesrow", [1, P])
        ones = sb("ones", [P, P])
        before_t = sb("before_t", [P, P])
        padtok = sb("padtok", [P, 2 * NX], I32)
        best1, best2, rank1, rank2, dbid, edbid, wsum, wfirst = (
            sb(n, [P, TB]) for n in ("best1", "best2", "rank1", "rank2", "dbid", "edbid", "wsum", "wfirst"))
        slotf = sb("slotf", [P, 2, TB])
        pri = sb("pri", [P, NX])
        rows = sb("rows", [P, TB, ROW])
        xn2 = sb("xn2", [P, TB, E])
        h2 = sb("h2", [P, TB, E])
        h2T = sb("h2T", [P, S])
        st2 = sb("st2", [P, TB, 6])
        mv2 = sb("mv2", [P, TB, 2])
        vare2 = sb("vare2", [P, TB])
        rstd2 = sb("rstd2", [P, TB])
        en = sb("en", [P, TB, NX])
        bids, masked_b, t2, t3, first, second, both = (
            sb(n, [P, TB, NX]) for n in ("bids", "masked_b", "t2", "t3", "first", "second", "both"))
        taken = sb("taken", [P, TB + 1, NX])
        tok = sb("tok", [P, NT])
        part0 = sb("part0", [P, 1])
        pri_i = sb("pri_i", [P, NX], I32)
        tok_i = sb("tok_i", [P, NT], I32)
        base_i = sb("base_i", [P, NX], I32)
        base = sb("base", [P, NX])
        slots = sb("slots", [P, 2, TB], I32)
        thr_i = sb("thr_i", [P, NT], I32)
        thr = sb("thr", [P, NT])
        jv_i = sb("jv_i", [P, FTILES], I32)
        jv = sb("jv", [P, FTILES])
        part_i = sb("part_i", [P, 1], I32)
        part = sb("part", [P, 1])
        ntile = sb("ntile", [P, NX])
        cums = [sb(f"cums{i}", [P, 4 + NX]) for i in range(2)]
        counts = sb("counts", [P, NX])
        padslots = sb("padslots", [P, NX], I32)
        tile_e = sb("tile_e", [P, FTILES])
        tile_row_i = sb("tile_row_i", [P, FTILES], I32)
        tile_w_i = sb("tile_w_i", [P, FTILES], I32)
        dsc = [sb(f"dsc{i}", [P, 4]) for i in range(U)]
        dest = [sb(f"dest{i}", [P, 1], I32) for i in range(U)]

        ew_in, fc_in = sem("ew_in"), sem("fc_in")
        f_zero, f_const, f_chain = sem("f_zero"), sem("f_const"), sem("f_chain")
        sr_chain, rsr_chain, rsr_ready, xr_ready = sem("sr_chain"), sem("rsr_chain"), sem("rsr_ready"), sem("xr_ready")
        h2_chain, h2_ready, h2T_full, h2T_ready = sem("h2_chain"), sem("h2_ready"), sem("h2T_full"), sem("h2T_ready")
        z_full, z_ready = sem("z_full"), sem("z_ready")
        rows_ready = sem("rows_ready")
        taken_chain = sem("taken_chain")
        r_chain, ed_ready, slot_full, count_full = (
            sem("r_chain"), sem("ed_ready"), sem("slot_full"), sem("count_full"))
        dispatch_ready, tiles_ready, dispatched, pads_out = (
            sem("dispatch_ready"), sem("tiles_ready"), sem("dispatched"), sem("pads_out"))
        xg_in = [sem(f"xg_in{i}") for i in range(U)]
        xgT_full, xgT_ready, gu_full, sg_ready, hh_ready = (
            sem("xgT_full"), sem("xgT_ready"), sem("gu_full"), sem("sg_ready"), sem("hh_ready"))
        hhT_full, hhT_ready, y_full, dsc_chain, y_ready = (
            sem("hhT_full"), sem("hhT_ready"), sem("y_full"), sem("dsc_chain"), sem("y_ready"))
        y_out = [sem(f"y_out{i}") for i in range(U)]
        yp_in = [sem(f"yp_in{i}") for i in range(2)]
        c2_chain, c2_ready, fin_ready = sem("c2_chain"), sem("c2_ready"), sem("fin_ready")
        fin_out = [sem(f"fin_out{i}") for i in range(2)]

        c_in, wm_in, w_in = sem("c_in"), sem("wm_in"), sem("w_in")
        x_in = [sem(f"x_in{b}") for b in range(B)]
        zeroed, ident_ready, consts_ready, vaug_set = sem("zeroed"), sem("ident_ready"), sem("consts_ready"), sem("vaug_set")
        c_exp, c_silu, c_chain = sem("c_exp"), sem("c_silu"), sem("c_chain")
        modT_full, modT_ready, mod8_full, mod8_chain, mod8_ready = (
            sem("modT_full"), sem("modT_ready"), sem("mod8_full"), sem("mod8_chain"), sem("mod8_ready"))
        bc_full, bc_ready = sem("bc_full"), sem("bc_ready")
        st_chain, rs_chain, rs_ready, xn_ready = sem("st_chain"), sem("rs_chain"), sem("rs_ready"), sem("xn_ready")
        xT_full, hT_ready = sem("xT_full"), sem("hT_ready")
        q_full, q_hi, q_r1, q_mid, q_parts = sem("q_full"), sem("q_hi"), sem("q_r1"), sem("q_mid"), sem("q_parts")
        k_full, k_hi, k_r1, k_mid, k_parts = sem("k_full"), sem("k_hi"), sem("k_r1"), sem("k_mid"), sem("k_parts")
        v_full, v_tmp, v_ready = sem("v_full"), sem("v_tmp"), sem("v_ready")
        qk_out = sem("qk_out")
        st_in = [sem(f"stack_in{g}") for g in range(G)]
        nat_full, nat_done = sem("nat_full"), sem("nat_done")
        m_chain, m_parts, mT_full, m_row = sem("m_chain"), sem("m_parts"), sem("mT_full"), sem("m_row")
        m_in = [sem(f"m_in{g}") for g in range(G)]
        t_full, exp_done, masked = sem("t_full"), sem("exp_done"), sem("masked")
        pv_done, oT_ready, og_full, og_rec, og_done = (
            sem("pv_done"), sem("oT_ready"), sem("og_full"), sem("og_rec"), sem("og_done"))
        so_chain, rso_chain, rso_ready, onn_ready = sem("so_chain"), sem("rso_chain"), sem("rso_ready"), sem("onn_ready")
        lnT_full, lnT_ready, wo_full, proj_ready, x1_ready = (
            sem("lnT_full"), sem("lnT_ready"), sem("wo_full"), sem("proj_ready"), sem("x1_ready"))
        out_done = sem("out_done")

        banks = [psN[:, i] for i in range(NBANKS)] + [psT[:, i] for i in range(TBANKS)]
        psG, psU, psH, psX = banks[0:2], banks[2:4], banks[4], banks[5][:, 0:P]
        psY = psO[:, 0:E]
        abs8, clamp8, sign8 = (probs[0:B, 1, i * 4 * E:(i + 1) * 4 * E].rearrange("p (i e) -> p i e", i=4)
                               for i in range(3))
        wm = probs[:, 0, 0:6 * E]
        rowsel = probs[0:B, 1, 12 * E:(12 + B) * E].rearrange("p (b t) -> p b t", b=B)
        space_v = [vaug[:].rearrange("p n h c -> p (n h c)"), 0]
        space_p = [probs[:, 1, :], 0]
        space_k = [kst_all[:].rearrange("p g j s -> p (g j s)").bitcast(F32), 0]
        space_q = [qst_all[:].rearrange("p g j s -> p (g j s)").bitcast(F32), 0]

        def carve(space, *shape):
            n = 1
            for d in shape:
                n *= d
            v = space[0][:, space[1]:space[1] + n]
            space[1] += n
            if len(shape) == 1:
                return v
            names = "abc"[:len(shape)]
            return v.rearrange("p (" + " ".join(names) + ") -> p " + " ".join(names),
                               **dict(zip(names, shape)))

        sg, hh, hhT = ([carve(space_p, FF) for _ in range(2)] for _ in range(3))
        xgT = [carve(space_p, P) for _ in range(2)]
        passed_by, passed_n = (carve(space_p, FTILES, NX) for _ in range(2))
        over_thr = carve(space_v, NX, NT)
        tile_used, tile_row = (carve(space_v, FTILES) for _ in range(2))
        xg = [carve(space_k, ROW) for _ in range(U)]
        ysb = [carve(space_k, E) for _ in range(U)]
        padrows = carve(space_q, 2 * NX, ROW)
        yp = [probs[:, i, 0:2 * TB * E].rearrange("p (k n e) -> p k n e", k=2, n=TB) for i in range(2)]
        ysum = [probs[:, i, 2 * TB * E:3 * TB * E].rearrange("p (n e) -> p n e", n=TB) for i in range(2)]

        passed = {e: sem(f"passed_{e}") for e in ("sp", "pe", "dve", "pool")}

        def hold(name, eng, s, value):
            eng.wait_ge(s, value)
            if not isinstance(value, int):
                eng.sem_inc(passed[name], 1)

        def step_at(b, g, n):
            return b + (g + n) // G, (g + n) % G

        def has_earlier(b):
            return not (isinstance(b, int) and b == 0)

        def there(b, g, n):
            return not isinstance(b, int) or 0 <= G * b + g + n < STEPS

        def has_batch(b):
            return not isinstance(b, int) or 0 <= b < B

        def all_steps(eng, step):
            for s in range(2 * G - 1):
                step(s // G, s % G)
            with eng.Fori(2, B - 1) as b:
                step(b - 1, G - 1)
                for g in range(G - 1):
                    step(b, g)
            step(B - 2, G - 1)
            for g in range(G):
                step(B - 1, g)

        block = ctx.enter_context(nc.Block())

        @block.sync
        def _(sp):
            sp.dma_start(cs[:], cT).then_inc(c_in, 16)
            sp.dma_start(wm, wmod).then_inc(wm_in, 16)
            for b in range(B):
                sp.dma_start(xall[:, b], x[b].rearrange("(n p) e -> p n e", p=P)).then_inc(x_in[b], 16)
                if b == 1:
                    sp.dma_start(conf_w[:], confT).then_inc(fc_in, 16)
                    sp.dma_start(confb[:], conf_b).then_inc(fc_in, 16)
                    sp.dma_start(wealth_bc[:], wealth.broadcast_to([P, NX])).then_inc(fc_in, 16)
                if b == 0:
                    for dst, src in ((wq, wqT), (wk, wkT), (wv, wvT), (wo, woT)):
                        sp.dma_start(dst[:], src).then_inc(w_in, 16)
                    sp.dma_start(gam[:], gamma).then_inc(w_in, 16)
                    sp.dma_start(bet[:], beta).then_inc(w_in, 16)

            def parts_out(b, parts, ready, dst):
                hold("sp", sp, ready, b + 1)
                for i in range(PARTS):
                    sp.dma_start(dst(bass.ds(b * E, E), i), parts[:]).then_inc(qk_out, 16)

            def q_out(b):
                parts_out(b, qparts, q_parts, lambda rows, i: qd[rows, :, i, :])

            def k_out(b):
                parts_out(b, kparts, k_parts, lambda rows, i: kd[rows, i, :, :])

            def stacks_in(b, g):
                for dst, src in ((qst[g], qd), (kst[g], kd)):
                    sp.dma_start(dst[0:KROWS], src[bass.ds(b * E + g * J * D, J * D)]
                                 .rearrange("(j d) a b t -> (d a b) j t", j=J)).then_inc(st_in[g], 16)

            def max_rows(b, g):
                hold("sp", sp, m_row, 4 * b + g + 1)
                for a in range(MPARTS):
                    sp.dma_start(qst[g][MROW + a:MROW + a + 1].rearrange("p j (n t) -> p (j n) t", t=P),
                                 mrow[a * J * TB:(a + 1) * J * TB, :]).then_inc(m_in[g], 16)

            def step(b, g):
                if there(b, g, -1) and there(b, g, 3):
                    if g == 1:
                        hold("sp", sp, qk_out, 96 * (b + 2))
                    hold("sp", sp, t_full, UNITS * (4 * b + g))
                    stacks_in(*step_at(b, g, 3))
                if there(b, g, 1):
                    max_rows(*step_at(b, g, 1))
                if g == 0 and has_batch(b + 1):
                    q_out(b + 1)
                    k_out(b + 1)

            hold("sp", sp, consts_ready, G)
            q_out(0)
            k_out(0)
            hold("sp", sp, qk_out, 96)
            for g in range(G):
                stacks_in(0, g)
            max_rows(0, 0)
            sp.dma_start(gate_w[:], gateT).then_inc(ew_in, 16)
            sp.dma_start(up_w[:], upT).then_inc(ew_in, 16)
            sp.dma_start(down_w[:], downT).then_inc(ew_in, 16)
            all_steps(sp, step)

            def tile_in(i, u):
                j = U * i + u
                if not (isinstance(i, int) and i == 0):
                    hold("sp", sp, xgT_full, j - U + 1)
                    hold("sp", sp, dsc_chain, 5 * (j - U + 1))
                row = sp.value_load(tile_row_i[0:1, bass.ds(j, 1)], min_val=0, max_val=XROWS - P)
                sp.dma_start(xg[u], xd[bass.ds(row, P), :]).then_inc(xg_in[u], 16)

            sp.wait_ge(pads_out, 16)
            sp.wait_ge(tiles_ready, 1)
            sp.wait_ge(dispatched, 16 * (2 * NT + NX))
            for u in range(U):
                tile_in(0, u)
            with sp.Fori(1, TURNS) as i:
                for u in range(U):
                    tile_in(i, u)

            def planes_in(i, par):
                b = 2 * i + par
                if not (isinstance(i, int) and i == 0):
                    hold("sp", sp, c2_chain, 2 * (b - 1))
                for k in range(2):
                    sp.dma_start(yp[par][:, k], yd[bass.ds(b * S + k * PLANE, S), :].rearrange("(n p) e -> p n e", p=P)
                                 ).then_inc(yp_in[par], 16)

            def store(i, par):
                b = 2 * i + par
                hold("sp", sp, fin_ready, b + 1)
                sp.dma_start(out[b].rearrange("(n p) e -> p n e", p=P), xall[:, b]).then_inc(fin_out[par], 16)

            for u in range(U):
                sp.wait_ge(y_out[u], 16 * TURNS)
            planes_in(0, 0)
            planes_in(0, 1)
            with sp.Fori(1, B // 2) as i:
                for par in range(2):
                    planes_in(i, par)
                    store(i - 1, par)
            for par in range(2):
                store(B // 2 - 1, par)
            for par in range(2):
                sp.wait_ge(fin_out[par], 16 * (B // 2))

        @block.tensor
        def _(pe):
            bank = [None]

            def take(free=None):
                if bank[0] is not None:
                    pe.wait_ge(*bank[0])
                bank[0] = free

            def nat(b, g, k):
                if k == 0:
                    pe.wait_ge(st_in[g], 32 * (b + 1))
                ago = freed_by(k, NAT, NBANKS)
                if not (isinstance(b, int) and NAT * (4 * b + g) + k < ago):
                    pe.wait_ge(nat_done, NAT * (4 * b + g) + k + 1 - ago)
                for col, j, tb, w in nat_blocks(k):
                    pe.matmul(psN[:, k % NBANKS, col:col + w], qst[g][0:KROWS, j, tb * P:(tb + 1) * P],
                              kst[g][0:KROWS, j, 0:w], start=True, stop=False)
                    mm = pe.matmul(psN[:, k % NBANKS, col + w - P:col + w], identb[:], maskts[:],
                                   start=False, stop=True)
                mm.then_inc(nat_full, 1)

            def scores(b, g, u):
                if u == 0:
                    pe.wait_ge(m_in[g], 16 * MPARTS * (b + 1))
                ago = freed_by(u, UNITS, TBANKS)
                if not (isinstance(b, int) and UNITS * (4 * b + g) + u < ago):
                    pe.wait_ge(exp_done, UNITS * (4 * b + g) + u + 1 - ago)
                for col, j, blk in exp_blocks(u):
                    mm = pe.matmul(psT[:, u % TBANKS, col:col + S - P * blk], kst[g][0:KALL, j, blk * P:(blk + 1) * P],
                                   qst[g][0:KALL, j, blk * P:S], start=True, stop=True)
                mm.then_inc(t_full, 1)

            def values(b, g, c):
                if c == 0:
                    if g == 0:
                        pe.wait_ge(v_ready, b + 1)
                    if not (isinstance(b, int) and b == 0 and g == 0):
                        pe.wait_ge(oT_ready, 4 * b + g)
                pe.wait_ge(masked, 16 * b + 4 * g + c + 1)
                blk = CHUNKS[c]
                base, stride, _ = probs_block(blk)
                w = S - P * blk
                for j in range(J):
                    o = base + stride * j
                    mm = pe.matmul(psO[32 * j:32 * j + 32, blk * P:S], vaug[:, blk, g * J + j, :],
                                   probs[:, g % 2, o:o + w], start=(c == 0), stop=(c == TB - 1))
                mm.then_inc(pv_done, 1)

            def turn_values(b, g):
                take((og_done, 4 * b + g + 1))
                pe.wait_ge(oT_ready, 4 * b + g + 1)
                for n in range(TB):
                    mm = pe.transpose(psM[:, n * P:(n + 1) * P], oT[:, n * P:(n + 1) * P], identf[:])
                mm.then_inc(og_full, 1)

            def turn_max(b, g):
                take((m_row, 4 * b + g + 1))
                hold("pe", pe, m_parts, 4 * b + g + 1)
                pe.transpose(psM[:].bitcast(BF16)[0:MPARTS * J * TB, 0:P], mparts[:].rearrange("p a j n -> p (a j n)"),
                             identb[:]).then_inc(mT_full, 1)

            def turn_x(b):
                take((hT_ready, b + 1))
                pe.wait_ge(xn_ready, b + 1)
                for n in range(TB):
                    mm = pe.transpose(psM[:, n * P:(n + 1) * P], xn[:, n, :], identf[:])
                mm.then_inc(xT_full, 1)

            def project_q(b):
                take((q_r1, b + 1))
                pe.matmul(psM[:], wq[:], hT[:], start=True, stop=True).then_inc(q_full, 1)

            def project_k(b):
                take((k_r1, b + 1))
                pe.matmul(psM[:], wk[:], hT[:], start=True, stop=True).then_inc(k_full, 1)

            def project_v(b):
                take((v_tmp, b + 1))
                for n in range(TB):
                    mm = pe.matmul(psM[:, n * P:(n + 1) * P], hT[:, n * P:(n + 1) * P], wv[:], start=True, stop=True)
                mm.then_inc(v_full, 1)

            def turn_attn(b):
                take((lnT_ready, b + 1))
                pe.wait_ge(onn_ready, b + 1)
                for n in range(TB):
                    mm = pe.transpose(psM[:, n * P:(n + 1) * P], onn[:, n, :], identf[:])
                mm.then_inc(lnT_full, 1)

            def project_o(b):
                take((proj_ready, b + 1))
                for n in range(TB):
                    mm = pe.matmul(psM[:, n * P:(n + 1) * P], lnT[:, n * P:(n + 1) * P], wo[:], start=True, stop=True)
                mm.then_inc(wo_full, 1)

            def turn_h(b):
                take((h2T_ready, b + 1))
                pe.wait_ge(h2_ready, b + 1)
                for n in range(TB):
                    mm = pe.transpose(psM[:, n * P:(n + 1) * P], h2[:, n, :], identf[:])
                mm.then_inc(h2T_full, 1)

            def experts(b):
                take((z_ready, b + 1))
                pe.matmul(psM[:, 0:TB * NX], onesrow[:], confb[:].unsqueeze(1).broadcast_to([1, TB, NX]),
                          start=True, stop=False)
                for n in range(TB):
                    mm = pe.matmul(psM[:, n * NX:(n + 1) * NX], h2T[:, n * P:(n + 1) * P], conf_w[:],
                                   start=False, stop=(n == TB - 1))
                mm.then_inc(z_full, 1)

            def rank(b):
                take((r_chain, LINKS * b + 21))
                pe.wait_ge(taken_chain, 5 * b + 6)
                pe.matmul(psM[:, 0:TB * NX], before_t[:], both[:].rearrange("p n e -> p (n e)"), start=True, stop=False)
                pe.matmul(psM[:, 0:TB * NX], ones[:], taken[:, 0:TB].rearrange("p n e -> p (n e)"),
                          start=False, stop=True).then_inc(slot_full, 1)

            def step(b, g):
                for k in range(NAT):
                    if there(b, g, 2):
                        nat(*step_at(b, g, 2), k)
                    if k < UNITS:
                        scores(b, g, k)
                    if k == 1 and g == 2 and has_batch(b - 2):
                        rank(b - 2)
                    if k == 2 and g == 2 and has_batch(b - 1):
                        turn_attn(b - 1)
                    if k == (3 if g == 2 else 2) and there(b, g, -2):
                        turn_values(*step_at(b, g, -2))
                    if k == (5 if g == 2 else 4) and there(b, g, 1):
                        turn_max(*step_at(b, g, 1))
                    if k in (1, 3, 5) and there(b, g, -1):
                        values(*step_at(b, g, -1), (k + 1) // 2)
                    if k == 9:
                        values(b, g, 0)
                    if g == 3 and has_batch(b + 2):
                        if k == 8:
                            turn_x(b + 2)
                        if k == 10:
                            project_q(b + 2)
                    if g == 0 and has_batch(b - 2):
                        if k == 8:
                            turn_h(b - 2)
                        if k == 10:
                            experts(b - 2)
                    if has_batch(b + 1):
                        if g == 0 and k == 6:
                            project_k(b + 1)
                        if g == 1 and k == 6:
                            project_v(b + 1)
                    if has_batch(b - 1):
                        if g == 2 and k == 7:
                            project_o(b - 1)

            pe.wait_ge(wm_in, 16)
            pe.wait_ge(c_silu, 1)
            take((modT_ready, 1))
            for i in range(2):
                mm = pe.matmul(psM[:, i * B:(i + 1) * B], wm[:, i * E:(i + 1) * E], csil[:], start=True, stop=True)
            mm.then_inc(modT_full, 1)
            take((mod8_chain, 1))
            pe.matmul(psM[0:B, :], csil[:], wm[:, 2 * E:6 * E], start=True, stop=True).then_inc(mod8_full, 1)
            pe.wait_ge(ident_ready, 3)
            pe.wait_ge(w_in, 96)
            turn_x(0)
            pe.wait_ge(hT_ready, 1)
            project_q(0)
            project_k(0)
            project_v(0)
            pe.wait_ge(mod8_ready, 2)
            for b in range(B):
                if b >= TBANKS:
                    pe.wait_ge(bc_ready, b - TBANKS + 1)
                pe.matmul(psT[:, b % TBANKS], rowsel[:, b, :],
                          mod8[:].rearrange("p i e -> p (i e)"), start=True, stop=True).then_inc(bc_full, 1)
            for k in range(NAT):
                nat(0, 0, k)
            turn_max(0, 0)
            for k in range(NAT):
                nat(0, 1, k)
            pe.wait_ge(bc_ready, B)
            turn_x(1)
            project_q(1)
            pe.wait_ge(fc_in, 48)
            pe.wait_ge(f_const, 2)
            for s in range(2 * G - 1):
                step(s // G, s % G)
            with pe.Fori(2, B - 1) as b:
                bank[0] = (m_row, 4 * b)
                step(b - 1, G - 1)
                for g in range(G - 1):
                    step(b, g)
            bank[0] = (m_row, 4 * (B - 1))
            step(B - 2, G - 1)
            for g in range(G):
                step(B - 1, g)
            L = B - 1
            turn_values(L, 2)
            turn_h(L - 1)
            experts(L - 1)
            for c in range(1, TB):
                values(L, 3, c)
            turn_values(L, 3)
            turn_attn(L)
            rank(L - 1)
            project_o(L)
            turn_h(L)
            experts(L)
            rank(L)
            take()
            pe.matmul(psM[:, 0:NX], ones[:], taken[:, TB], start=True, stop=True).then_inc(count_full, 1)

            def turn_in(i, u):
                j, par = U * i + u, u % 2
                pe.wait_ge(xg_in[u], 16 * (i + 1))
                if not (isinstance(i, int) and j == 0):
                    pe.wait_ge(xgT_ready, j)
                pe.transpose(psX, xg[u][:, 0:E], identf[:]).then_inc(xgT_full, 1)

            def gate_up(i, u):
                j, par = U * i + u, u % 2
                e = pe.value_load(tile_w_i[0:1, bass.ds(j, 1)], min_val=0, max_val=NX - 1)
                pe.wait_ge(xgT_ready, j + 1)
                if not (isinstance(i, int) and j < 2):
                    pe.wait_ge(hh_ready, j - 1)
                pe.matmul(psG[par], xgT[par], gate_w[:, bass.ds(e, 1), :], start=True, stop=True)
                pe.matmul(psU[par], xgT[par], up_w[:, bass.ds(e, 1), :], start=True, stop=True).then_inc(gu_full, 1)

            def turn_hidden(i, u):
                j, par = U * i + u, u % 2
                pe.wait_ge(hh_ready, j + 1)
                if not (isinstance(i, int) and j == 0):
                    pe.wait_ge(hhT_ready, j)
                for c in range(FC):
                    mm = pe.transpose(psH[:, c * P:(c + 1) * P], hh[par][:, c * P:(c + 1) * P], identf[:])
                mm.then_inc(hhT_full, 1)

            def down(i, u):
                j, par = U * i + u, u % 2
                e = pe.value_load(tile_w_i[0:1, bass.ds(j, 1)], min_val=0, max_val=NX - 1)
                pe.wait_ge(hhT_ready, j + 1)
                if not (isinstance(i, int) and j == 0):
                    pe.wait_ge(y_ready, j)
                for c in range(FC):
                    mm = pe.matmul(psY, hhT[par][:, c * P:(c + 1) * P], down_w[:, bass.ds(e, 1), c, :],
                                   start=(c == 0), stop=(c == FC - 1))
                mm.then_inc(y_full, 1)

            def at(i, u):
                return i + u // U, u % U

            def turn(i, first=False, last=False):
                for u in range(U):
                    if not (last and u == U - 1):
                        turn_in(*at(i, u + 1))
                    gate_up(i, u)
                    if not (first and u < 1):
                        turn_hidden(*at(i, u - 1))
                    if not (first and u < 2):
                        down(*at(i, u - 2))

            pe.wait_ge(ew_in, 48)
            pe.wait_ge(tiles_ready, 1)
            turn_in(0, 0)
            turn(0, first=True)
            with pe.Fori(1, TURNS - 1) as i:
                turn(i)
            turn(TURNS - 1, last=True)
            turn_hidden(TURNS - 1, U - 1)
            down(TURNS - 1, U - 2)
            down(TURNS - 1, U - 1)

        @block.scalar
        def _(act):
            act.wait_ge(c_in, 16)
            nc.scalar.activation(cse[:], cs[:], ACT.Exp, scale=-1.0).then_inc(c_exp, 1)

            def h_norm(b, tiles=range(TB)):
                if 0 in tiles:
                    act.wait_ge(rsr_ready, b + 1)
                    if has_earlier(b):
                        act.wait_ge(h2_ready, b)
                for n in tiles:
                    last = nc.scalar.activation(xn2[:, n, :], xall[:, b, n, :], ACT.Identity, scale=rstd2[:, n:n + 1],
                                                bias=shift2[:, n:n + 1])
                if TB - 1 in tiles:
                    last.then_inc(xr_ready, 1)

            def shift_in(b):
                act.wait_ge(xT_full, b + 1)
                nc.scalar.activation(hT[:], psM[:], ACT.Identity, scale=modT[:, 1, bass.ds(b, 1)],
                                     bias=modT[:, 0, bass.ds(b, 1)]).then_inc(hT_ready, 1)

            def high(b, full, parts, done):
                act.wait_ge(full, b + 1)
                if not (isinstance(b, int) and b == 0):
                    act.wait_ge(qk_out, 96 * b)
                nc.scalar.activation(parts[:, 0, :], psM[:], ACT.Copy).then_inc(done, 1)

            def keep_v(b):
                act.wait_ge(v_full, b + 1)
                if not (isinstance(b, int) and b == 0):
                    act.wait_ge(v_ready, b)
                nc.scalar.activation(vtmp[:].rearrange("p n h d -> p (n h d)"), psM[:], ACT.Copy).then_inc(v_tmp, 1)

            def keep_max(b, g):
                act.wait_ge(mT_full, 4 * b + g + 1)
                s = 4 * b + g
                if not (isinstance(b, int) and s == 0):
                    pb, pg = (b, g - 1) if g else (b - 1, G - 1)
                    act.wait_ge(m_in[pg], 16 * MPARTS * (pb + 1))
                nc.scalar.activation(mrow[:], psM[:].bitcast(BF16)[0:MPARTS * J * TB, 0:P], ACT.Copy).then_inc(m_row, 1)

            def exps(b, g, u):
                act.wait_ge(t_full, UNITS * (4 * b + g) + u + 1)
                if u == 0 and not (isinstance(b, int) and 4 * b + g < 2):
                    act.wait_ge(pv_done, 16 * b + 4 * g - 4)
                nc.scalar.activation(probs[:, g % 2, 512 * u:512 * (u + 1)], psT[:, u % TBANKS, :], ACT.Exp,
                                     scale=SOFTMAX_SCALE).then_inc(exp_done, 1)

            def keep_values(b, g):
                act.wait_ge(pv_done, 16 * b + 4 * g + 4)
                if not (isinstance(b, int) and 4 * b + g < 1):
                    act.wait_ge(og_full, 4 * b + g)
                nc.scalar.activation(oT[:], psO[:], ACT.Copy).then_inc(oT_ready, 1)

            def keep_attn(b):
                act.wait_ge(lnT_full, b + 1)
                nc.scalar.activation(lnT[:], psM[:], ACT.Identity, scale=gam[:, 0:1], bias=bet[:, 0:1]
                                     ).then_inc(lnT_ready, 1)

            def keep_h(b):
                act.wait_ge(h2T_full, b + 1)
                if has_earlier(b):
                    act.wait_ge(z_full, b)
                nc.scalar.activation(h2T[:], psM[:], ACT.Copy).then_inc(h2T_ready, 1)

            def keep_rows(b):
                act.wait_ge(h2_ready, b + 1)
                if has_earlier(b):
                    act.wait_ge(dispatched, 16 * 2 * TB * b)
                nc.scalar.activation(rows[:, :, 0:E], h2[:], ACT.Copy).then_inc(rows_ready, 1)

            def keep_z(b):
                act.wait_ge(z_full, b + 1)
                if has_earlier(b):
                    act.wait_ge(r_chain, LINKS * b)
                nc.scalar.activation(en[:].rearrange("p n e -> p (n e)"), psM[:, 0:TB * NX], ACT.Exp, scale=-1.0
                                     ).then_inc(z_ready, 1)

            def exp_bids(b):
                act.wait_ge(r_chain, LINKS * b + 16)
                nc.scalar.activation(edbid[:], dbid[:], ACT.Exp).then_inc(ed_ready, 1)

            def step(b, g):
                for k in range(NAT):
                    if g == 0 and k == 0 and has_batch(b + 1) and not (isinstance(b, int) and b == 0):
                        high(b + 1, q_full, qparts, q_hi)
                    if g == 3 and k == 8 and has_batch(b + 2):
                        shift_in(b + 2)
                    if k < UNITS:
                        exps(b, g, k)
                    if k == 6 and there(b, g, -1):
                        keep_values(*step_at(b, g, -1))
                    if k == (5 if g == 2 else 4) and there(b, g, 1):
                        keep_max(*step_at(b, g, 1))
                    if g == 3 and k in (9, 10) and has_batch(b - 1):
                        h_norm(b - 1, (k - 9,))
                    if g == 0 and k in (1, 2) and has_batch(b - 2):
                        h_norm(b - 2, (k + 1,))
                    if g == 0 and has_batch(b - 2):
                        if k == 8:
                            keep_h(b - 2)
                        if k == 9:
                            keep_rows(b - 2)
                        if k == 10:
                            keep_z(b - 2)
                    if g == 1 and k == 10 and has_batch(b - 2):
                        exp_bids(b - 2)
                    if has_batch(b + 1):
                        if g == 0 and k == 6:
                            high(b + 1, k_full, kparts, k_hi)
                        if g == 1 and k == 6:
                            keep_v(b + 1)
                    if g == 2 and k == 2 and has_batch(b - 1):
                        keep_attn(b - 1)

            act.wait_ge(modT_ready, 1)
            shift_in(0)
            high(0, q_full, qparts, q_hi)
            high(0, k_full, kparts, k_hi)
            keep_v(0)
            for b in range(B):
                act.wait_ge(bc_full, b + 1)
                nc.scalar.activation(modbc[:, b].rearrange("p i e -> p (i e)"),
                                     psT[:, b % TBANKS], ACT.Copy).then_inc(bc_ready, 1)
            keep_max(0, 0)
            shift_in(1)
            high(1, q_full, qparts, q_hi)
            all_steps(act, step)
            h_norm(B - 2, (2, 3))
            keep_h(B - 2)
            keep_rows(B - 2)
            keep_z(B - 2)
            keep_values(B - 1, 3)
            exp_bids(B - 2)
            keep_attn(B - 1)
            h_norm(B - 1)
            keep_h(B - 1)
            keep_rows(B - 1)
            keep_z(B - 1)
            exp_bids(B - 1)

            def silu(i, u):
                j, par = U * i + u, u % 2
                act.wait_ge(gu_full, j + 1)
                if not (isinstance(i, int) and j < 2):
                    act.wait_ge(hh_ready, j - 1)
                nc.scalar.activation(sg[par], psG[par], ACT.Silu).then_inc(sg_ready, 1)

            def keep_hidden(i, u):
                j, par = U * i + u, u % 2
                act.wait_ge(hhT_full, j + 1)
                if not (isinstance(i, int) and j < 2):
                    act.wait_ge(y_full, j - 1)
                nc.scalar.activation(hhT[par], psH, ACT.Copy).then_inc(hhT_ready, 1)

            def turn(i, first=False):
                for u in range(U):
                    silu(i, u)
                    if not (first and u == 0):
                        keep_hidden(i + (u - 1) // U, (u - 1) % U)

            nc.scalar.preload_act_table(ACT.Silu)
            turn(0, first=True)
            with act.Fori(1, TURNS) as i:
                turn(i)
            keep_hidden(TURNS - 1, U - 1)

        @block.vector
        def _(dve):
            V = nc.vector
            for g in range(G):
                nc.vector.memset(kst[g][64:96], 1.0).then_inc(consts_ready, 1)
            dve.wait_ge(c_exp, 1)
            nc.vector.tensor_scalar_add(cse[:], cse[:], 1.0).then_inc(c_chain, 1)
            dve.wait_ge(c_chain, 1)
            nc.vector.reciprocal(cse[:], cse[:]).then_inc(c_chain, 1)
            dve.wait_ge(c_chain, 2)
            nc.vector.tensor_tensor(csil[:], cs[:], cse[:], ALU.mult).then_inc(c_silu, 1)

            def stats(src, s6, chain, tiles):
                for n in tiles:
                    V.bn_stats(s6[:, n, :], src[:, n, :]).then_inc(chain, 1)

            def mean_var(s6, m2, chain, b, used):
                if used is not None and has_earlier(b):
                    hold("dve", dve, used, b)
                hold("dve", dve, chain, 8 * b + 4)
                for n in range(TB):
                    V.bn_aggr(m2[:, n, :], s6[:, n, :]).then_inc(chain, 1)

            def norm(src, m2, rs, dst, done, tiles):
                for n in tiles:
                    last = V.tensor_scalar(dst[:, n, :], src[:, n, :], m2(n), rs(n), ALU.subtract, ALU.mult)
                if TB - 1 in tiles:
                    last.then_inc(done, 1)

            def x_stats(b):
                dve.wait_ge(x_in[b], 16)
                if b > 0:
                    dve.wait_ge(st_chain, 8 * b)
                stats(xall[:, b], st, st_chain, range(TB))
                mean_var(st, mv[:, b], st_chain, b, None)

            def x_norm(b, tiles=range(TB)):
                if 0 in tiles and has_earlier(b):
                    hold("dve", dve, xT_full, b)
                norm(xall[:, b], lambda n: mv[:, bass.ds(b, 1), n, 0], lambda n: rstd[:, bass.ds(b, 1), n],
                     xn, xn_ready, tiles)

            def o_norm(b, tiles=range(TB)):
                if 0 in tiles:
                    hold("dve", dve, rso_ready, b + 1)
                    if has_earlier(b):
                        hold("dve", dve, lnT_full, b)
                norm(on, lambda n: mvO[:, n, 0:1], lambda n: rstdO[:, n:n + 1], onn, onn_ready, tiles)

            def max_high(b, g):
                s = 4 * b + g
                hold("dve", dve, nat_done, NAT * (4 * b + g + 1))
                if not (isinstance(b, int) and s == 0):
                    hold("dve", dve, mT_full, s)
                nc.vector.tensor_copy(mparts[:, 0], negm[:, g % 2]).then_inc(m_chain, 1)

            def max_low(b, g):
                hold("dve", dve, m_chain, 4 * b + g + 1)
                nc.vector.tensor_tensor(mparts[:, 1], negm[:, g % 2], mparts[:, 0], ALU.subtract).then_inc(m_parts, 1)

            def middle(b, res, parts, r1, mid):
                hold("dve", dve, r1, b + 1)
                nc.vector.tensor_copy(parts[:, 1, :], res[:]).then_inc(mid, 1)

            def place_v(b):
                hold("dve", dve, v_tmp, b + 1)
                if not (isinstance(b, int) and b == 0):
                    hold("dve", dve, pv_done, 16 * b)
                nc.vector.tensor_copy(vaug[:, :, :, 0:D], vtmp[:]).then_inc(v_ready, 1)

            def residue(b, hi, parts, res, done, split):
                dve.wait_ge(hi, b + 1)
                if not (isinstance(b, int) and b == 0):
                    dve.wait_ge(split, b)
                nc.vector.tensor_tensor(res[:], psM[:], parts[:, 0, :], ALU.subtract).then_inc(done, 1)

            def maxima(b, g, k):
                dve.wait_ge(nat_full, NAT * (4 * b + g) + k + 1)
                if k == 0 and not (isinstance(b, int) and 4 * b + g < 2):
                    hold("dve", dve, m_parts, 4 * b + g - 1)
                blocks = nat_blocks(k)
                w = blocks[0][3]
                dst = negm[:, g % 2, blocks[0][1]:blocks[-1][1] + 1, blocks[0][2]]
                src = psN[:, k % NBANKS, 0:w * len(blocks)].rearrange("p (h s) -> p h s", s=w)
                nc.vector.tensor_reduce(dst, src, axis=AX.X, op=ALU.max, negate=True).then_inc(nat_done, 1)

            def normalise(b, g):
                dve.wait_ge(og_full, 4 * b + g + 1)
                v = psM[:].rearrange("p (n j c) -> p n j c", n=TB, j=J)
                nc.vector.reciprocal(rec[:], v[:, :, :, D]).then_inc(og_rec, 1)
                dve.wait_ge(og_rec, 4 * b + g + 1)
                nc.vector.tensor_tensor(on[:, :, g * J * D:(g + 1) * J * D].rearrange("p n (j d) -> p n j d", j=J),
                                        v[:, :, :, 0:D], rec[:].unsqueeze(3).broadcast_to([P, TB, J, D]),
                                        ALU.mult).then_inc(og_done, 1)

            def gate_out(b):
                dve.wait_ge(wo_full, b + 1)
                if not (isinstance(b, int) and b == 0):
                    dve.wait_ge(x1_ready, b)
                nc.vector.tensor_tensor(proj[:], psM[:].rearrange("p (n e) -> p n e", n=TB),
                                        modbc[:, b, 0:1, :].broadcast_to([P, TB, E]), ALU.mult).then_inc(proj_ready, 1)

            def h_stats(b, tiles):
                hold("dve", dve, x1_ready, b + 1)
                stats(xall[:, b], st2, sr_chain, tiles)

            def over(ap, shape):
                return ap.unsqueeze(2).broadcast_to(shape)

            grid = [P, TB, NX]

            def route(b, i):
                def done(n):
                    hold("dve", dve, r_chain, LINKS * b + n)

                def last(ins):
                    ins.then_inc(r_chain, 1)

                slot = psM[:, 0:TB * NX].rearrange("p (n e) -> p n e", n=TB)
                if i == 0:
                    hold("dve", dve, z_ready, b + 1)
                    last(V.tensor_scalar_add(t2[:], en[:], 1.0))
                if i == 1:
                    done(1)
                    last(V.reciprocal(t3[:], t2[:]))
                if i == 2:
                    done(2)
                    last(V.tensor_tensor(bids[:], t3[:], wealth_bc[:].unsqueeze(1).broadcast_to(grid), ALU.mult))
                for at, src, pick, best, rk in ((3, bids, first, best1, rank1), (9, masked_b, second, best2, rank2)):
                    if i == at:
                        done(at)
                        last(V.tensor_reduce(best[:], src[:], axis=AX.X, op=ALU.max))
                    if i == at + 1:
                        done(at + 1)
                        last(V.tensor_tensor(t2[:], src[:], over(best[:], grid), ALU.is_equal))
                    if i == at + 2:
                        done(at + 2)
                        last(V.tensor_tensor(t3[:], t2[:], pri[:].unsqueeze(1).broadcast_to(grid), ALU.mult))
                    if i == at + 3:
                        done(at + 3)
                        last(V.tensor_reduce(rk[:], t3[:], axis=AX.X, op=ALU.max))
                    if i == at + 4:
                        done(at + 4)
                        last(V.tensor_tensor(pick[:], t3[:], over(rk[:], grid), ALU.is_equal))
                if i == 8:
                    done(8)
                    last(V.scalar_tensor_tensor(out=masked_b[:], in0=first[:], scalar=BIG, in1=bids[:],
                                                op0=ALU.mult, op1=ALU.add))
                if i == 14:
                    done(14)
                    last(V.tensor_tensor(both[:], first[:], second[:], ALU.add))
                if i == 15:
                    done(15)
                    last(V.tensor_tensor(dbid[:], best2[:], best1[:], ALU.subtract))
                if i == 16:
                    hold("dve", dve, rows_ready, b + 1)
                    last(V.tensor_scalar(rows[:, :, C_E0], rank1[:], -1.0, float(NX), ALU.mult, ALU.add))
                if i == 17:
                    last(V.tensor_copy(rows[:, :, C_TOK], tok[:, bass.ds(TB * b, TB)]))
                if i == 18:
                    hold("dve", dve, ed_ready, b + 1)
                    last(V.tensor_scalar_add(wsum[:], edbid[:], 1.0))
                if i == 19:
                    hold("dve", dve, slot_full, b + 1)
                    last(V.tensor_tensor(t2[:], first[:], slot, ALU.mult))
                if i == 20:
                    last(V.tensor_tensor(t3[:], second[:], slot, ALU.mult))
                if i == 21:
                    done(19)
                    last(V.reciprocal(wfirst[:], wsum[:]))
                if i == 22:
                    done(20)
                    last(V.tensor_reduce(slotf[:, 0], t2[:], axis=AX.X, op=ALU.add))
                if i == 23:
                    done(21)
                    last(V.tensor_reduce(slotf[:, 1], t3[:], axis=AX.X, op=ALU.add))
                if i == 24:
                    done(22)
                    last(V.tensor_copy(rows[:, :, C_W0], wfirst[:]))
                if i == 25:
                    last(V.tensor_tensor(rows[:, :, C_W1], edbid[:], wfirst[:], ALU.mult))
                if i == 26:
                    done(24)
                    last(V.tensor_copy(slots[:], slotf[:]))

            def step(b, g):
                for k in range(NAT):
                    if has_batch(b - 2):
                        if g == 1 and k <= 8:
                            route(b - 2, 2 * k)
                        if g == 2 and k == 1:
                            route(b - 2, 18)
                        if g == 2 and k == 2:
                            route(b - 2, 21)
                        if g == 2 and k == 3:
                            route(b - 2, 24)
                            route(b - 2, 25)
                    if there(b, g, 2):
                        maxima(*step_at(b, g, 2), k)
                    if has_batch(b - 2):
                        if g == 1 and k <= 8:
                            route(b - 2, 2 * k + 1)
                        if g == 2 and k == 1:
                            route(b - 2, 19)
                            route(b - 2, 20)
                        if g == 2 and k == 2:
                            route(b - 2, 22)
                            route(b - 2, 23)
                        if g == 2 and k == 3:
                            route(b - 2, 26)
                    if k == 0 and there(b, g, 1):
                        max_high(*step_at(b, g, 1))
                    if k == 1 and there(b, g, 1):
                        max_low(*step_at(b, g, 1))
                    if k == (3 if g == 2 else 2) and there(b, g, -2):
                        normalise(*step_at(b, g, -2))
                    if g == 3 and has_batch(b - 1):
                        if k == 3:
                            h_stats(b - 1, (0, 1))
                        if k == 4:
                            h_stats(b - 1, (2, 3))
                        if k == 5:
                            mean_var(st2, mv2, sr_chain, b - 1, rsr_ready)
                    if g == 3 and has_batch(b + 2):
                        if k == 2:
                            x_norm(b + 2, (0, 1))
                        if k == 4:
                            x_norm(b + 2, (2, 3))
                    if g == 0 and has_batch(b + 1):
                        if k == 0 and has_earlier(b):
                            residue(b + 1, q_hi, qparts, qres, q_r1, q_parts)
                        if k == 2 and has_earlier(b):
                            middle(b + 1, qres, qparts, q_r1, q_mid)
                        if k == 7:
                            residue(b + 1, k_hi, kparts, kres, k_r1, k_parts)
                        if k == 8:
                            middle(b + 1, kres, kparts, k_r1, k_mid)
                    if g == 0 and k == 6 and has_earlier(b):
                        place_v(b)
                    if has_batch(b - 1):
                        if g == 1:
                            if k == 2:
                                hold("dve", dve, og_done, 4 * b)
                                stats(on, stO, so_chain, (0, 1))
                            if k == 3:
                                stats(on, stO, so_chain, (2, 3))
                            if k == 4:
                                mean_var(stO, mvO, so_chain, b - 1, onn_ready)
                            if k == 6:
                                o_norm(b - 1, (0, 1))
                            if k == 7:
                                o_norm(b - 1, (2, 3))
                        if g == 2 and k == 8:
                            gate_out(b - 1)

            links = [0]

            def link(ins):
                ins.then_inc(f_chain, 1)
                links[0] += 1
                dve.wait_ge(f_chain, links[0])

            x_stats(0)
            dve.wait_ge(modT_full, 1)
            nc.vector.tensor_scalar_add(modT[:, 1, :], psM[:, B:2 * B], 1.0).then_inc(c_chain, 1)
            nc.vector.tensor_copy(modT[:, 0, :], psM[:, 0:B]).then_inc(modT_ready, 1)
            dve.wait_ge(mod8_full, 1)
            nc.vector.tensor_copy(mod8[:].rearrange("p i e -> p (i e)"), psM[0:B, :]).then_inc(mod8_chain, 1)
            dve.wait_ge(rs_ready, 1)
            x_norm(0)
            dve.wait_ge(mod8_chain, 1)
            for i in (0, 3):
                nc.vector.scalar_tensor_tensor(out=abs8[:, i, :], in0=mod8[:, i, :], scalar=-1.0, in1=mod8[:, i, :],
                                               op0=ALU.mult, op1=ALU.max).then_inc(mod8_chain, 1)
                nc.vector.tensor_scalar(sign8[:, i, :], mod8[:, i, :], 0.0, 2.0, ALU.is_ge, ALU.mult).then_inc(mod8_chain, 1)
            dve.wait_ge(mod8_chain, 5)
            for i in (0, 3):
                nc.vector.tensor_scalar_max(clamp8[:, i, :], abs8[:, i, :], 0.25).then_inc(mod8_chain, 1)
            dve.wait_ge(mod8_chain, 7)
            for i in (0, 3):
                nc.vector.scalar_tensor_tensor(out=mod8[:, i, :], in0=sign8[:, i, :], scalar=-1.0, in1=clamp8[:, i, :],
                                               op0=ALU.add, op1=ALU.mult).then_inc(mod8_chain, 1)
            nc.vector.tensor_scalar_add(mod8[:, 2, :], mod8[:, 2, :], 1.0).then_inc(mod8_chain, 1)
            dve.wait_ge(mod8_chain, 10)
            nc.vector.nop().then_inc(mod8_ready, 1)
            residue(0, q_hi, qparts, qres, q_r1, q_parts)
            middle(0, qres, qparts, q_r1, q_mid)
            residue(0, k_hi, kparts, kres, k_r1, k_parts)
            middle(0, kres, kparts, k_r1, k_mid)
            dve.wait_ge(vaug_set, 2)
            place_v(0)
            dve.wait_ge(f_const, 3)
            for dst, src in ((pri, pri_i), (base, base_i), (thr, thr_i), (jv, jv_i), (part, part_i), (tok, tok_i)):
                link(V.tensor_copy(dst[:], src[:]))
            link(V.tensor_scalar(part0[:], part[:], 0.0, None, ALU.is_equal))
            link(V.tensor_scalar(taken[:, TB], base[:], part0[:, 0:1], None, ALU.mult))
            V.nop().then_inc(taken_chain, 1)
            dve.wait_ge(fc_in, 48)
            for b in range(1, B):
                x_stats(b)
            dve.wait_ge(rs_ready, 2)
            x_norm(1)
            for k in range(NAT):
                maxima(0, 0, k)
            max_high(0, 0)
            max_low(0, 0)
            for k in range(NAT):
                maxima(0, 1, k)
            residue(1, q_hi, qparts, qres, q_r1, q_parts)
            middle(1, qres, qparts, q_r1, q_mid)
            all_steps(dve, step)
            L = B - 1
            normalise(L, 2)
            for i in range(18):
                route(L - 1, i)
            normalise(L, 3)
            hold("dve", dve, og_done, 4 * B)
            stats(on, stO, so_chain, range(TB))
            mean_var(stO, mvO, so_chain, L, onn_ready)
            o_norm(L)
            for i in range(18, LINKS):
                route(L - 1, i)
            gate_out(L)
            link(V.memset(padrows, 0.0))
            link(V.memset(padrows[:, :, C_E0], -1.0))
            V.tensor_copy(padrows[:, :, C_TOK], padtok[:]).then_inc(dispatch_ready, 1)
            h_stats(L, range(TB))
            mean_var(st2, mv2, sr_chain, L, rsr_ready)
            for i in range(LINKS):
                route(L, i)
            dve.wait_ge(count_full, 1)
            link(V.tensor_scalar(padslots[:], psM[:, 0:NX], part[:, 0:1], None, ALU.add))
            V.nop().then_inc(dispatch_ready, 1)
            link(V.tensor_tensor(counts[:], psM[:, 0:NX], base[:], ALU.subtract))
            link(V.tensor_tensor(over_thr, over(counts[:], [P, NX, NT]), thr[:].unsqueeze(1).broadcast_to([P, NX, NT]),
                                 ALU.is_gt))
            link(V.tensor_reduce(ntile[:], over_thr, axis=AX.X, op=ALU.add))
            link(V.memset(cums[0][:, 0:4], 0.0))
            link(V.memset(cums[1][:, 0:4], 0.0))
            link(V.tensor_copy(cums[0][:, 4:], ntile[:]))
            a, c = cums
            for sh in (1, 2, 4):
                link(V.tensor_tensor(c[:, 4:], a[:, 4:], a[:, 4 - sh:4 + NX - sh], ALU.add))
                a, c = c, a
            wide = [P, FTILES, NX]
            link(V.tensor_tensor(passed_by, over(jv[:], wide), a[:, 4:].unsqueeze(1).broadcast_to(wide), ALU.is_ge))
            link(V.tensor_reduce(tile_e[:], passed_by, axis=AX.X, op=ALU.add))
            link(V.tensor_tensor(passed_n, passed_by, ntile[:].unsqueeze(1).broadcast_to(wide), ALU.mult))
            link(V.tensor_reduce(tile_used, passed_n, axis=AX.X, op=ALU.add))
            link(V.tensor_tensor(tile_used, jv[:], tile_used, ALU.subtract))
            link(V.tensor_scalar(tile_row, tile_e[:], float(REGION), None, ALU.mult))
            link(V.scalar_tensor_tensor(out=tile_row_i[:], in0=tile_used, scalar=float(P), in1=tile_row,
                                        op0=ALU.mult, op1=ALU.add))
            link(V.tensor_scalar(tile_w_i[:], tile_e[:], float(NX - 1), None, ALU.min))
            V.nop().then_inc(tiles_ready, 1)

            def keep_tile(i, u):
                j, par = U * i + u, u % 2
                dve.wait_ge(xgT_full, j + 1)
                if not (isinstance(i, int) and j < 2):
                    dve.wait_ge(gu_full, j - 1)
                V.tensor_copy(xgT[par], psX).then_inc(xgT_ready, 1)

            def multiply(i, u):
                j, par = U * i + u, u % 2
                dve.wait_ge(sg_ready, j + 1)
                if not (isinstance(i, int) and j < 2):
                    dve.wait_ge(hhT_full, j - 1)
                V.tensor_tensor(hh[par], sg[par], psU[par], ALU.mult).then_inc(hh_ready, 1)

            def weights(i, u):
                j = U * i + u
                dve.wait_ge(xg_in[u], 16 * (i + 1))
                if not (isinstance(i, int) and i == 0):
                    dve.wait_ge(y_out[u], 16 * i)
                m = xg[u]
                e = tile_e[:, bass.ds(j, 1)]
                d = dsc[u]
                V.scalar_tensor_tensor(out=d[:, 0:1], in0=m[:, C_E0:C_E0 + 1], scalar=e, in1=m[:, C_W0:C_W0 + 1],
                                       op0=ALU.is_equal, op1=ALU.mult).then_inc(dsc_chain, 1)
                V.scalar_tensor_tensor(out=d[:, 1:2], in0=m[:, C_E0:C_E0 + 1], scalar=e, in1=m[:, C_W1:C_W1 + 1],
                                       op0=ALU.not_equal, op1=ALU.mult).then_inc(dsc_chain, 1)
                V.tensor_scalar(d[:, 2:3], m[:, C_E0:C_E0 + 1], e, float(PLANE), ALU.not_equal, ALU.mult).then_inc(dsc_chain, 1)
                dve.wait_ge(dsc_chain, 5 * j + 3)
                V.tensor_tensor(d[:, 3:4], d[:, 0:1], d[:, 1:2], ALU.add).then_inc(dsc_chain, 1)
                V.tensor_tensor(dest[u][:], d[:, 2:3], m[:, C_TOK:C_TOK + 1], ALU.add).then_inc(dsc_chain, 1)

            def weigh(i, u):
                j = U * i + u
                dve.wait_ge(y_full, j + 1)
                dve.wait_ge(dsc_chain, 5 * j + 5)
                V.tensor_scalar(ysb[u], psY, dsc[u][:, 3:4], None, ALU.mult).then_inc(y_ready, 1)

            def at(i, u):
                return i + u // U, u % U

            def turn(i, first=False, last=False):
                for u in range(U):
                    if not (last and u == U - 1):
                        keep_tile(*at(i, u + 1))
                    multiply(i, u)
                    if not (first and u < 2):
                        weigh(*at(i, u - 2))
                    weights(i, u)

            keep_tile(0, 0)
            turn(0, first=True)
            with dve.Fori(1, TURNS - 1) as i:
                turn(i)
            turn(TURNS - 1, last=True)
            weigh(TURNS - 1, U - 2)
            weigh(TURNS - 1, U - 1)

            def combine(i, par):
                b = 2 * i + par
                dve.wait_ge(yp_in[par], 32 * (i + 1))
                if not (isinstance(i, int) and i == 0):
                    dve.wait_ge(fin_ready, b - 1)
                V.tensor_tensor(ysum[par], yp[par][:, 0], yp[par][:, 1], ALU.add).then_inc(c2_chain, 1)
                dve.wait_ge(c2_chain, 2 * b + 1)
                V.tensor_tensor(ysum[par], ysum[par], modbc[:, b, 3:4, :].broadcast_to([P, TB, E]), ALU.mult
                                ).then_inc(c2_chain, 1)

            combine(0, 0)
            combine(0, 1)
            with dve.Fori(1, B // 2) as i:
                combine(i, 0)
                combine(i, 1)

        @block.gpsimd
        def _(pool):
            gp = nc.gpsimd
            gp.memset(neghalf[:], -0.5).then_inc(zeroed, 1)
            gp.memset(identf[:], 0.0).then_inc(zeroed, 1)
            gp.memset(identb[:], 0.0).then_inc(zeroed, 1)
            gp.memset(zero_b[:], 0.0).then_inc(zeroed, 1)
            gp.memset(rowsel, 0.0).then_inc(zeroed, 1)
            hold("pool", pool, zeroed, 5)
            gp.affine_select(out=identf[:], in_=identf[:], compare_op=ALU.not_equal, fill=1.0, base=0,
                             pattern=[[-1, P]], channel_multiplier=1).then_inc(ident_ready, 1)
            gp.affine_select(out=identb[:], in_=identb[:], compare_op=ALU.not_equal, fill=1.0, base=0,
                             pattern=[[-1, P]], channel_multiplier=1).then_inc(ident_ready, 1)
            gp.affine_select(out=maskts[:], in_=zero_b[:], compare_op=ALU.is_ge, fill=BIG, base=0,
                             pattern=[[-1, P]], channel_multiplier=1).then_inc(ident_ready, 1)

            def inv_std(m2, ve, rs, chain, ready):
                gp.tensor_scalar(ve, m2, EPS, None, ALU.add).then_inc(chain[0], 1)
                hold("pool", pool, *chain)
                n = neghalf[:, 0] if len(ve.shape) == 2 else neghalf[:, 0:ve.shape[1]]
                gp.tensor_tensor(rs, ve, n, ALU.pow).then_inc(ready, 1)

            def x_inv(batches, n):
                pool.wait_ge(st_chain, 8 * batches.stop)
                inv_std(mv[:, batches, :, 1], vare[:, batches], rstd[:, batches], (rs_chain, n), rs_ready)

            def o_inv(b):
                hold("pool", pool, so_chain, 8 * b + 8)
                if has_earlier(b):
                    hold("pool", pool, onn_ready, b)
                inv_std(mvO[:, :, 1], vareO[:], rstdO[:], (rso_chain, b + 1), rso_ready)

            def h_inv(b):
                hold("pool", pool, sr_chain, 8 * b + 8)
                if has_earlier(b):
                    hold("pool", pool, xr_ready, b)
                gp.tensor_scalar(shift2[:], mv2[:, :, 0], -1.0, None, ALU.mult).then_inc(rsr_chain, 1)
                inv_std(mv2[:, :, 1], vare2[:], rstd2[:], (rsr_chain, 3 * b + 2), rsr_chain)
                hold("pool", pool, rsr_chain, 3 * b + 3)
                gp.tensor_tensor(shift2[:], shift2[:], rstd2[:], ALU.mult).then_inc(rsr_ready, 1)

            def low(b, res, parts, mid, done):
                hold("pool", pool, mid, b + 1)
                gp.tensor_tensor(parts[:, 2, :], res[:], parts[:, 1, :], ALU.subtract).then_inc(done, 1)

            def mask(b, g, c):
                base, stride, units = probs_block(CHUNKS[c])
                hold("pool", pool, exp_done, UNITS * (4 * b + g) + units)
                v = probs[:, g % 2, base:base + J * stride].rearrange("p (j c) -> p j c", j=J)[:, :, 0:P]
                gp.affine_select(out=v, in_=v, compare_op=ALU.is_ge, fill=0.0, base=0,
                                 pattern=[[0, J], [1, P]], channel_multiplier=-1).then_inc(masked, 1)

            def add_attn(b):
                hold("pool", pool, proj_ready, b + 1)
                gp.tensor_tensor(xall[:, b], xall[:, b], proj[:], ALU.add).then_inc(x1_ready, 1)

            def h_scale(b):
                hold("pool", pool, xr_ready, b + 1)
                gp.tensor_tensor(xn2[:], xn2[:], modbc[:, b, 2:3, :].broadcast_to([P, TB, E]), ALU.mult).then_inc(h2_chain, 1)

            def h_shift(b):
                hold("pool", pool, h2_chain, b + 1)
                if has_earlier(b):
                    hold("pool", pool, h2T_full, b)
                    hold("pool", pool, rows_ready, b)
                gp.tensor_tensor(h2[:], xn2[:], modbc[:, b, 1:2, :].broadcast_to([P, TB, E]), ALU.add).then_inc(h2_ready, 1)

            def count(b):
                if has_earlier(b):
                    hold("pool", pool, slot_full, b)
                hold("pool", pool, taken_chain, 5 * b + 1)
                gp.tensor_copy(taken[:, 0], taken[:, TB]).then_inc(taken_chain, 1)
                hold("pool", pool, r_chain, LINKS * b + 15)
                for n in range(TB):
                    hold("pool", pool, taken_chain, 5 * b + 2 + n)
                    gp.tensor_tensor(taken[:, n + 1], taken[:, n], both[:, n], ALU.add).then_inc(taken_chain, 1)

            def scatter(b, tiles):
                hold("pool", pool, r_chain, LINKS * (b + 1))
                for n in tiles:
                    for k in range(2):
                        gp.indirect_dma_start(xd[:, :], bass.IndirectOffsetOnAxis(ap=slots[:, k, n:n + 1], axis=0),
                                              rows[:, n, :], None).then_inc(dispatched, 16)

            def step(b, g):
                if g == 0 and has_batch(b - 2):
                    h_scale(b - 2)
                if g == 0 and has_batch(b + 1) and has_earlier(b):
                    low(b + 1, qres, qparts, q_mid, q_parts)
                if g == 0 and has_batch(b - 2):
                    h_shift(b - 2)
                if g == 1 and has_batch(b - 1):
                    o_inv(b - 1)
                mask(b, g, 0)
                if g == 2 and has_batch(b - 2):
                    scatter(b - 2, (0, 1))
                if g == 3 and has_batch(b - 1):
                    h_inv(b - 1)
                mask(b, g, 1)
                mask(b, g, 2)
                if g == 0 and has_batch(b + 1):
                    low(b + 1, kres, kparts, k_mid, k_parts)
                mask(b, g, 3)
                if g == 1 and has_batch(b - 2):
                    count(b - 2)
                if g == 2 and has_batch(b - 1):
                    add_attn(b - 1)
                if g == 2 and has_batch(b - 2):
                    scatter(b - 2, (2, 3))

            x_inv(slice(0, 1), 1)
            gp.affine_select(out=rowsel, in_=rowsel, compare_op=ALU.not_equal, fill=1.0, base=0,
                             pattern=[[-1, B], [0, P]], channel_multiplier=1).then_inc(mod8_ready, 1)
            gp.memset(vaug[:], 0.0).then_inc(vaug_set, 1)
            hold("pool", pool, vaug_set, 1)
            gp.memset(vaug[:, :, :, D:D + 1], 1.0).then_inc(vaug_set, 1)
            gp.memset(onesrow[:], 1.0).then_inc(f_const, 1)
            gp.memset(ones[:], 1.0).then_inc(f_zero, 1)
            pool.wait_ge(f_zero, 1)
            gp.affine_select(out=before_t[:], in_=ones[:], compare_op=ALU.is_ge, fill=0.0, base=-1,
                             pattern=[[1, P]], channel_multiplier=-1).then_inc(f_const, 1)
            gp.iota(pri_i[:], pattern=[[-1, NX]], base=NX, channel_multiplier=0)
            gp.iota(base_i[:], pattern=[[REGION, NX]], base=0, channel_multiplier=0)
            gp.iota(thr_i[:], pattern=[[P, NT]], base=0, channel_multiplier=0)
            gp.iota(jv_i[:], pattern=[[1, FTILES]], base=0, channel_multiplier=0)
            gp.iota(part_i[:], pattern=[[0, 1]], base=0, channel_multiplier=1)
            gp.iota(tok_i[:], pattern=[[P, NT]], base=0, channel_multiplier=1)
            gp.iota(padtok[:], pattern=[[P, 2 * NX]], base=TOK, channel_multiplier=1).then_inc(f_const, 1)

            low(0, qres, qparts, q_mid, q_parts)
            low(0, kres, kparts, k_mid, k_parts)
            x_inv(slice(1, B), 2)
            low(1, qres, qparts, q_mid, q_parts)
            all_steps(pool, step)
            h_scale(B - 2)
            h_shift(B - 2)
            o_inv(B - 1)
            count(B - 2)
            scatter(B - 2, range(TB))
            add_attn(B - 1)
            h_inv(B - 1)
            h_scale(B - 1)
            h_shift(B - 1)

            pool.wait_ge(dispatch_ready, 1)
            pool.dma_start(xd[NX * REGION:XROWS, :].rearrange("(n p) c -> p n c", p=P), padrows[:, NX:, :]
                           ).then_inc(pads_out, 16)
            count(B - 1)
            scatter(B - 1, range(TB))
            pool.wait_ge(dispatch_ready, 2)
            for e in range(NX):
                gp.indirect_dma_start(xd[:, :], bass.IndirectOffsetOnAxis(ap=padslots[:, e:e + 1], axis=0),
                                      padrows[:, e, :], None).then_inc(dispatched, 16)

            def send(i, u):
                hold("pool", pool, y_ready, U * i + u + 1)
                gp.indirect_dma_start(yd[:, :], bass.IndirectOffsetOnAxis(ap=dest[u][:, 0:1], axis=0),
                                      ysb[u], None).then_inc(y_out[u], 16)

            with pool.Fori(0, TURNS) as i:
                for u in range(U):
                    send(i, u)
            with pool.Fori(0, B // 2) as i:
                for par in range(2):
                    hold("pool", pool, c2_chain, 2 * (2 * i + par) + 2)
                    gp.tensor_tensor(xall[:, 2 * i + par], xall[:, 2 * i + par], ysum[par], ALU.add).then_inc(fin_ready, 1)


def kernel(**inputs):
    import numpy as np
    import concourse.bacc as bacc
    from concourse import mybir as mb
    from concourse.bass_utils import run_bass_kernel_spmd as run

    a = {n: np.asarray(v) for n, v in inputs.items()}
    arrays = {
        "x": a["L0_attn_x"],
        "cT": a["L0_c"].T,
        "wmod": a["L0_wmod"],
        "wqT": a["L0_attn_Wq"].T,
        "wkT": a["L0_attn_Wk"].T,
        "wvT": a["L0_attn_Wv"].reshape(D, H, E).transpose(2, 1, 0).reshape(E, E),
        "woT": a["L0_attn_Wo"].T,
        "gamma": a["L0_attn_gamma"].reshape(E, 1),
        "beta": a["L0_attn_beta"].reshape(E, 1),
        "confT": a["L0_ffn_conf_w"].T,
        "conf_b": a["L0_ffn_conf_b"].reshape(1, NX),
        "wealth": a["L0_ffn_wealth"].reshape(1, NX),
        "gateT": a["L0_ffn_gate_w"].transpose(2, 0, 1),
        "upT": a["L0_ffn_up_w"].transpose(2, 0, 1),
        "downT": a["L0_ffn_down_w"].reshape(NX, E, FC, P).transpose(3, 0, 2, 1),
    }
    nc = bacc.Bacc("TRN2", target_bir_lowering=False, num_devices=1)
    feed, args = {}, []
    for name, v in arrays.items():
        v = np.ascontiguousarray(v)
        feed["in_" + name] = v
        args.append(nc.dram_tensor("in_" + name, v.shape, mb.dt.from_np(v.dtype), kind="ExternalInput").ap())
    out = nc.dram_tensor("out_0", (B, S, E), mb.dt.float32, kind="ExternalOutput").ap()
    adaln_attention_moe(nc, *args, out)
    r = run(nc, [feed], core_ids=[0])
    return r.results[0]["out_0"]
```

```python
from contextlib import ExitStack

import concourse.bass as bass
from concourse import mybir

ALU = mybir.AluOpType
ACT = mybir.ActivationFunctionType
AX = mybir.AxisListType
F32 = mybir.dt.float32
BF16 = mybir.dt.bfloat16
I32 = mybir.dt.int32

P = 128
B = 8
S = 512
E = 128
H = 16
D = E // H
TB = S // P
G = 4
J = H // G
NT = B * TB
PARTS = 3
KROWS = D * PARTS * PARTS
MROW = KROWS
MPARTS = 2
KALL = KROWS + MPARTS
STEPS = B * G
SOFTMAX_SCALE = float(D) ** -0.5
EPS = 1e-5
BIG = -1.0e30
NAT = 11
UNITS = 10
NBANKS, TBANKS = 4, 2
CHUNKS = (0, 1, 3, 2)

NX = 8
FF = 512
FC = FF // P
REGION = B * S + P
ROW = 132
TOK = B * S
FTILES = (2 * TOK) // P + NX - 1
PLANE = TOK
YROWS = 2 * TOK + 2 * NX * P
XROWS = NX * REGION + NX * P
U = 6
TURNS = -(-FTILES // U)
LAST = FTILES - U * (TURNS - 1)
LINKS = 27
C_TOK, C_E0, C_W0, C_W1 = 128, 129, 130, 131


def nat_blocks(k):
    if k < 4:
        return [(0, k, 3, 512)]
    if k < 8:
        return [(0, k - 4, 2, 384)]
    if k < 10:
        return [(0, 2 * (k - 8), 1, 256), (256, 2 * (k - 8) + 1, 1, 256)]
    return [(P * j, j, 0, P) for j in range(J)]


def exp_blocks(u):
    if u < J:
        return [(0, u, 0)]
    if u < 2 * J:
        return [(0, u - J, 1), (384, u - J, 3)]
    return [(0, 2 * (u - 2 * J), 2), (256, 2 * (u - 2 * J) + 1, 2)]


def probs_block(sb):
    return {0: (0, 512, J), 1: (512 * J, 512, 2 * J), 3: (512 * J + 384, 512, 2 * J), 2: (1024 * J, 256, UNITS)}[sb]


def freed_by(unit, units, banks):
    return banks if unit >= banks else units - max(u for u in range(units) if u % banks == unit) + unit


def adaln_attention_moe(nc, x, cT, wmod, wqT, wkT, wvT, woT, gamma, beta,
                        confT, conf_b, wealth, gateT, upT, downT, out):
    qd = nc.dram_tensor("q_parts_dram", [B * E, PARTS, PARTS, S], BF16, kind="Internal").ap()
    kd = nc.dram_tensor("k_parts_dram", [B * E, PARTS, PARTS, S], BF16, kind="Internal").ap()

    xd = nc.dram_tensor("dispatched", [XROWS, ROW], F32, kind="Internal").ap()
    yd = nc.dram_tensor("expert_out", [YROWS, E], F32, kind="Internal").ap()

    with ExitStack() as ctx:
        def sb(name, shape, dt=F32):
            return ctx.enter_context(nc.sbuf_tensor(name, shape, dt))

        sems = {}

        def sem(name):
            sems[name] = ctx.enter_context(nc.semaphore(name))
            return sems[name]

        psN = ctx.enter_context(nc.psum_tensor("psN", [P, NBANKS, 512], F32))
        psT = ctx.enter_context(nc.psum_tensor("psT", [P, TBANKS, 512], F32))
        psO = ctx.enter_context(nc.psum_tensor("psO", [P, 512], F32))
        psM = ctx.enter_context(nc.psum_tensor("psM", [P, 512], F32))

        xall = sb("xall", [P, B, TB, E])
        qst_all = sb("qst_all", [P, G, J, S], BF16)
        kst_all = sb("kst_all", [P, G, J, S], BF16)
        qst = [qst_all[:, g] for g in range(G)]
        kst = [kst_all[:, g] for g in range(G)]
        probs = sb("probs", [P, 2, UNITS * 512])
        vaug = sb("vaug", [P, TB, H, 32])
        vtmp = sb("vtmp", [P, TB, H, D])
        qparts = sb("qparts", [P, PARTS, S], BF16)
        kparts = sb("kparts", [P, PARTS, S], BF16)
        qres = sb("qres", [P, S])
        kres = sb("kres", [P, S])
        hT = sb("hT", [P, S])
        xn = sb("xn", [P, TB, E])
        oT = sb("oT", [P, S])
        on = sb("on", [P, TB, E])
        onn = sb("onn", [P, TB, E])
        lnT = sb("lnT", [P, S])
        proj = sb("proj", [P, TB, E])
        rec = sb("rec", [P, TB, J])
        negm = sb("negm", [P, 2, J, TB])
        mparts = sb("mparts", [P, MPARTS, J, TB], BF16)
        mrow = sb("mrow", [MPARTS * J * TB, P], BF16)
        st = sb("st", [P, TB, 6])
        mv = sb("mv", [P, B, TB, 2])
        vare = sb("vare", [P, B, TB])
        rstd = sb("rstd", [P, B, TB])
        stO = sb("stO", [P, TB, 6])
        mvO = sb("mvO", [P, TB, 2])
        vareO = sb("vareO", [P, TB])
        rstdO = sb("rstdO", [P, TB])
        shift2, shiftO = (sb(n, [P, TB]) for n in ("shift2", "shiftO"))
        neghalf = sb("neghalf", [P, B, TB])
        identf = sb("identf", [P, P])
        identb = sb("identb", [P, P], BF16)
        zero_b = sb("zero_b", [P, P], BF16)
        maskts = sb("maskts", [P, P], BF16)
        cs = sb("cs", [P, B])
        cse = sb("cse", [P, B])
        csil = sb("csil", [P, B])
        modT = sb("modT", [P, 2, B])
        mod8 = sb("mod8", [B, 4, E])
        modbc = sb("modbc", [P, B, 4, E])
        wq = sb("wq", [P, E])
        wk = sb("wk", [P, E])
        wv = sb("wv", [P, E])
        wo = sb("wo", [P, E])
        gam = sb("gam", [P, 1])
        bet = sb("bet", [P, 1])

        gate_w = sb("gate_w", [P, NX, FF])
        up_w = sb("up_w", [P, NX, FF])
        down_w = sb("down_w", [P, NX, FC, E])
        conf_w = sb("conf_w", [P, NX])
        confb = sb("confb", [1, NX])
        wealth_bc = sb("wealth_bc", [P, NX])
        onesrow = sb("onesrow", [1, P])
        ones = sb("ones", [P, P])
        before_t = sb("before_t", [P, P])
        padtok = sb("padtok", [P, 2 * NX], I32)
        best1, best2, rank1, rank2, dbid, edbid, wsum, wfirst = (
            sb(n, [P, TB]) for n in ("best1", "best2", "rank1", "rank2", "dbid", "edbid", "wsum", "wfirst"))
        slotf = sb("slotf", [P, 2, TB])
        pri = sb("pri", [P, NX])
        rows = sb("rows", [P, TB, ROW])
        xn2 = sb("xn2", [P, TB, E])
        h2 = sb("h2", [P, TB, E])
        h2T = sb("h2T", [P, S])
        st2 = sb("st2", [P, TB, 6])
        mv2 = sb("mv2", [P, TB, 2])
        vare2 = sb("vare2", [P, TB])
        rstd2 = sb("rstd2", [P, TB])
        en = sb("en", [P, TB, NX])
        bids, masked_b, t2, t3, first, second, both = (
            sb(n, [P, TB, NX]) for n in ("bids", "masked_b", "t2", "t3", "first", "second", "both"))
        taken = sb("taken", [P, TB + 1, NX])
        tok = sb("tok", [P, NT])
        part0 = sb("part0", [P, 1])
        pri_i = sb("pri_i", [P, NX], I32)
        tok_i = sb("tok_i", [P, NT], I32)
        base_i = sb("base_i", [P, NX], I32)
        base = sb("base", [P, NX])
        slots = sb("slots", [P, 2, TB], I32)
        slots_last = sb("slots_last", [P, 2, TB], I32)
        thr_i = sb("thr_i", [P, NT], I32)
        thr = sb("thr", [P, NT])
        jv_i = sb("jv_i", [P, FTILES], I32)
        jv = sb("jv", [P, FTILES])
        part_i = sb("part_i", [P, 1], I32)
        part = sb("part", [P, 1])
        ntile = sb("ntile", [P, NX])
        cums = [sb(f"cums{i}", [P, 4 + NX]) for i in range(2)]
        counts = sb("counts", [P, NX])
        padslots = sb("padslots", [P, NX], I32)
        tile_e = sb("tile_e", [P, FTILES])
        tile_row_i = sb("tile_row_i", [P, FTILES], I32)
        tile_w_i = sb("tile_w_i", [P, FTILES], I32)
        dsc = [sb(f"dsc{i}", [P, 4]) for i in range(U)]
        dest = [sb(f"dest{i}", [P, 1], I32) for i in range(U)]

        ew_in, fc_in = sem("ew_in"), sem("fc_in")
        f_zero, f_const, f_chain = sem("f_zero"), sem("f_const"), sem("f_chain")
        sr_chain, rsr_chain, rsr_ready, xr_ready = sem("sr_chain"), sem("rsr_chain"), sem("rsr_ready"), sem("xr_ready")
        h2_chain, h2_ready, h2T_full, h2T_ready = sem("h2_chain"), sem("h2_ready"), sem("h2T_full"), sem("h2T_ready")
        z_full, z_ready = sem("z_full"), sem("z_ready")
        rows_ready = sem("rows_ready")
        taken_chain = sem("taken_chain")
        r_chain, ed_ready, slot_full, count_full = (
            sem("r_chain"), sem("ed_ready"), sem("slot_full"), sem("count_full"))
        dispatch_ready, tiles_ready, dispatched, pads_out = (
            sem("dispatch_ready"), sem("tiles_ready"), sem("dispatched"), sem("pads_out"))
        xg_in = [sem(f"xg_in{i}") for i in range(U)]
        xgT_full, xgT_ready, gu_full, sg_ready, hh_ready = (
            sem("xgT_full"), sem("xgT_ready"), sem("gu_full"), sem("sg_ready"), sem("hh_ready"))
        hhT_full, hhT_ready, y_full, dsc_chain, y_ready = (
            sem("hhT_full"), sem("hhT_ready"), sem("y_full"), sem("dsc_chain"), sem("y_ready"))
        y_out = [sem(f"y_out{i}") for i in range(U)]
        yp_in = [sem(f"yp_in{i}") for i in range(B)]
        c2_chain, c2_ready, fin_ready = sem("c2_chain"), sem("c2_ready"), sem("fin_ready")
        fin_out = sem("fin_out")

        c_in, wm_in, w_in = sem("c_in"), sem("wm_in"), sem("w_in")
        x_in = [sem(f"x_in{b}") for b in range(B)]
        zeroed, ident_ready, consts_ready, vaug_set = sem("zeroed"), sem("ident_ready"), sem("consts_ready"), sem("vaug_set")
        c_exp, c_silu, c_chain = sem("c_exp"), sem("c_silu"), sem("c_chain")
        modT_full, modT_ready, mod8_full, mod8_chain, mod8_ready = (
            sem("modT_full"), sem("modT_ready"), sem("mod8_full"), sem("mod8_chain"), sem("mod8_ready"))
        bc_full, bc_ready = sem("bc_full"), sem("bc_ready")
        st_chain, rs_chain, rs_ready, xn_ready = sem("st_chain"), sem("rs_chain"), sem("rs_ready"), sem("xn_ready")
        xT_full, hT_ready = sem("xT_full"), sem("hT_ready")
        q_full, q_hi, q_r1, q_mid, q_parts = sem("q_full"), sem("q_hi"), sem("q_r1"), sem("q_mid"), sem("q_parts")
        k_full, k_hi, k_r1, k_mid, k_parts = sem("k_full"), sem("k_hi"), sem("k_r1"), sem("k_mid"), sem("k_parts")
        v_full, v_tmp, v_ready = sem("v_full"), sem("v_tmp"), sem("v_ready")
        qk_out = sem("qk_out")
        st_in = [sem(f"stack_in{g}") for g in range(G)]
        nat_full, nat_done = sem("nat_full"), sem("nat_done")
        m_chain, m_parts, mT_full, m_row = sem("m_chain"), sem("m_parts"), sem("mT_full"), sem("m_row")
        m_in = [sem(f"m_in{g}") for g in range(G)]
        t_full, exp_done, masked = sem("t_full"), sem("exp_done"), sem("masked")
        pv_done, oT_ready, og_full, og_rec, og_done = (
            sem("pv_done"), sem("oT_ready"), sem("og_full"), sem("og_rec"), sem("og_done"))
        so_chain, rso_chain, rso_ready, onn_ready = sem("so_chain"), sem("rso_chain"), sem("rso_ready"), sem("onn_ready")
        lnT_full, lnT_ready, wo_full, proj_ready, x1_ready = (
            sem("lnT_full"), sem("lnT_ready"), sem("wo_full"), sem("proj_ready"), sem("x1_ready"))
        out_done = sem("out_done")

        banks = [psN[:, i] for i in range(NBANKS)] + [psT[:, i] for i in range(TBANKS)]
        psG, psU, psH, psX = banks[0:2], banks[2:4], banks[4], banks[5][:, 0:P]
        psY = psO[:, 0:E]
        abs8, clamp8, sign8 = (probs[0:B, 1, i * 4 * E:(i + 1) * 4 * E].rearrange("p (i e) -> p i e", i=4)
                               for i in range(3))
        wm = probs[:, 0, 0:6 * E]
        rowsel = down_w[0:B, NX - 2:NX].rearrange("p e c f -> p (e c f)").rearrange("p (b t) -> p b t", b=B)
        space_v = [vaug[:].rearrange("p n h c -> p (n h c)"), 0]
        space_p = [probs[:, 1, :], 0]
        space_k = [kst_all[:].rearrange("p g j s -> p (g j s)").bitcast(F32), 0]
        space_q = [qst_all[:].rearrange("p g j s -> p (g j s)").bitcast(F32), 0]

        def carve(space, *shape):
            n = 1
            for d in shape:
                n *= d
            v = space[0][:, space[1]:space[1] + n]
            space[1] += n
            if len(shape) == 1:
                return v
            names = "abc"[:len(shape)]
            return v.rearrange("p (" + " ".join(names) + ") -> p " + " ".join(names),
                               **dict(zip(names, shape)))

        sg, hh, hhT = ([carve(space_p, FF) for _ in range(2)] for _ in range(3))
        xgT = [carve(space_p, P) for _ in range(2)]
        passed_by, passed_n = (carve(space_p, FTILES, NX) for _ in range(2))
        over_thr = carve(space_v, NX, NT)
        tile_used, tile_row = (carve(space_v, FTILES) for _ in range(2))
        xg = [carve(space_k, ROW) for _ in range(U)]
        ysb = [carve(space_k, E) for _ in range(U)]
        padrows = carve(space_q, 2 * NX, ROW)
        rows_last = carve(space_k, TB, ROW)

        def h_bank(b):
            return psN[:, 0] if isinstance(b, int) and b == B - 2 else psM

        def rows_of(b):
            return rows_last if isinstance(b, int) and b == B - 1 else rows
        yp = [probs[:, b // 4, b % 4 * 2 * TB * E:(b % 4 + 1) * 2 * TB * E].rearrange("p (k n e) -> p k n e", k=2, n=TB)
              for b in range(B)]

        def slots_of(b):
            return slots_last if isinstance(b, int) and b == B - 1 else slots

        passed = {e: sem(f"passed_{e}") for e in ("sp", "pe", "dve", "pool")}

        def hold(name, eng, s, value):
            eng.wait_ge(s, value)
            if not isinstance(value, int):
                eng.sem_inc(passed[name], 1)

        def step_at(b, g, n):
            return b + (g + n) // G, (g + n) % G

        def has_earlier(b):
            return not (isinstance(b, int) and b == 0)

        def there(b, g, n):
            return not isinstance(b, int) or 0 <= G * b + g + n < STEPS

        def has_batch(b):
            return not isinstance(b, int) or 0 <= b < B

        EARLY = 4
        LATER = {0: 4, 1: 5, 2: 6, 4: 7}

        def all_steps(eng, step):
            for s in range(2 * G - 1):
                step(s // G, s % G)
            with eng.Fori(2, B - 1) as b:
                step(b - 1, G - 1)
                for g in range(G - 1):
                    step(b, g)
            step(B - 2, G - 1)
            for g in range(G):
                step(B - 1, g)

        block = ctx.enter_context(nc.Block())

        @block.sync
        def _(sp):
            def x_load(b):
                sp.dma_start(xall[:, b], x[b].rearrange("(n p) e -> p n e", p=P)).then_inc(x_in[b], 16)

            sp.dma_start(cs[:], cT).then_inc(c_in, 16)
            x_load(0)
            sp.dma_start(wm, wmod).then_inc(wm_in, 16)
            for dst, src in ((wq, wqT), (wk, wkT), (wv, wvT), (wo, woT)):
                sp.dma_start(dst[:], src).then_inc(w_in, 16)
            sp.dma_start(gam[:], gamma).then_inc(w_in, 16)
            sp.dma_start(bet[:], beta).then_inc(w_in, 16)
            x_load(1)
            sp.dma_start(conf_w[:], confT).then_inc(fc_in, 16)
            sp.dma_start(confb[:], conf_b).then_inc(fc_in, 16)
            sp.dma_start(wealth_bc[:], wealth.broadcast_to([P, NX])).then_inc(fc_in, 16)
            for b in range(2, B):
                x_load(b)

            def parts_out(b, parts, ready, dst):
                hold("sp", sp, ready, b + 1)
                for i in range(PARTS):
                    sp.dma_start(dst(bass.ds(b * E, E), i), parts[:]).then_inc(qk_out, 16)

            def q_out(b):
                parts_out(b, qparts, q_parts, lambda rows, i: qd[rows, :, i, :])

            def k_out(b):
                parts_out(b, kparts, k_parts, lambda rows, i: kd[rows, i, :, :])

            def stacks_in(b, g):
                for dst, src in ((qst[g], qd), (kst[g], kd)):
                    sp.dma_start(dst[0:KROWS], src[bass.ds(b * E + g * J * D, J * D)]
                                 .rearrange("(j d) a b t -> (d a b) j t", j=J)).then_inc(st_in[g], 16)

            def max_rows(b, g):
                hold("sp", sp, m_row, 4 * b + g + 1)
                for a in range(MPARTS):
                    sp.dma_start(qst[g][MROW + a:MROW + a + 1].rearrange("p j (n t) -> p (j n) t", t=P),
                                 mrow[a * J * TB:(a + 1) * J * TB, :]).then_inc(m_in[g], 16)

            def step(b, g):
                if there(b, g, -1) and there(b, g, 3):
                    if g == 1:
                        hold("sp", sp, qk_out, 96 * (b + 2))
                    hold("sp", sp, t_full, UNITS * (4 * b + g))
                    stacks_in(*step_at(b, g, 3))
                if there(b, g, 1):
                    max_rows(*step_at(b, g, 1))
                if g == 0 and has_batch(b + 1):
                    q_out(b + 1)
                    k_out(b + 1)
                if isinstance(b, int) and 1 <= G * b + g <= 6:
                    for i in (2 * (G * b + g - 1), 2 * (G * b + g - 1) + 1):
                        dst, src = ((gate_w, gateT), (up_w, upT), (down_w, downT))[i // 4]
                        e = slice(i % 4 * (NX // 4), (i % 4 + 1) * (NX // 4))
                        sp.dma_start(dst[:, e], src[:, e]).then_inc(ew_in, 16)

            q_out(0)
            k_out(0)
            hold("sp", sp, qk_out, 96)
            for g in range(G):
                sp.wait_ge(consts_ready, g + 1)
                stacks_in(0, g)
            max_rows(0, 0)
            all_steps(sp, step)

            def tile_in(i, u):
                j = U * i + u
                if not (isinstance(i, int) and i == 0):
                    hold("sp", sp, xgT_full, j - U + 1)
                    hold("sp", sp, dsc_chain, 5 * (j - U + 1))
                row = sp.value_load(tile_row_i[0:1, bass.ds(j, 1)], min_val=0, max_val=XROWS - P)
                sp.dma_start(xg[u], xd[bass.ds(row, P), :]).then_inc(xg_in[u], 16)

            sp.wait_ge(dispatch_ready, 1)
            sp.dma_start(xd[NX * REGION:XROWS, :].rearrange("(n p) c -> p n c", p=P), padrows[:, NX:, :]
                         ).then_inc(pads_out, 16)
            sp.wait_ge(dispatch_ready, 2)
            for e in range(NX):
                row = sp.value_load(padslots[0:1, e:e + 1], min_val=0, max_val=XROWS - P)
                sp.dma_start(xd[bass.ds(row, P), :], padrows[:, e, :]).then_inc(pads_out, 16)
            sp.wait_ge(pads_out, 16 * (1 + NX))
            sp.wait_ge(tiles_ready, 1)
            sp.wait_ge(dispatched, 16 * 2 * NT)
            for u in range(U):
                tile_in(0, u)
            with sp.Fori(1, TURNS - 1) as i:
                for u in range(U):
                    tile_in(i, u)
            for u in range(LAST):
                tile_in(TURNS - 1, u)

            for u in range(U):
                sp.wait_ge(y_out[u], 16 * (TURNS if u < LAST else TURNS - 1))
            for b in range(B):
                for k in range(2):
                    sp.dma_start(yp[b][:, k], yd[b * S + k * PLANE:(b + 1) * S + k * PLANE, :]
                                 .rearrange("(n p) e -> p n e", p=P)).then_inc(yp_in[b], 16)
            for b in range(B):
                sp.wait_ge(fin_ready, b + 1)
                sp.dma_start(out[b].rearrange("(n p) e -> p n e", p=P), xall[:, b]).then_inc(fin_out, 16)
            sp.wait_ge(fin_out, 16 * B)

        @block.tensor
        def _(pe):
            bank = [None]

            def take(free=None):
                if bank[0] is not None:
                    pe.wait_ge(*bank[0])
                bank[0] = free

            def nat(b, g, k):
                if k == 0:
                    pe.wait_ge(st_in[g], 32 * (b + 1))
                ago = freed_by(k, NAT, NBANKS)
                if not (isinstance(b, int) and NAT * (4 * b + g) + k < ago):
                    pe.wait_ge(nat_done, NAT * (4 * b + g) + k + 1 - ago)
                for col, j, tb, w in nat_blocks(k):
                    pe.matmul(psN[:, k % NBANKS, col:col + w], qst[g][0:KROWS, j, tb * P:(tb + 1) * P],
                              kst[g][0:KROWS, j, 0:w], start=True, stop=False)
                    mm = pe.matmul(psN[:, k % NBANKS, col + w - P:col + w], identb[:], maskts[:],
                                   start=False, stop=True)
                mm.then_inc(nat_full, 1)

            def scores(b, g, u):
                if u == 0:
                    pe.wait_ge(m_in[g], 16 * MPARTS * (b + 1))
                ago = freed_by(u, UNITS, TBANKS)
                if not (isinstance(b, int) and UNITS * (4 * b + g) + u < ago):
                    pe.wait_ge(exp_done, UNITS * (4 * b + g) + u + 1 - ago)
                for col, j, blk in exp_blocks(u):
                    mm = pe.matmul(psT[:, u % TBANKS, col:col + S - P * blk], kst[g][0:KALL, j, blk * P:(blk + 1) * P],
                                   qst[g][0:KALL, j, blk * P:S], start=True, stop=True)
                mm.then_inc(t_full, 1)

            def values(b, g, c):
                if c == 0:
                    if g == 0:
                        pe.wait_ge(v_ready, b + 1)
                    if not (isinstance(b, int) and b == 0 and g == 0):
                        pe.wait_ge(oT_ready, 4 * b + g)
                pe.wait_ge(masked, 16 * b + 4 * g + c + 1)
                blk = CHUNKS[c]
                base, stride, _ = probs_block(blk)
                w = S - P * blk
                for j in range(J):
                    o = base + stride * j
                    mm = pe.matmul(psO[32 * j:32 * j + 32, blk * P:S], vaug[:, blk, g * J + j, :],
                                   probs[:, g % 2, o:o + w], start=(c == 0), stop=(c == TB - 1))
                mm.then_inc(pv_done, 1)

            def turn_values(b, g):
                take((og_done, 4 * b + g + 1))
                pe.wait_ge(oT_ready, 4 * b + g + 1)
                for n in range(TB):
                    mm = pe.transpose(psM[:, n * P:(n + 1) * P], oT[:, n * P:(n + 1) * P], identf[:])
                mm.then_inc(og_full, 1)

            def turn_max(b, g):
                take((m_row, 4 * b + g + 1))
                hold("pe", pe, m_parts, 4 * b + g + 1)
                pe.transpose(psM[:].bitcast(BF16)[0:MPARTS * J * TB, 0:P], mparts[:].rearrange("p a j n -> p (a j n)"),
                             identb[:]).then_inc(mT_full, 1)

            def turn_x(b):
                take((hT_ready, b + 1))
                pe.wait_ge(xn_ready, b + 1)
                for n in range(TB):
                    mm = pe.transpose(psM[:, n * P:(n + 1) * P], xn[:, n, :], identf[:])
                mm.then_inc(xT_full, 1)

            def project_q(b):
                take((q_r1, b + 1))
                pe.matmul(psM[:], wq[:], hT[:], start=True, stop=True).then_inc(q_full, 1)

            def project_k(b):
                take((k_r1, b + 1))
                pe.matmul(psM[:], wk[:], hT[:], start=True, stop=True).then_inc(k_full, 1)

            def project_v(b):
                take((v_tmp, b + 1))
                for n in range(TB):
                    mm = pe.matmul(psM[:, n * P:(n + 1) * P], hT[:, n * P:(n + 1) * P], wv[:], start=True, stop=True)
                mm.then_inc(v_full, 1)

            def turn_attn(b):
                take((lnT_ready, b + 1))
                pe.wait_ge(onn_ready, b + 1)
                for n in range(TB):
                    mm = pe.transpose(psM[:, n * P:(n + 1) * P], onn[:, n, :], identf[:])
                mm.then_inc(lnT_full, 1)

            def project_o(b):
                take((proj_ready, b + 1))
                for n in range(TB):
                    mm = pe.matmul(psM[:, n * P:(n + 1) * P], lnT[:, n * P:(n + 1) * P], wo[:], start=True, stop=True)
                mm.then_inc(wo_full, 1)

            def spread(b, bank):
                pe.matmul(bank, rowsel[:, b, :], mod8[:].rearrange("p i e -> p (i e)"),
                          start=True, stop=True).then_inc(bc_full, 1)

            def turn_h(b):
                if h_bank(b) is psM:
                    take((h2T_ready, b + 1))
                pe.wait_ge(h2_ready, b + 1)
                for n in range(TB):
                    mm = pe.transpose(h_bank(b)[:, n * P:(n + 1) * P], h2[:, n, :], identf[:])
                mm.then_inc(h2T_full, 1)

            def experts(b):
                if h_bank(b) is psM:
                    take((z_ready, b + 1))
                else:
                    pe.wait_ge(h2T_ready, b + 1)
                pe.matmul(h_bank(b)[:, 0:TB * NX], onesrow[:], confb[:].unsqueeze(1).broadcast_to([1, TB, NX]),
                          start=True, stop=False)
                for n in range(TB):
                    mm = pe.matmul(h_bank(b)[:, n * NX:(n + 1) * NX], h2T[:, n * P:(n + 1) * P], conf_w[:],
                                   start=False, stop=(n == TB - 1))
                mm.then_inc(z_full, 1)

            def rank(b):
                if h_bank(b) is psM:
                    take((r_chain, LINKS * b + 21))
                else:
                    pe.wait_ge(z_ready, b + 1)
                pe.wait_ge(taken_chain, 5 * b + 6)
                pe.matmul(h_bank(b)[:, 0:TB * NX], before_t[:], both[:].rearrange("p n e -> p (n e)"), start=True, stop=False)
                pe.matmul(h_bank(b)[:, 0:TB * NX], ones[:], taken[:, 0:TB].rearrange("p n e -> p (n e)"),
                          start=False, stop=True).then_inc(slot_full, 1)

            def step(b, g):
                for k in range(NAT):
                    if there(b, g, 2):
                        nat(*step_at(b, g, 2), k)
                    if k < UNITS:
                        scores(b, g, k)
                    if k == 1 and g == 2 and has_batch(b - 2):
                        rank(b - 2)
                    if k == 2 and g == 2 and has_batch(b - 1):
                        turn_attn(b - 1)
                    if k == (3 if g == 2 else 2) and there(b, g, -2):
                        turn_values(*step_at(b, g, -2))
                    if k == (5 if g == 2 else 4) and there(b, g, 1):
                        turn_max(*step_at(b, g, 1))
                    if k in (1, 3, 5) and there(b, g, -1):
                        values(*step_at(b, g, -1), (k + 1) // 2)
                    if k == 9:
                        values(b, g, 0)
                    if isinstance(b, int) and k == 9 and 4 * b + g in LATER:
                        take((bc_ready, LATER[4 * b + g] + 1))
                        spread(LATER[4 * b + g], psM[:])
                    if g == 3 and has_batch(b + 2):
                        if k == 8:
                            turn_x(b + 2)
                        if k == 10:
                            project_q(b + 2)
                    if g == 0 and has_batch(b - 2):
                        if k == 8:
                            turn_h(b - 2)
                        if k == 10:
                            experts(b - 2)
                    if has_batch(b + 1):
                        if g == 0 and k == 6:
                            project_k(b + 1)
                        if g == 1 and k == 6:
                            project_v(b + 1)
                    if has_batch(b - 1):
                        if g == 2 and k == 7:
                            project_o(b - 1)

            pe.wait_ge(wm_in, 16)
            pe.wait_ge(c_silu, 1)
            take((modT_ready, 1))
            for i in range(2):
                mm = pe.matmul(psM[:, i * B:(i + 1) * B], wm[:, i * E:(i + 1) * E], csil[:], start=True, stop=True)
            mm.then_inc(modT_full, 1)
            take((mod8_chain, 1))
            pe.matmul(psM[0:B, :], csil[:], wm[:, 2 * E:6 * E], start=True, stop=True).then_inc(mod8_full, 1)
            pe.wait_ge(ident_ready, 3)
            pe.wait_ge(w_in, 96)
            turn_x(0)
            pe.wait_ge(hT_ready, 1)
            project_q(0)
            project_k(0)
            project_v(0)
            pe.wait_ge(mod8_ready, 2)
            for b in range(EARLY):
                if b >= TBANKS:
                    pe.wait_ge(bc_ready, b - TBANKS + 1)
                spread(b, psT[:, b % TBANKS])
            for k in range(NAT):
                nat(0, 0, k)
            turn_max(0, 0)
            for k in range(NAT):
                nat(0, 1, k)
            pe.wait_ge(bc_ready, EARLY)
            turn_x(1)
            project_q(1)
            pe.wait_ge(fc_in, 48)
            pe.wait_ge(f_const, 2)
            for s in range(2 * G - 1):
                step(s // G, s % G)
            with pe.Fori(2, B - 1) as b:
                bank[0] = (m_row, 4 * b)
                step(b - 1, G - 1)
                for g in range(G - 1):
                    step(b, g)
            bank[0] = (m_row, 4 * (B - 1))
            step(B - 2, G - 1)
            for g in range(G):
                step(B - 1, g)
            L = B - 1
            turn_values(L, 2)
            for c in range(1, TB):
                values(L, 3, c)
            turn_values(L, 3)
            turn_attn(L)
            turn_h(L - 1)
            project_o(L)
            experts(L - 1)
            turn_h(L)
            rank(L - 1)
            experts(L)
            rank(L)
            take()
            pe.matmul(psM[:, 0:NX], ones[:], taken[:, TB], start=True, stop=True).then_inc(count_full, 1)

            def turn_in(i, u):
                j, par = U * i + u, u % 2
                pe.wait_ge(xg_in[u], 16 * (i + 1))
                if not (isinstance(i, int) and j == 0):
                    pe.wait_ge(xgT_ready, j)
                pe.transpose(psX, xg[u][:, 0:E], identf[:]).then_inc(xgT_full, 1)

            def gate_up(i, u):
                j, par = U * i + u, u % 2
                e = pe.value_load(tile_w_i[0:1, bass.ds(j, 1)], min_val=0, max_val=NX - 1)
                pe.wait_ge(xgT_ready, j + 1)
                if not (isinstance(i, int) and j < 2):
                    pe.wait_ge(hh_ready, j - 1)
                pe.matmul(psG[par], xgT[par], gate_w[:, bass.ds(e, 1), :], start=True, stop=True)
                pe.matmul(psU[par], xgT[par], up_w[:, bass.ds(e, 1), :], start=True, stop=True).then_inc(gu_full, 1)

            def turn_hidden(i, u):
                j, par = U * i + u, u % 2
                pe.wait_ge(hh_ready, j + 1)
                if not (isinstance(i, int) and j == 0):
                    pe.wait_ge(hhT_ready, j)
                for c in range(FC):
                    mm = pe.transpose(psH[:, c * P:(c + 1) * P], hh[par][:, c * P:(c + 1) * P], identf[:])
                mm.then_inc(hhT_full, 1)

            def down(i, u):
                j, par = U * i + u, u % 2
                e = pe.value_load(tile_w_i[0:1, bass.ds(j, 1)], min_val=0, max_val=NX - 1)
                pe.wait_ge(hhT_ready, j + 1)
                if not (isinstance(i, int) and j == 0):
                    pe.wait_ge(y_ready, j)
                for c in range(FC):
                    mm = pe.matmul(psY, hhT[par][:, c * P:(c + 1) * P], down_w[:, bass.ds(e, 1), c, :],
                                   start=(c == 0), stop=(c == FC - 1))
                mm.then_inc(y_full, 1)

            def at(i, u):
                return i + u // U, u % U

            def turn(i, first=False, last=False):
                for u in range(LAST if last else U):
                    if not (last and u == LAST - 1):
                        turn_in(*at(i, u + 1))
                    gate_up(i, u)
                    if not (first and u < 1):
                        turn_hidden(*at(i, u - 1))
                    if not (first and u < 2):
                        down(*at(i, u - 2))

            pe.wait_ge(ew_in, 16 * 12)
            pe.wait_ge(tiles_ready, 1)
            turn_in(0, 0)
            turn(0, first=True)
            with pe.Fori(1, TURNS - 1) as i:
                turn(i)
            turn(TURNS - 1, last=True)
            turn_hidden(TURNS - 1, LAST - 1)
            down(TURNS - 1, LAST - 2)
            down(TURNS - 1, LAST - 1)

        @block.scalar
        def _(act):
            act.wait_ge(c_in, 16)
            nc.scalar.activation(cse[:], cs[:], ACT.Exp, scale=-1.0).then_inc(c_exp, 1)

            def h_norm(b, tiles=range(TB)):
                if 0 in tiles:
                    act.wait_ge(rsr_ready, b + 1)
                    if has_earlier(b):
                        act.wait_ge(h2_ready, b)
                for n in tiles:
                    last = nc.scalar.activation(xn2[:, n, :], xall[:, b, n, :], ACT.Identity, scale=rstd2[:, n:n + 1],
                                                bias=shift2[:, n:n + 1])
                if TB - 1 in tiles:
                    last.then_inc(xr_ready, 1)

            def o_norm(b, tiles=range(TB)):
                if 0 in tiles:
                    act.wait_ge(rso_ready, b + 1)
                    if has_earlier(b):
                        act.wait_ge(lnT_full, b)
                for n in tiles:
                    last = nc.scalar.activation(onn[:, n, :], on[:, n, :], ACT.Identity, scale=rstdO[:, n:n + 1],
                                                bias=shiftO[:, n:n + 1])
                if TB - 1 in tiles:
                    last.then_inc(onn_ready, 1)

            def shift_in(b):
                act.wait_ge(xT_full, b + 1)
                nc.scalar.activation(hT[:], psM[:], ACT.Identity, scale=modT[:, 1, bass.ds(b, 1)],
                                     bias=modT[:, 0, bass.ds(b, 1)]).then_inc(hT_ready, 1)

            def high(b, full, parts, done):
                act.wait_ge(full, b + 1)
                if not (isinstance(b, int) and b == 0):
                    act.wait_ge(qk_out, 96 * b)
                nc.scalar.activation(parts[:, 0, :], psM[:], ACT.Copy).then_inc(done, 1)

            def keep_v(b):
                act.wait_ge(v_full, b + 1)
                if not (isinstance(b, int) and b == 0):
                    act.wait_ge(v_ready, b)
                nc.scalar.activation(vtmp[:].rearrange("p n h d -> p (n h d)"), psM[:], ACT.Copy).then_inc(v_tmp, 1)

            def keep_max(b, g):
                act.wait_ge(mT_full, 4 * b + g + 1)
                s = 4 * b + g
                if not (isinstance(b, int) and s == 0):
                    pb, pg = (b, g - 1) if g else (b - 1, G - 1)
                    act.wait_ge(m_in[pg], 16 * MPARTS * (pb + 1))
                nc.scalar.activation(mrow[:], psM[:].bitcast(BF16)[0:MPARTS * J * TB, 0:P], ACT.Copy).then_inc(m_row, 1)

            def exps(b, g, u):
                act.wait_ge(t_full, UNITS * (4 * b + g) + u + 1)
                if u == 0 and not (isinstance(b, int) and 4 * b + g < 2):
                    act.wait_ge(pv_done, 16 * b + 4 * g - 4)
                nc.scalar.activation(probs[:, g % 2, 512 * u:512 * (u + 1)], psT[:, u % TBANKS, :], ACT.Exp,
                                     scale=SOFTMAX_SCALE).then_inc(exp_done, 1)

            def keep_values(b, g):
                act.wait_ge(pv_done, 16 * b + 4 * g + 4)
                if not (isinstance(b, int) and 4 * b + g < 1):
                    act.wait_ge(og_full, 4 * b + g)
                nc.scalar.activation(oT[:], psO[:], ACT.Copy).then_inc(oT_ready, 1)

            def keep_attn(b):
                act.wait_ge(lnT_full, b + 1)
                nc.scalar.activation(lnT[:], psM[:], ACT.Identity, scale=gam[:, 0:1], bias=bet[:, 0:1]
                                     ).then_inc(lnT_ready, 1)

            def keep_spread(b, bank):
                act.wait_ge(bc_full, b + 1)
                nc.scalar.activation(modbc[:, b].rearrange("p i e -> p (i e)"), bank, ACT.Copy).then_inc(bc_ready, 1)

            def keep_h(b):
                act.wait_ge(h2T_full, b + 1)
                if has_earlier(b):
                    act.wait_ge(z_full, b)
                nc.scalar.activation(h2T[:], h_bank(b)[:], ACT.Copy).then_inc(h2T_ready, 1)

            def keep_rows(b):
                act.wait_ge(h2_ready, b + 1)
                if has_earlier(b) and not (isinstance(b, int) and b == B - 1):
                    act.wait_ge(dispatched, 16 * 2 * TB * b)
                nc.scalar.activation(rows_of(b)[:, :, 0:E], h2[:], ACT.Copy).then_inc(rows_ready, 1)

            def keep_z(b):
                act.wait_ge(z_full, b + 1)
                if has_earlier(b):
                    act.wait_ge(r_chain, LINKS * (b - 1) + 1 if isinstance(b, int) else LINKS * b)
                nc.scalar.activation(en[:].rearrange("p n e -> p (n e)"), h_bank(b)[:, 0:TB * NX], ACT.Exp, scale=-1.0
                                     ).then_inc(z_ready, 1)

            def exp_bids(b):
                act.wait_ge(r_chain, LINKS * b + 16)
                nc.scalar.activation(edbid[:], dbid[:], ACT.Exp).then_inc(ed_ready, 1)

            def step(b, g):
                for k in range(NAT):
                    if g == 0 and k == 0 and has_batch(b + 1) and not (isinstance(b, int) and b == 0):
                        high(b + 1, q_full, qparts, q_hi)
                    if g == 3 and k == 8 and has_batch(b + 2):
                        shift_in(b + 2)
                    if k < UNITS:
                        exps(b, g, k)
                    if isinstance(b, int) and k == 9 and 4 * b + g in LATER:
                        keep_spread(LATER[4 * b + g], psM[:])
                    if k == 6 and there(b, g, -1):
                        keep_values(*step_at(b, g, -1))
                    if k == (5 if g == 2 else 4) and there(b, g, 1):
                        keep_max(*step_at(b, g, 1))
                    if g == 1 and k >= 7 and has_batch(b - 1):
                        o_norm(b - 1, (k - 7,))
                    if g == 3 and k in (9, 10) and has_batch(b - 1):
                        h_norm(b - 1, (k - 9,))
                    if g == 0 and k in (1, 2) and has_batch(b - 2):
                        h_norm(b - 2, (k + 1,))
                    if g == 0 and has_batch(b - 2):
                        if k == 8:
                            keep_h(b - 2)
                        if k == 9:
                            keep_rows(b - 2)
                        if k == 10:
                            keep_z(b - 2)
                    if g == 1 and k == 10 and has_batch(b - 2):
                        exp_bids(b - 2)
                    if has_batch(b + 1):
                        if g == 0 and k == 6:
                            high(b + 1, k_full, kparts, k_hi)
                        if g == 1 and k == 6:
                            keep_v(b + 1)
                    if g == 2 and k == 2 and has_batch(b - 1):
                        keep_attn(b - 1)

            act.wait_ge(modT_ready, 1)
            shift_in(0)
            high(0, q_full, qparts, q_hi)
            high(0, k_full, kparts, k_hi)
            keep_v(0)
            for b in range(EARLY):
                keep_spread(b, psT[:, b % TBANKS])
            keep_max(0, 0)
            shift_in(1)
            high(1, q_full, qparts, q_hi)
            all_steps(act, step)
            h_norm(B - 2, (2, 3))
            keep_values(B - 1, 3)
            o_norm(B - 1)
            keep_attn(B - 1)
            keep_h(B - 2)
            keep_z(B - 2)
            keep_rows(B - 2)
            exp_bids(B - 2)
            keep_h(B - 1)
            keep_rows(B - 1)
            keep_z(B - 1)
            exp_bids(B - 1)

            def silu(i, u):
                j, par = U * i + u, u % 2
                act.wait_ge(gu_full, j + 1)
                if not (isinstance(i, int) and j < 2):
                    act.wait_ge(hh_ready, j - 1)
                nc.scalar.activation(sg[par], psG[par], ACT.Silu).then_inc(sg_ready, 1)

            def keep_hidden(i, u):
                j, par = U * i + u, u % 2
                act.wait_ge(hhT_full, j + 1)
                if not (isinstance(i, int) and j < 2):
                    act.wait_ge(y_full, j - 1)
                nc.scalar.activation(hhT[par], psH, ACT.Copy).then_inc(hhT_ready, 1)

            def turn(i, first=False, last=False):
                for u in range(LAST if last else U):
                    silu(i, u)
                    if not (first and u == 0):
                        keep_hidden(i + (u - 1) // U, (u - 1) % U)

            nc.scalar.preload_act_table(ACT.Silu)
            turn(0, first=True)
            with act.Fori(1, TURNS - 1) as i:
                turn(i)
            turn(TURNS - 1, last=True)
            keep_hidden(TURNS - 1, LAST - 1)

        @block.vector
        def _(dve):
            V = nc.vector
            def ones_rows(g):
                V.memset(kst[g][64:96], 1.0).then_inc(consts_ready, 1)

            dve.wait_ge(c_exp, 1)
            nc.vector.tensor_scalar_add(cse[:], cse[:], 1.0).then_inc(c_chain, 1)
            dve.wait_ge(c_chain, 1)
            nc.vector.reciprocal(cse[:], cse[:]).then_inc(c_chain, 1)
            dve.wait_ge(c_chain, 2)
            nc.vector.tensor_tensor(csil[:], cs[:], cse[:], ALU.mult).then_inc(c_silu, 1)

            def stats(src, s6, chain, tiles):
                for n in tiles:
                    V.bn_stats(s6[:, n, :], src[:, n, :]).then_inc(chain, 1)

            def mean_var(s6, m2, chain, b, used):
                if used is not None and has_earlier(b):
                    hold("dve", dve, used, b)
                hold("dve", dve, chain, 8 * b + 4)
                for n in range(TB):
                    V.bn_aggr(m2[:, n, :], s6[:, n, :]).then_inc(chain, 1)

            def norm(src, m2, rs, dst, done, tiles):
                for n in tiles:
                    last = V.tensor_scalar(dst[:, n, :], src[:, n, :], m2(n), rs(n), ALU.subtract, ALU.mult)
                if TB - 1 in tiles:
                    last.then_inc(done, 1)

            def x_stats(b):
                dve.wait_ge(x_in[b], 16)
                if b > 0:
                    dve.wait_ge(st_chain, 8 * b)
                stats(xall[:, b], st, st_chain, range(TB))
                mean_var(st, mv[:, b], st_chain, b, None)

            def x_norm(b, tiles=range(TB)):
                if 0 in tiles and isinstance(b, int) and b == 2:
                    dve.wait_ge(rs_ready, 3)
                if 0 in tiles and has_earlier(b):
                    hold("dve", dve, xT_full, b)
                norm(xall[:, b], lambda n: mv[:, bass.ds(b, 1), n, 0], lambda n: rstd[:, bass.ds(b, 1), n],
                     xn, xn_ready, tiles)

            def max_high(b, g):
                s = 4 * b + g
                hold("dve", dve, nat_done, NAT * (4 * b + g + 1))
                if not (isinstance(b, int) and s == 0):
                    hold("dve", dve, mT_full, s)
                nc.vector.tensor_copy(mparts[:, 0], negm[:, g % 2]).then_inc(m_chain, 1)

            def max_low(b, g):
                hold("dve", dve, m_chain, 4 * b + g + 1)
                nc.vector.tensor_tensor(mparts[:, 1], negm[:, g % 2], mparts[:, 0], ALU.subtract).then_inc(m_parts, 1)

            def middle(b, res, parts, r1, mid):
                hold("dve", dve, r1, b + 1)
                nc.vector.tensor_copy(parts[:, 1, :], res[:]).then_inc(mid, 1)

            def place_v(b):
                hold("dve", dve, v_tmp, b + 1)
                if not (isinstance(b, int) and b == 0):
                    hold("dve", dve, pv_done, 16 * b)
                nc.vector.tensor_copy(vaug[:, :, :, 0:D], vtmp[:]).then_inc(v_ready, 1)

            def residue(b, hi, parts, res, done, split):
                dve.wait_ge(hi, b + 1)
                if not (isinstance(b, int) and b == 0):
                    dve.wait_ge(split, b)
                nc.vector.tensor_tensor(res[:], psM[:], parts[:, 0, :], ALU.subtract).then_inc(done, 1)

            def maxima(b, g, k):
                dve.wait_ge(nat_full, NAT * (4 * b + g) + k + 1)
                if k == 0 and not (isinstance(b, int) and 4 * b + g < 2):
                    hold("dve", dve, m_parts, 4 * b + g - 1)
                blocks = nat_blocks(k)
                w = blocks[0][3]
                dst = negm[:, g % 2, blocks[0][1]:blocks[-1][1] + 1, blocks[0][2]]
                src = psN[:, k % NBANKS, 0:w * len(blocks)].rearrange("p (h s) -> p h s", s=w)
                nc.vector.tensor_reduce(dst, src, axis=AX.X, op=ALU.max, negate=True).then_inc(nat_done, 1)

            def normalise(b, g):
                dve.wait_ge(og_full, 4 * b + g + 1)
                v = psM[:].rearrange("p (n j c) -> p n j c", n=TB, j=J)
                nc.vector.reciprocal(rec[:], v[:, :, :, D]).then_inc(og_rec, 1)
                dve.wait_ge(og_rec, 4 * b + g + 1)
                if g == 0 and has_earlier(b):
                    hold("dve", dve, onn_ready, b)
                nc.vector.tensor_tensor(on[:, :, g * J * D:(g + 1) * J * D].rearrange("p n (j d) -> p n j d", j=J),
                                        v[:, :, :, 0:D], rec[:].unsqueeze(3).broadcast_to([P, TB, J, D]),
                                        ALU.mult).then_inc(og_done, 1)

            def gate_out(b):
                dve.wait_ge(wo_full, b + 1)
                if not (isinstance(b, int) and b == 0):
                    dve.wait_ge(x1_ready, b)
                nc.vector.tensor_tensor(proj[:], psM[:].rearrange("p (n e) -> p n e", n=TB),
                                        modbc[:, b, 0:1, :].broadcast_to([P, TB, E]), ALU.mult).then_inc(proj_ready, 1)

            def h_stats(b, tiles):
                hold("dve", dve, x1_ready, b + 1)
                stats(xall[:, b], st2, sr_chain, tiles)

            def over(ap, shape):
                return ap.unsqueeze(2).broadcast_to(shape)

            grid = [P, TB, NX]

            def route(b, i):
                def done(n):
                    hold("dve", dve, r_chain, LINKS * b + n)

                def last(ins):
                    ins.then_inc(r_chain, 1)

                slot = h_bank(b)[:, 0:TB * NX].rearrange("p (n e) -> p n e", n=TB)
                if i == 0:
                    hold("dve", dve, z_ready, b + 1)
                    last(V.tensor_scalar_add(t2[:], en[:], 1.0))
                if i == 1:
                    done(1)
                    last(V.reciprocal(t3[:], t2[:]))
                if i == 2:
                    done(2)
                    last(V.tensor_tensor(bids[:], t3[:], wealth_bc[:].unsqueeze(1).broadcast_to(grid), ALU.mult))
                for at, src, pick, best, rk in ((3, bids, first, best1, rank1), (9, masked_b, second, best2, rank2)):
                    if i == at:
                        done(at)
                        last(V.tensor_reduce(best[:], src[:], axis=AX.X, op=ALU.max))
                    if i == at + 1:
                        done(at + 1)
                        last(V.tensor_tensor(t2[:], src[:], over(best[:], grid), ALU.is_equal))
                    if i == at + 2:
                        done(at + 2)
                        last(V.tensor_tensor(t3[:], t2[:], pri[:].unsqueeze(1).broadcast_to(grid), ALU.mult))
                    if i == at + 3:
                        done(at + 3)
                        last(V.tensor_reduce(rk[:], t3[:], axis=AX.X, op=ALU.max))
                    if i == at + 4:
                        done(at + 4)
                        last(V.tensor_tensor(pick[:], t3[:], over(rk[:], grid), ALU.is_equal))
                if i == 8:
                    done(8)
                    last(V.scalar_tensor_tensor(out=masked_b[:], in0=first[:], scalar=BIG, in1=bids[:],
                                                op0=ALU.mult, op1=ALU.add))
                if i == 14:
                    done(14)
                    last(V.tensor_tensor(both[:], first[:], second[:], ALU.add))
                if i == 15:
                    done(15)
                    last(V.tensor_tensor(dbid[:], best2[:], best1[:], ALU.subtract))
                if i == 16:
                    hold("dve", dve, rows_ready, b + 1)
                    last(V.tensor_scalar(rows_of(b)[:, :, C_E0], rank1[:], -1.0, float(NX), ALU.mult, ALU.add))
                if i == 17:
                    last(V.tensor_copy(rows_of(b)[:, :, C_TOK], tok[:, bass.ds(TB * b, TB)]))
                if i == 18:
                    hold("dve", dve, ed_ready, b + 1)
                    last(V.tensor_scalar_add(wsum[:], edbid[:], 1.0))
                if i == 19:
                    hold("dve", dve, slot_full, b + 1)
                    last(V.tensor_tensor(t2[:], first[:], slot, ALU.mult))
                if i == 20:
                    last(V.tensor_tensor(t3[:], second[:], slot, ALU.mult))
                if i == 21:
                    done(19)
                    last(V.reciprocal(wfirst[:], wsum[:]))
                if i == 22:
                    done(20)
                    last(V.tensor_reduce(slotf[:, 0], t2[:], axis=AX.X, op=ALU.add))
                if i == 23:
                    done(21)
                    last(V.tensor_reduce(slotf[:, 1], t3[:], axis=AX.X, op=ALU.add))
                if i == 24:
                    done(22)
                    last(V.tensor_copy(rows_of(b)[:, :, C_W0], wfirst[:]))
                if i == 25:
                    last(V.tensor_tensor(rows_of(b)[:, :, C_W1], edbid[:], wfirst[:], ALU.mult))
                if i == 26:
                    done(24)
                    last(V.tensor_copy(slots_of(b)[:], slotf[:]))

            def step(b, g):
                for k in range(NAT):
                    if isinstance(b, int) and (b, k) == (0, 5) and g < 2:
                        x_stats(6 + g)
                    if has_batch(b - 2):
                        if g == 1 and k <= 8:
                            route(b - 2, 2 * k)
                        if g == 2 and k == 1:
                            route(b - 2, 18)
                        if g == 2 and k == 2:
                            route(b - 2, 21)
                        if g == 2 and k == 3:
                            route(b - 2, 24)
                            route(b - 2, 25)
                    if there(b, g, 2):
                        maxima(*step_at(b, g, 2), k)
                    if has_batch(b - 2):
                        if g == 1 and k <= 8:
                            route(b - 2, 2 * k + 1)
                        if g == 2 and k == 1:
                            route(b - 2, 19)
                            route(b - 2, 20)
                        if g == 2 and k == 2:
                            route(b - 2, 22)
                            route(b - 2, 23)
                        if g == 2 and k == 3:
                            route(b - 2, 26)
                    if k == 0 and there(b, g, 1):
                        max_high(*step_at(b, g, 1))
                    if k == 1 and there(b, g, 1):
                        max_low(*step_at(b, g, 1))
                    if k == (3 if g == 2 else 2) and there(b, g, -2):
                        normalise(*step_at(b, g, -2))
                    if g == 3 and has_batch(b - 1):
                        if k == 3:
                            h_stats(b - 1, (0, 1))
                        if k == 4:
                            h_stats(b - 1, (2, 3))
                        if k == 5:
                            mean_var(st2, mv2, sr_chain, b - 1, rsr_ready)
                    if g == 3 and has_batch(b + 2):
                        if k == 2:
                            x_norm(b + 2, (0, 1))
                        if k == 4:
                            x_norm(b + 2, (2, 3))
                    if g == 0 and has_batch(b + 1):
                        if k == 0 and has_earlier(b):
                            residue(b + 1, q_hi, qparts, qres, q_r1, q_parts)
                        if k == 2 and has_earlier(b):
                            middle(b + 1, qres, qparts, q_r1, q_mid)
                        if k == 7:
                            residue(b + 1, k_hi, kparts, kres, k_r1, k_parts)
                        if k == 8:
                            middle(b + 1, kres, kparts, k_r1, k_mid)
                    if g == 0 and k == 6 and has_earlier(b):
                        place_v(b)
                    if has_batch(b - 1):
                        if g == 1:
                            if k == 2:
                                hold("dve", dve, og_done, 4 * b)
                                stats(on, stO, so_chain, (0, 1))
                            if k == 3:
                                stats(on, stO, so_chain, (2, 3))
                            if k == 4:
                                mean_var(stO, mvO, so_chain, b - 1, onn_ready)
                        if g == 2 and k == 8:
                            gate_out(b - 1)

            links = [0]

            def link(ins):
                ins.then_inc(f_chain, 1)
                links[0] += 1
                dve.wait_ge(f_chain, links[0])

            x_stats(0)
            dve.wait_ge(modT_full, 1)
            nc.vector.tensor_scalar_add(modT[:, 1, :], psM[:, B:2 * B], 1.0).then_inc(c_chain, 1)
            nc.vector.tensor_copy(modT[:, 0, :], psM[:, 0:B]).then_inc(modT_ready, 1)
            dve.wait_ge(mod8_full, 1)
            nc.vector.tensor_copy(mod8[:].rearrange("p i e -> p (i e)"), psM[0:B, :]).then_inc(mod8_chain, 1)
            dve.wait_ge(rs_ready, 1)
            x_norm(0)
            ones_rows(0)
            ones_rows(1)
            residue(0, q_hi, qparts, qres, q_r1, q_parts)
            middle(0, qres, qparts, q_r1, q_mid)
            residue(0, k_hi, kparts, kres, k_r1, k_parts)
            middle(0, kres, kparts, k_r1, k_mid)
            dve.wait_ge(mod8_chain, 1)
            for i in (0, 3):
                nc.vector.scalar_tensor_tensor(out=abs8[:, i, :], in0=mod8[:, i, :], scalar=-1.0, in1=mod8[:, i, :],
                                               op0=ALU.mult, op1=ALU.max).then_inc(mod8_chain, 1)
                nc.vector.tensor_scalar(sign8[:, i, :], mod8[:, i, :], 0.0, 2.0, ALU.is_ge, ALU.mult).then_inc(mod8_chain, 1)
            dve.wait_ge(mod8_chain, 5)
            for i in (0, 3):
                nc.vector.tensor_scalar_max(clamp8[:, i, :], abs8[:, i, :], 0.25).then_inc(mod8_chain, 1)
            dve.wait_ge(mod8_chain, 7)
            for i in (0, 3):
                nc.vector.scalar_tensor_tensor(out=mod8[:, i, :], in0=sign8[:, i, :], scalar=-1.0, in1=clamp8[:, i, :],
                                               op0=ALU.add, op1=ALU.mult).then_inc(mod8_chain, 1)
            nc.vector.tensor_scalar_add(mod8[:, 2, :], mod8[:, 2, :], 1.0).then_inc(mod8_chain, 1)
            dve.wait_ge(mod8_chain, 10)
            nc.vector.nop().then_inc(mod8_ready, 1)
            ones_rows(2)
            ones_rows(3)
            dve.wait_ge(vaug_set, 2)
            place_v(0)
            dve.wait_ge(f_const, 3)
            for dst, src in ((pri, pri_i), (base, base_i), (thr, thr_i), (jv, jv_i), (part, part_i), (tok, tok_i)):
                link(V.tensor_copy(dst[:], src[:]))
            link(V.tensor_scalar(part0[:], part[:], 0.0, None, ALU.is_equal))
            link(V.tensor_scalar(taken[:, TB], base[:], part0[:, 0:1], None, ALU.mult))
            V.nop().then_inc(taken_chain, 1)
            dve.wait_ge(fc_in, 48)
            for b in range(1, 4):
                x_stats(b)
            for k in range(NAT):
                maxima(0, 0, k)
            max_high(0, 0)
            max_low(0, 0)
            dve.wait_ge(rs_ready, 2)
            x_norm(1)
            for k in range(NAT):
                maxima(0, 1, k)
            for b in range(4, 6):
                x_stats(b)
            residue(1, q_hi, qparts, qres, q_r1, q_parts)
            middle(1, qres, qparts, q_r1, q_mid)
            all_steps(dve, step)
            L = B - 1
            normalise(L, 2)
            normalise(L, 3)
            hold("dve", dve, og_done, 4 * B)
            stats(on, stO, so_chain, range(TB))
            mean_var(stO, mvO, so_chain, L, onn_ready)
            gate_out(L)
            dve.wait_ge(proj_ready, B)
            V.tensor_tensor(xall[:, L], xall[:, L], proj[:], ALU.add).then_inc(x1_ready, 1)
            h_stats(L, range(TB))
            mean_var(st2, mv2, sr_chain, L, rsr_ready)
            for i in range(8):
                route(L - 1, i)
            dve.wait_ge(rsr_chain, 3 * B)
            norm(xall[:, L], lambda n: mv2[:, n, 0:1], lambda n: rstd2[:, n:n + 1], xn2, xr_ready, range(TB))
            dve.wait_ge(xr_ready, B)
            V.tensor_tensor(xn2[:], xn2[:], modbc[:, L, 2:3, :].broadcast_to([P, TB, E]), ALU.mult).then_inc(h2_chain, 1)
            dve.wait_ge(h2_chain, B)
            dve.wait_ge(rows_ready, B - 1)
            V.tensor_tensor(h2[:], xn2[:], modbc[:, L, 1:2, :].broadcast_to([P, TB, E]), ALU.add).then_inc(h2_ready, 1)
            for i in range(8, LINKS):
                route(L - 1, i)
            link(V.memset(padrows[:, :, 0:C_E0], 0.0))
            link(V.memset(padrows[:, :, C_E0], -1.0))
            link(V.memset(padrows[:, :, C_W0:], 0.0))
            V.tensor_copy(padrows[:, :, C_TOK], padtok[:]).then_inc(dispatch_ready, 1)
            for i in range(LINKS):
                route(L, i)
            dve.wait_ge(count_full, 1)
            link(V.tensor_copy(padslots[:], psM[:, 0:NX]))
            V.nop().then_inc(dispatch_ready, 1)
            link(V.tensor_tensor(counts[:], psM[:, 0:NX], base[:], ALU.subtract))
            link(V.tensor_tensor(over_thr, over(counts[:], [P, NX, NT]), thr[:].unsqueeze(1).broadcast_to([P, NX, NT]),
                                 ALU.is_gt))
            link(V.tensor_reduce(ntile[:], over_thr, axis=AX.X, op=ALU.add))
            link(V.memset(cums[0][:, 0:4], 0.0))
            link(V.memset(cums[1][:, 0:4], 0.0))
            link(V.tensor_copy(cums[0][:, 4:], ntile[:]))
            a, c = cums
            for sh in (1, 2, 4):
                link(V.tensor_tensor(c[:, 4:], a[:, 4:], a[:, 4 - sh:4 + NX - sh], ALU.add))
                a, c = c, a
            wide = [P, FTILES, NX]
            link(V.tensor_tensor(passed_by, over(jv[:], wide), a[:, 4:].unsqueeze(1).broadcast_to(wide), ALU.is_ge))
            link(V.tensor_reduce(tile_e[:], passed_by, axis=AX.X, op=ALU.add))
            link(V.tensor_tensor(passed_n, passed_by, ntile[:].unsqueeze(1).broadcast_to(wide), ALU.mult))
            link(V.tensor_reduce(tile_used, passed_n, axis=AX.X, op=ALU.add))
            link(V.tensor_tensor(tile_used, jv[:], tile_used, ALU.subtract))
            link(V.tensor_scalar(tile_row, tile_e[:], float(REGION), None, ALU.mult))
            link(V.scalar_tensor_tensor(out=tile_row_i[:], in0=tile_used, scalar=float(P), in1=tile_row,
                                        op0=ALU.mult, op1=ALU.add))
            link(V.tensor_scalar(tile_w_i[:], tile_e[:], float(NX - 1), None, ALU.min))
            V.nop().then_inc(tiles_ready, 1)

            def keep_tile(i, u):
                j, par = U * i + u, u % 2
                dve.wait_ge(xgT_full, j + 1)
                if not (isinstance(i, int) and j < 2):
                    dve.wait_ge(gu_full, j - 1)
                V.tensor_copy(xgT[par], psX).then_inc(xgT_ready, 1)

            def multiply(i, u):
                j, par = U * i + u, u % 2
                dve.wait_ge(sg_ready, j + 1)
                if not (isinstance(i, int) and j < 2):
                    dve.wait_ge(hhT_full, j - 1)
                V.tensor_tensor(hh[par], sg[par], psU[par], ALU.mult).then_inc(hh_ready, 1)

            def weights(i, u):
                j = U * i + u
                dve.wait_ge(xg_in[u], 16 * (i + 1))
                if not (isinstance(i, int) and i == 0):
                    dve.wait_ge(y_out[u], 16 * i)
                m = xg[u]
                e = tile_e[:, bass.ds(j, 1)]
                d = dsc[u]
                V.scalar_tensor_tensor(out=d[:, 0:1], in0=m[:, C_E0:C_E0 + 1], scalar=e, in1=m[:, C_W0:C_W0 + 1],
                                       op0=ALU.is_equal, op1=ALU.mult).then_inc(dsc_chain, 1)
                V.scalar_tensor_tensor(out=d[:, 1:2], in0=m[:, C_E0:C_E0 + 1], scalar=e, in1=m[:, C_W1:C_W1 + 1],
                                       op0=ALU.not_equal, op1=ALU.mult).then_inc(dsc_chain, 1)
                V.tensor_scalar(d[:, 2:3], m[:, C_E0:C_E0 + 1], e, float(PLANE), ALU.not_equal, ALU.mult).then_inc(dsc_chain, 1)
                dve.wait_ge(dsc_chain, 5 * j + 3)
                V.tensor_tensor(d[:, 3:4], d[:, 0:1], d[:, 1:2], ALU.add).then_inc(dsc_chain, 1)
                V.tensor_tensor(dest[u][:], d[:, 2:3], m[:, C_TOK:C_TOK + 1], ALU.add).then_inc(dsc_chain, 1)

            def weigh(i, u):
                j = U * i + u
                dve.wait_ge(y_full, j + 1)
                dve.wait_ge(dsc_chain, 5 * j + 5)
                V.tensor_scalar(ysb[u], psY, dsc[u][:, 3:4], None, ALU.mult).then_inc(y_ready, 1)

            def at(i, u):
                return i + u // U, u % U

            def turn(i, first=False, last=False):
                for u in range(LAST if last else U):
                    if not (last and u == LAST - 1):
                        keep_tile(*at(i, u + 1))
                    multiply(i, u)
                    if not (first and u < 2):
                        weigh(*at(i, u - 2))
                    weights(i, u)

            keep_tile(0, 0)
            turn(0, first=True)
            with dve.Fori(1, TURNS - 1) as i:
                turn(i)
            turn(TURNS - 1, last=True)
            weigh(TURNS - 1, LAST - 2)
            weigh(TURNS - 1, LAST - 1)

            for b in range(B):
                dve.wait_ge(yp_in[b], 32)
                V.tensor_tensor(yp[b][:, 0], yp[b][:, 0], yp[b][:, 1], ALU.add).then_inc(c2_chain, 1)
                dve.wait_ge(c2_chain, 2 * b + 1)
                V.tensor_tensor(yp[b][:, 0], yp[b][:, 0], modbc[:, b, 3:4, :].broadcast_to([P, TB, E]), ALU.mult
                                ).then_inc(c2_chain, 1)

        @block.gpsimd
        def _(pool):
            gp = nc.gpsimd
            gp.memset(neghalf[:], -0.5).then_inc(zeroed, 1)
            gp.memset(identf[:], 0.0).then_inc(zeroed, 1)
            gp.memset(identb[:], 0.0).then_inc(zeroed, 1)
            gp.memset(zero_b[:], 0.0).then_inc(zeroed, 1)
            gp.memset(rowsel, 0.0).then_inc(zeroed, 1)
            hold("pool", pool, zeroed, 5)
            gp.affine_select(out=identf[:], in_=identf[:], compare_op=ALU.not_equal, fill=1.0, base=0,
                             pattern=[[-1, P]], channel_multiplier=1).then_inc(ident_ready, 1)
            gp.affine_select(out=identb[:], in_=identb[:], compare_op=ALU.not_equal, fill=1.0, base=0,
                             pattern=[[-1, P]], channel_multiplier=1).then_inc(ident_ready, 1)
            gp.affine_select(out=maskts[:], in_=zero_b[:], compare_op=ALU.is_ge, fill=BIG, base=0,
                             pattern=[[-1, P]], channel_multiplier=1).then_inc(ident_ready, 1)

            def inv_std(m2, ve, rs, chain, ready):
                gp.tensor_scalar(ve, m2, EPS, None, ALU.add).then_inc(chain[0], 1)
                hold("pool", pool, *chain)
                n = neghalf[:, 0] if len(ve.shape) == 2 else neghalf[:, 0:ve.shape[1]]
                gp.tensor_tensor(rs, ve, n, ALU.pow).then_inc(ready, 1)

            def x_inv(batches, n):
                pool.wait_ge(st_chain, 8 * batches.stop)
                inv_std(mv[:, batches, :, 1], vare[:, batches], rstd[:, batches], (rs_chain, n), rs_ready)

            def inv_shift(m2, ve, rs, sh, src_chain, used, chain, ready, b):
                hold("pool", pool, src_chain, 8 * b + 8)
                if has_earlier(b):
                    hold("pool", pool, used, b)
                gp.tensor_scalar(sh[:], m2[:, :, 0], -1.0, None, ALU.mult).then_inc(chain, 1)
                inv_std(m2[:, :, 1], ve[:], rs[:], (chain, 3 * b + 2), chain)
                hold("pool", pool, chain, 3 * b + 3)
                gp.tensor_tensor(sh[:], sh[:], rs[:], ALU.mult).then_inc(ready, 1)

            def o_inv(b):
                inv_shift(mvO, vareO, rstdO, shiftO, so_chain, onn_ready, rso_chain, rso_ready, b)

            def h_inv(b):
                inv_shift(mv2, vare2, rstd2, shift2, sr_chain, xr_ready, rsr_chain, rsr_ready, b)

            def low(b, res, parts, mid, done):
                hold("pool", pool, mid, b + 1)
                gp.tensor_tensor(parts[:, 2, :], res[:], parts[:, 1, :], ALU.subtract).then_inc(done, 1)

            def mask(b, g, c):
                base, stride, units = probs_block(CHUNKS[c])
                hold("pool", pool, exp_done, UNITS * (4 * b + g) + units)
                v = probs[:, g % 2, base:base + J * stride].rearrange("p (j c) -> p j c", j=J)[:, :, 0:P]
                gp.affine_select(out=v, in_=v, compare_op=ALU.is_ge, fill=0.0, base=0,
                                 pattern=[[0, J], [1, P]], channel_multiplier=-1).then_inc(masked, 1)

            def add_attn(b):
                hold("pool", pool, proj_ready, b + 1)
                gp.tensor_tensor(xall[:, b], xall[:, b], proj[:], ALU.add).then_inc(x1_ready, 1)

            def h_scale(b):
                hold("pool", pool, xr_ready, b + 1)
                gp.tensor_tensor(xn2[:], xn2[:], modbc[:, b, 2:3, :].broadcast_to([P, TB, E]), ALU.mult).then_inc(h2_chain, 1)

            def h_shift(b):
                hold("pool", pool, h2_chain, b + 1)
                if has_earlier(b):
                    hold("pool", pool, h2T_full, b)
                    hold("pool", pool, rows_ready, b)
                gp.tensor_tensor(h2[:], xn2[:], modbc[:, b, 1:2, :].broadcast_to([P, TB, E]), ALU.add).then_inc(h2_ready, 1)

            def count(b):
                if has_earlier(b):
                    hold("pool", pool, slot_full, b)
                hold("pool", pool, taken_chain, 5 * b + 1)
                gp.tensor_copy(taken[:, 0], taken[:, TB]).then_inc(taken_chain, 1)
                hold("pool", pool, r_chain, LINKS * b + 15)
                for n in range(TB):
                    hold("pool", pool, taken_chain, 5 * b + 2 + n)
                    gp.tensor_tensor(taken[:, n + 1], taken[:, n], both[:, n], ALU.add).then_inc(taken_chain, 1)

            def scatter(b, tiles):
                hold("pool", pool, r_chain, LINKS * (b + 1))
                for n in tiles:
                    for k in range(2):
                        gp.indirect_dma_start(xd[:, :], bass.IndirectOffsetOnAxis(ap=slots_of(b)[:, k, n:n + 1], axis=0),
                                              rows_of(b)[:, n, :], None).then_inc(dispatched, 16)

            def step(b, g):
                if g == 0 and has_batch(b - 2):
                    h_scale(b - 2)
                if g == 0 and has_batch(b + 1) and has_earlier(b):
                    low(b + 1, qres, qparts, q_mid, q_parts)
                if g == 0 and has_batch(b - 2):
                    h_shift(b - 2)
                mask(b, g, 0)
                if g == 1 and has_batch(b - 1):
                    o_inv(b - 1)
                if g == 2 and has_batch(b - 2):
                    scatter(b - 2, (0, 1))
                if g == 3 and has_batch(b - 1):
                    h_inv(b - 1)
                mask(b, g, 1)
                if g == 1 and has_batch(b - 2):
                    count(b - 2)
                mask(b, g, 2)
                if g == 0 and has_batch(b + 1):
                    low(b + 1, kres, kparts, k_mid, k_parts)
                mask(b, g, 3)
                if isinstance(b, int) and (b, g) == (0, 1):
                    x_inv(slice(2, B), 3)
                if g == 2 and has_batch(b - 1):
                    add_attn(b - 1)
                if g == 2 and has_batch(b - 2) and not (isinstance(b, int) and b == B - 1):
                    scatter(b - 2, (2, 3))

            x_inv(slice(0, 1), 1)
            gp.affine_select(out=rowsel, in_=rowsel, compare_op=ALU.not_equal, fill=1.0, base=0,
                             pattern=[[-1, B], [0, P]], channel_multiplier=1).then_inc(mod8_ready, 1)
            gp.memset(vaug[:], 0.0).then_inc(vaug_set, 1)
            hold("pool", pool, vaug_set, 1)
            gp.memset(vaug[:, :, :, D:D + 1], 1.0).then_inc(vaug_set, 1)
            gp.memset(onesrow[:], 1.0).then_inc(f_const, 1)
            gp.memset(ones[:], 1.0).then_inc(f_zero, 1)
            pool.wait_ge(f_zero, 1)
            gp.affine_select(out=before_t[:], in_=ones[:], compare_op=ALU.is_ge, fill=0.0, base=-1,
                             pattern=[[1, P]], channel_multiplier=-1).then_inc(f_const, 1)
            gp.iota(pri_i[:], pattern=[[-1, NX]], base=NX, channel_multiplier=0)
            gp.iota(base_i[:], pattern=[[REGION, NX]], base=0, channel_multiplier=0)
            gp.iota(thr_i[:], pattern=[[P, NT]], base=0, channel_multiplier=0)
            gp.iota(jv_i[:], pattern=[[1, FTILES]], base=0, channel_multiplier=0)
            gp.iota(part_i[:], pattern=[[0, 1]], base=0, channel_multiplier=1)
            gp.iota(tok_i[:], pattern=[[P, NT]], base=0, channel_multiplier=1)
            gp.iota(padtok[:], pattern=[[P, 2 * NX]], base=TOK, channel_multiplier=1).then_inc(f_const, 1)

            low(0, qres, qparts, q_mid, q_parts)
            low(0, kres, kparts, k_mid, k_parts)
            x_inv(slice(1, 2), 2)
            low(1, qres, qparts, q_mid, q_parts)
            all_steps(pool, step)
            scatter(B - 3, (2, 3))
            o_inv(B - 1)
            h_scale(B - 2)
            h_shift(B - 2)
            h_inv(B - 1)
            count(B - 2)
            scatter(B - 2, (0, 1, 2))
            count(B - 1)
            scatter(B - 2, (3,))
            scatter(B - 1, range(TB))

            def send(i, u):
                hold("pool", pool, y_ready, U * i + u + 1)
                gp.indirect_dma_start(yd[:, :], bass.IndirectOffsetOnAxis(ap=dest[u][:, 0:1], axis=0),
                                      ysb[u], None).then_inc(y_out[u], 16)

            with pool.Fori(0, TURNS - 1) as i:
                for u in range(U):
                    send(i, u)
            for u in range(LAST):
                send(TURNS - 1, u)
            for b in range(B):
                pool.wait_ge(c2_chain, 2 * b + 2)
                gp.tensor_tensor(xall[:, b], xall[:, b], yp[b][:, 0], ALU.add).then_inc(fin_ready, 1)


def kernel(**inputs):
    import numpy as np
    import concourse.bacc as bacc
    from concourse import mybir as mb
    from concourse.bass_utils import run_bass_kernel_spmd as run

    a = {n: np.asarray(v) for n, v in inputs.items()}
    arrays = {
        "x": a["L0_attn_x"],
        "cT": a["L0_c"].T,
        "wmod": a["L0_wmod"],
        "wqT": a["L0_attn_Wq"].T,
        "wkT": a["L0_attn_Wk"].T,
        "wvT": a["L0_attn_Wv"].reshape(D, H, E).transpose(2, 1, 0).reshape(E, E),
        "woT": a["L0_attn_Wo"].T,
        "gamma": a["L0_attn_gamma"].reshape(E, 1),
        "beta": a["L0_attn_beta"].reshape(E, 1),
        "confT": a["L0_ffn_conf_w"].T,
        "conf_b": a["L0_ffn_conf_b"].reshape(1, NX),
        "wealth": a["L0_ffn_wealth"].reshape(1, NX),
        "gateT": a["L0_ffn_gate_w"].transpose(2, 0, 1),
        "upT": a["L0_ffn_up_w"].transpose(2, 0, 1),
        "downT": a["L0_ffn_down_w"].reshape(NX, E, FC, P).transpose(3, 0, 2, 1),
    }
    nc = bacc.Bacc("TRN2", target_bir_lowering=False, num_devices=1)
    feed, args = {}, []
    for name, v in arrays.items():
        v = np.ascontiguousarray(v)
        feed["in_" + name] = v
        args.append(nc.dram_tensor("in_" + name, v.shape, mb.dt.from_np(v.dtype), kind="ExternalInput").ap())
    out = nc.dram_tensor("out_0", (B, S, E), mb.dt.float32, kind="ExternalOutput").ap()
    adaln_attention_moe(nc, *args, out)
    r = run(nc, [feed], core_ids=[0])
    return r.results[0]["out_0"]
```
